# Optimizing a Trainium2 kernel written in Bass

```python
import numpy as np
import jax
import jax.numpy as jnp

def _softmax(x, axis=-1):
    return jax.nn.softmax(x, axis=axis)

def _gelu(x):
    return jax.nn.gelu(x, approximate=True)

def _silu(x):
    return jax.nn.silu(x)

def _sigmoid(x):
    return jax.nn.sigmoid(x)

def _layernorm(x, axis=-1, eps=1e-05):
    m = jnp.mean(x, axis=axis, keepdims=True)
    v = jnp.var(x, axis=axis, keepdims=True)
    return (x - m) / jnp.sqrt(v + eps)

def _scatter_add(tgt, idx, src, axis=0):
    return tgt.at[idx].add(src)

def _segment_sum(src, seg, n):
    return jax.ops.segment_sum(src, seg, n)
kernel_name = 'mk_conv_preact_d2_conv_nchw1024_r4_b82f04'

def setup_inputs(seed: int=0):
    np.random.seed(seed)
    _w = jnp.asarray

    def _rec_inputs():
        import jax
        import jax.numpy as jnp
        _gk = jax.random.key(seed)
        x = -7.109e-06 + 0.09999 * jax.random.normal(jax.random.fold_in(_gk, 1), (16, 256, 16, 16), jnp.float32)
        return x
    x = _rec_inputs()

    def _L0_conv_setup():
        import jax, jax.numpy as jnp
        import numpy as np
        B, N, Fh, T, K, C = (16, 256, 16, 16, 3, 16)

        def _col_softmax(S):
            return jax.nn.softmax(S, axis=1)
        key = jax.random.key(seed)
        ks = jax.random.split(key, 16)
        rn = lambda k, shape, s: jax.random.normal(k, shape, dtype=jnp.float32) * s
        x = rn(ks[0], (B, N, Fh, T), 0.1)
        cheb = rn(ks[1], (K, N, N), 1.0 / np.sqrt(N))
        Theta = rn(ks[2], (K, Fh, C), (2.0 / (Fh + C)) ** 0.5)
        W1 = rn(ks[3], (T,), T ** (-0.5))
        W2 = rn(ks[4], (Fh, T), (2.0 / (Fh + T)) ** 0.5)
        W3 = rn(ks[5], (Fh,), Fh ** (-0.5))
        b_s = jnp.zeros((1, N, N), jnp.float32)
        V_s = rn(ks[6], (N, N), N ** (-0.5))
        U1 = rn(ks[7], (N,), N ** (-0.5))
        U2 = rn(ks[8], (Fh, N), (2.0 / (Fh + N)) ** 0.5)
        U3 = rn(ks[9], (Fh,), Fh ** (-0.5))
        b_e = jnp.zeros((1, T, T), jnp.float32)
        V_e = rn(ks[10], (T, T), T ** (-0.5))
        tw = rn(ks[11], (C, C, 1, 3), (2.0 / (C * 3)) ** 0.5)
        tb = jnp.zeros((C,), jnp.float32)
        rw = rn(ks[12], (C, Fh), (2.0 / Fh) ** 0.5)
        rb = jnp.zeros((C,), jnp.float32)
        gamma = jnp.ones((C,), jnp.float32)
        beta = jnp.zeros((C,), jnp.float32)
        return dict(x=x, cheb=cheb, Theta=Theta, W1=W1, W2=W2, W3=W3, b_s=b_s, V_s=V_s, U1=U1, U2=U2, U3=U3, b_e=b_e, V_e=V_e, tw=tw, tb=tb, rw=rw, rb=rb, gamma=gamma, beta=beta)
    _L0_conv_all = _L0_conv_setup()
    _L0_conv_in = {k: v for k, v in _L0_conv_all.items() if k in ('cheb', 'Theta', 'W1', 'W2', 'W3', 'b_s', 'V_s', 'U1', 'U2', 'U3', 'b_e', 'V_e', 'tw', 'tb', 'rw', 'rb', 'gamma', 'beta')}
    del _L0_conv_all

    def _L1_conv_setup():
        import jax, jax.numpy as jnp
        import numpy as np
        B, C, H, W = (2, 256, 16, 16)
        E, TOP_K = (8, 2)
        FFN = C
        key = jax.random.key(seed)
        ks = jax.random.split(key, 5)
        s = 0.02
        return {'hidden_states': jax.random.normal(ks[0], (B, C, H, W), jnp.float32), 'gate_w': jax.random.normal(ks[1], (E, C), jnp.float32) * s, 'w1': jax.random.normal(ks[2], (E, FFN, C), jnp.float32) * s, 'w2': jax.random.normal(ks[3], (E, C, FFN), jnp.float32) * s, 'w3': jax.random.normal(ks[4], (E, FFN, C), jnp.float32) * s}
    _L1_conv_all = _L1_conv_setup()
    _L1_conv_in = {k: v for k, v in _L1_conv_all.items() if k in ('gate_w', 'w1', 'w2', 'w3')}
    del _L1_conv_all
    return {'x': x, 'L0_conv_cheb': _L0_conv_in['cheb'], 'L0_conv_Theta': _L0_conv_in['Theta'], 'L0_conv_W1': _L0_conv_in['W1'], 'L0_conv_W2': _L0_conv_in['W2'], 'L0_conv_W3': _L0_conv_in['W3'], 'L0_conv_b_s': _L0_conv_in['b_s'], 'L0_conv_V_s': _L0_conv_in['V_s'], 'L0_conv_U1': _L0_conv_in['U1'], 'L0_conv_U2': _L0_conv_in['U2'], 'L0_conv_U3': _L0_conv_in['U3'], 'L0_conv_b_e': _L0_conv_in['b_e'], 'L0_conv_V_e': _L0_conv_in['V_e'], 'L0_conv_tw': _L0_conv_in['tw'], 'L0_conv_tb': _L0_conv_in['tb'], 'L0_conv_rw': _L0_conv_in['rw'], 'L0_conv_rb': _L0_conv_in['rb'], 'L0_conv_gamma': _L0_conv_in['gamma'], 'L0_conv_beta': _L0_conv_in['beta'], 'L1_conv_gate_w': _L1_conv_in['gate_w'], 'L1_conv_w1': _L1_conv_in['w1'], 'L1_conv_w2': _L1_conv_in['w2'], 'L1_conv_w3': _L1_conv_in['w3']}

def reference(x, L0_conv_cheb, L0_conv_Theta, L0_conv_W1, L0_conv_W2, L0_conv_W3, L0_conv_b_s, L0_conv_V_s, L0_conv_U1, L0_conv_U2, L0_conv_U3, L0_conv_b_e, L0_conv_V_e, L0_conv_tw, L0_conv_tb, L0_conv_rw, L0_conv_rb, L0_conv_gamma, L0_conv_beta, L1_conv_gate_w, L1_conv_w1, L1_conv_w2, L1_conv_w3):
    import jax
    import jax.numpy as jnp

    def _L0_conv_ref(x, cheb, Theta, W1, W2, W3, b_s, V_s, U1, U2, U3, b_e, V_e, tw, tb, rw, rb, gamma, beta):
        import jax, jax.numpy as jnp
        import numpy as np
        B, N, Fh, T, K, C = (16, 256, 16, 16, 3, 16)

        def _col_softmax(S):
            return jax.nn.softmax(S, axis=1)
        lhs = jnp.einsum('bnft,n->btf', x, U1) @ U2
        rhs = jnp.einsum('f,bnft->bnt', U3, x)
        prod = jnp.einsum('btn,bns->bts', lhs, rhs)
        E = jnp.einsum('kj,bij->bik', V_e, jax.nn.sigmoid(prod + b_e))
        E = _col_softmax(E)
        x_tat = jnp.einsum('bnfj,bjt->bnft', x, E)
        lhs2 = jnp.einsum('bnft,t->bnf', x_tat, W1) @ W2
        rhs2 = jnp.einsum('f,bnft->btn', W3, x_tat)
        prod2 = jnp.einsum('bnt,btm->bnm', lhs2, rhs2)
        S = jnp.einsum('kj,bij->bik', V_s, jax.nn.sigmoid(prod2 + b_s))
        S = _col_softmax(S)
        out = jnp.zeros((B, N, C, T), x.dtype)
        for k in range(cheb.shape[0]):
            r = jnp.einsum('mn,bmn,bmft->bnft', cheb[k], S, x)
            out = out + jnp.einsum('bnft,fo->bnot', r, Theta[k])
        sg = jax.nn.relu(out)
        tc = jax.lax.conv_general_dilated(sg.transpose(0, 2, 1, 3), tw, (1, 1), ((0, 0), (1, 1)), dimension_numbers=('NCHW', 'OIHW', 'NCHW'))
        tc = (tc + tb[None, :, None, None]).transpose(0, 2, 1, 3)
        res = jnp.einsum('bnft,of->bnot', x, rw) + rb[None, None, :, None]
        y = jax.nn.relu(res + tc)
        mu = jnp.mean(y, axis=-1, keepdims=True)
        var = jnp.var(y, axis=-1, keepdims=True)
        return (y - mu) / jnp.sqrt(var + 1e-05) * gamma + beta

    def _L1_conv_ref(hidden_states, gate_w, w1, w2, w3):
        import jax, jax.numpy as jnp
        import numpy as np
        B, C, H, W = (2, 256, 16, 16)
        E, TOP_K = (8, 2)
        FFN = C
        b, c = (hidden_states.shape[0], hidden_states.shape[1])
        space = hidden_states.shape[2:]
        x = jnp.transpose(hidden_states, (0, 2, 3, 1)).reshape(-1, c)
        logits = x @ gate_w.T
        probs = jax.nn.softmax(logits.astype(jnp.float32), axis=-1)
        rw, sel = jax.lax.top_k(probs, TOP_K)
        rw = rw / jnp.sum(rw, axis=-1, keepdims=True)
        rw = rw.astype(x.dtype)
        combine = jnp.sum(jax.nn.one_hot(sel, E, dtype=x.dtype) * rw[..., None], axis=1)
        out = jnp.zeros_like(x)
        for e in range(E):
            h = jax.nn.gelu(x @ w1[e].T, approximate=False) * (x @ w3[e].T)
            out = out + combine[:, e:e + 1] * (h @ w2[e].T)
        out = out.reshape(b, *space, c)
        return jnp.transpose(out, (0, 3, 1, 2))

    def _gn(v, G=32, eps=1e-05):
        B_, C_, H_, W_ = v.shape
        g = v.reshape(B_, G, C_ // G, H_, W_)
        m = jnp.mean(g, axis=(2, 3, 4), keepdims=True)
        s = jnp.var(g, axis=(2, 3, 4), keepdims=True)
        return ((g - m) / jnp.sqrt(s + eps)).reshape(v.shape)

    def _ln_c(v, eps=1e-06):
        m = jnp.mean(v, axis=1, keepdims=True)
        s = jnp.var(v, axis=1, keepdims=True)
        return (v - m) / jnp.sqrt(s + eps)

    def _ln_t(v, eps=1e-05):
        m = jnp.mean(v, axis=-1, keepdims=True)
        s = jnp.var(v, axis=-1, keepdims=True)
        return (v - m) / jnp.sqrt(s + eps)

    def _to_tokens(v):
        B_, C_, H_, W_ = v.shape
        return v.reshape(B_, C_, H_ * W_).transpose(0, 2, 1)

    def _from_tokens(t, like):
        B_, C_, H_, W_ = like.shape
        return t.transpose(0, 2, 1).reshape(B_, C_, H_, W_)
    x = x + _L0_conv_ref(_gn(x), L0_conv_cheb, L0_conv_Theta, L0_conv_W1, L0_conv_W2, L0_conv_W3, L0_conv_b_s, L0_conv_V_s, L0_conv_U1, L0_conv_U2, L0_conv_U3, L0_conv_b_e, L0_conv_V_e, L0_conv_tw, L0_conv_tb, L0_conv_rw, L0_conv_rb, L0_conv_gamma, L0_conv_beta)
    x = x + _L1_conv_ref(_gn(x), L1_conv_gate_w, L1_conv_w1, L1_conv_w2, L1_conv_w3)
    return x

_drawn_inputs = setup_inputs


def setup_inputs(seed=0):
    import zlib

    import numpy as np

    out = dict(_drawn_inputs(seed))
    spreads = {'L0_conv_b_s': (0.0, 0.8),
     'L0_conv_b_e': (0.0, 0.8),
     'L0_conv_tb': (0.0, 0.1),
     'L0_conv_rb': (0.0, 0.1),
     'L0_conv_gamma': (1.0, 0.2),
     'L0_conv_beta': (0.0, 0.1)}
    factors = {'L0_conv_cheb': 8.0,
     'L0_conv_Theta': 8.0,
     'L0_conv_W1': 8.0,
     'L0_conv_W2': 8.0,
     'L0_conv_W3': 8.0,
     'L0_conv_V_s': 8.0,
     'L0_conv_U1': 8.0,
     'L0_conv_U2': 8.0,
     'L0_conv_U3': 8.0,
     'L0_conv_V_e': 8.0,
     'L0_conv_tw': 8.0,
     'L1_conv_gate_w': 4.551,
     'L1_conv_w1': 4.073,
     'L1_conv_w2': 3.937,
     'L1_conv_w3': 3.953}
    for name, (base, spread) in spreads.items():
        noise = np.random.default_rng([zlib.crc32(name.encode()), seed]).standard_normal(out[name].shape)
        drawn = base * np.exp(spread * noise) if base else spread * noise
        out[name] = jnp.asarray(drawn.astype(out[name].dtype))
    for name, factor in factors.items():
        out[name] = (out[name] * factor).astype(out[name].dtype)
    return out
```

```python
from contextlib import ExitStack

import concourse.bass as bass
from concourse import mybir

F32 = mybir.dt.float32
I32 = mybir.dt.int32
ALU = mybir.AluOpType
ACT = mybir.ActivationFunctionType
AX = mybir.AxisListType.X

P = 128
B, N, F, T = 16, 256, 16, 16
C = N // P
FT = F * T
TH = P // F
H = FT // P
K = 3
BAND = (TH + 1) * F
GB = 4
GROUPS = B // GB
E = 8
TT = FT // P
TOKENS = B * FT
CAP = TOKENS + P
ROW = N + 2
TILES = 2 * TOKENS // P + E
EPS = 1e-5
START = 2

ID, TRI, ONE, GRP = 0, P, 2 * P, 3 * P
BLK = 4 * P
DSC = BLK + TH + 4
EBASE = DSC + E
TIDX = EBASE + E
PCOL = TIDX + TILES
NCONST = PCOL + 1

SIZES = dict(theta=K * 16, rw=16, tw=3 * 16, w2=T, u3=1, w3=1, tb=16, rb=16, gamma=T, beta=T,
             u1=C, u2=C * F, gate=C * E, vet=T, bet=T, w1=1)
COL, NSMALL = {}, 0
for _name, _size in SIZES.items():
    COL[_name] = NSMALL
    NSMALL += _size


def done(b):
    return b + (1 + START)


class Steps:

    def __init__(self, eng, sem, turn, per_turn):
        self.eng, self.sem, self.base, self.per, self.n = eng, sem, turn * per_turn, per_turn, 0

    def __call__(self, ins):
        ins.then_inc(self.sem, 1)
        self.n += 1
        self.eng.wait_ge(self.sem, self.base + self.n)

    def close(self):
        assert self.n == self.per, (self.n, self.per)


def schedule(eng, turn):
    for i in range(-2, 0):
        turn(i, i % 2, True, i + 1 >= 0, False, False, False)
    for i in range(0, 2):
        turn(i, i % 2, True, True, True, i >= 1, False)
    with eng.Fori(0, (B - 4) // 2) as j:
        for q in range(2):
            turn(2 * j + (2 + q), q, True, True, True, True, True)
    for i in range(B - 2, B + 2):
        turn(i, i % 2, False, i + 1 < B, i < B, i - 1 < B, True)


def schedule_pool(pool, turn, scatter, landed):
    def both(i, q, flags, pairs=None):
        turn(i, q, *flags)
        if pairs is not None:
            landed(1 - q, pairs)
        if flags[4]:
            scatter(i - 2, q)
    for i in range(-2, 0):
        both(i, i % 2, (True, i + 1 >= 0, False, False, False))
    for i in range(0, 4):
        both(i, i % 2, (True, True, True, i >= 1, i >= 2), 1 if i == 3 else None)
    with pool.Fori(0, (B - 6) // 2) as j:
        for q in range(2):
            both(2 * j + (4 + q), q, (True,) * 5, j + (1 + q))
    for i in range(B - 2, B + 2):
        both(i, i % 2, (False, i + 1 < B, i < B, i - 1 < B, True), (i - 3) // 2 + 1)
    landed((B - 1) % 2, B // 2)


def build(nc, x, consts, small, cheb, vst, bst, w13t, w2t, xrows, yrows, out, stop_after=None):
    with ExitStack() as ctx:
        def sb(name, shape, dt=F32):
            return ctx.enter_context(nc.sbuf_tensor(name, [P] + shape, dt))

        def sem(name):
            return ctx.enter_context(nc.semaphore(name))

        bank = [ctx.enter_context(nc.psum_tensor(f"bank{i}", [P, 512], F32)) for i in range(8)]

        cst = sb("cst", [NCONST])
        sml = sb("sml", [NSMALL])
        xs = sb("xs", [B, C, FT])
        xT = sb("xT", [B, H, N])
        xTb = sb("xTb", [2, H, N])
        ghb = sb("ghb", [2, H, 2, T])
        chebs = sb("chebs", [C, K, N])
        vs = sb("vs", [C, N])
        bs = sb("bs", [C, N])
        w13 = sb("w13", [E, C, 2, N])
        w2 = sb("w2", [E, C, N])
        thetabd = sb("thetabd", [K, TH, 16])
        rwbd = sb("rwbd", [TH, 16])
        convm = sb("convm", [H, BAND])
        convt = sb("convt", [2, BAND])
        u3bd = sb("u3bd", [TH])
        u2rep = sb("u2rep", [C, TH, F])
        negb = sb("negb", [16])
        half = sb("half", [32])
        i16w1 = sb("i16w1", [T + 1])
        zs, As, xs1 = 2 * C * K * H * P, C * K * N, GB * C * FT
        work = sb("work", [zs + As + C * FT])
        z = work[:, 0:zs].rearrange("p (b c k h n) -> p b c k h n", b=2, c=C, k=K, h=H)
        A = work[:, zs:zs + As].rearrange("p (c k n) -> p c k n", c=C, k=K)
        y = work[:, zs + As:].rearrange("p (c n) -> p c n", c=C)
        xn = work[:, 0:xs1].rearrange("p (b c n) -> p b c n", b=GB, c=C)
        erep = work[:, xs1:zs].rearrange("p (b t f) -> p b t f", b=GB, t=T)
        xTg = work[:, zs:zs + xs1].rearrange("p (b h n) -> p b h n", b=GB, h=H)
        st6 = sb("st6", [GB * C, 6])
        mv = sb("mv", [GB * C, 2])
        gd = sb("gd", [4, GB * C])
        gr = sb("gr", [2, GB * C])
        rn = sb("rn", [C, GB, T])
        aind = sb("aind", [GB, H, TH])
        crep = sb("crep", [GB, T])
        eb = sb("eb", [3, GB, T])
        es = sb("es", [3, GB])
        gh = sb("gh", [B, H, 2, T])
        lr = sb("lr", [2, 2 * N])
        sg = sb("sg", [2, C, N])
        nmx = sb("nmx", [2, 2, C])
        es2 = sb("es2", [2, 2, C])
        pe_ = sb("pe_", [C, N])
        pn = sb("pn", [C, N])
        sgT = sb("sgT", [H, N])
        sq = sb("sq", [C, FT])
        s1 = sb("s1", [4, C, 16])
        rs = sb("rs", [C, 16])
        yg = sb("yg", [C, FT])
        st62 = sb("st62", [C, 6])
        mv2 = sb("mv2", [C, 2])
        gd2 = sb("gd2", [4, C])
        gr2 = sb("gr2", [2, C])
        xn2 = sb("xn2", [C, FT])
        xtok = sb("xtok", [2, TT, ROW])
        tok = sb("tok", [TT])
        rt = sb("rt", [12, TT, E])
        r2 = sb("r2", [10, TT])
        wts = sb("wts", [B, 2, TT])
        cnt = sb("cnt", [E])
        slotf = sb("slotf", [2, TT])
        slot = sb("slot", [2, 2, TT], I32)
        ci = sb("ci", [2, E], I32)
        nt = sb("nt", [3, E])
        ge = sb("ge", [2, TILES, E])
        tb3 = sb("tb3", [5, TILES])
        itab = sb("itab", [2, TILES], I32)
        filli = sb("filli", [E], I32)
        fillf = sb("fillf", [E])
        fill = sb("fill", [ROW])
        dest = sb("dest", [2, 1], I32)
        room = xT[:].rearrange("p b h n -> p (b h n)")
        used = [0]

        def over_xT(*shape):
            size = 1
            for d in shape:
                size *= d
            a = room[:, used[0]:used[0] + size]
            used[0] += size
            names = " ".join("abcd"[:len(shape)])
            return a.rearrange(f"p ({names}) -> p {names}", **dict(zip(names.split(), shape)))

        xt = over_xT(2, ROW)
        xc = over_xT(2, C, P)
        gl = over_xT(2, C, P)
        hh = over_xT(2, C, P)
        hT = over_xT(2, C, P)
        yo = over_xT(2, N)
        dn = over_xT(2, 4, 1)
        yy = over_xT(2, 2, TT, N)
        ys = over_xT(2, TT, N)
        oo = over_xT(2, C, FT)

        ld_c = sem("ld_c"); ld_w = sem("ld_w"); ld_m = sem("ld_m")
        ld_x = [sem(f"ld_x{i}") for i in range(2)]
        x_in = sem("x_in")
        wk = sem("wk"); wkp = sem("wkp"); consts_ready = sem("consts_ready"); zeros_ready = sem("zeros_ready")
        a_v = sem("a_v"); a_stat = sem("a_stat"); a_mean = sem("a_mean"); a_q = sem("a_q"); a_var = sem("a_var")
        a_ve = sem("a_ve"); a_rstd = sem("a_rstd"); a_nb = sem("a_nb"); a_xn = sem("a_xn"); a_tr = sem("a_tr")
        a_xT = sem("a_xT"); a_av = sem("a_av"); a_rn = sem("a_rn"); a_cr = sem("a_cr"); a_ai = sem("a_ai")
        a_pr = sem("a_pr"); a_pb = sem("a_pb"); a_th = sem("a_th"); a_er = sem("a_er"); a_es = sem("a_es")
        a_ex = sem("a_ex"); a_et = sem("a_et"); a_rep = sem("a_rep"); a_gh = sem("a_gh"); a_cp = sem("a_cp")
        names = ("b_gh b_lr b_pr b_bs b_th b_L b_max b_exp b_rec b_pn b_tr b_A b_z b_zc b_main b_relu b_conv "
                 "b_y b_cen b_sq b_var b_rs b_dn b_x1 b_st b_g1 b_q b_g2 b_ve b_rstd b_nb b_xn b_tk b_tkc "
                 "b_sh b_ex b_M b_pf b_slot b_sc b_gb b_xb").split()
        s = {n: sem(n) for n in names}
        v_ln = sem("v_ln"); v_gn = sem("v_gn"); v_rt = sem("v_rt"); v_rt2 = sem("v_rt2"); p_rs = sem("p_rs")
        p_x1 = sem("p_x1"); v_mx = sem("v_mx"); tok_ready = sem("tok_ready")
        sc_done = [sem("sc_done0"), sem("sc_done1")]
        v_tb = sem("v_tb"); tables = sem("tables"); fill_ready = sem("fill_ready"); fill_done = sem("fill_done")
        rows_ready = sem("rows_ready")
        c_ld = [sem("c_ld0"), sem("c_ld1")]; c_in = sem("c_in"); c_tr = sem("c_tr"); c_xc = sem("c_xc"); c_up = sem("c_up")
        c_gl = sem("c_gl"); c_h = sem("c_h"); c_ht = sem("c_ht"); c_hc = sem("c_hc"); c_dn = sem("c_dn"); c_y = sem("c_y"); c_dd = sem("c_dd")
        c_de = sem("c_de"); c_di = sem("c_di")
        c_st = [sem("c_st0"), sem("c_st1")]; c_out = sem("c_out")
        d_ld = [sem("d_ld0"), sem("d_ld1")]; d_in = sem("d_in"); d_m = sem("d_m"); d_s = sem("d_s"); d_tr = sem("d_tr")
        d_o = sem("d_o"); d_st = [sem("d_st0"), sem("d_st1")]; d_out = sem("d_out")

        cs = lambda a, n: cst[:, a:a + n]
        sm = lambda name: sml[:, COL[name]:COL[name] + SIZES[name]]
        ident = cs(ID, P)
        blk = cs(BLK + 2, TH)

        x_v = x.rearrange("b (c p) f t -> p b c (f t)", p=P)
        out_v = out.rearrange("b (c p) f t -> p b c (f t)", p=P)
        y_v = yrows[0:2 * TOKENS, :].rearrange("(w b k p) n -> p w b k n", w=2, b=B, k=TT)

        block = ctx.enter_context(nc.Block())

        @block.sync
        def _(sp):
            sp.dma_start(cst[:], consts).then_inc(ld_c, 16)
            sp.dma_start(sml[:], small).then_inc(ld_c, 16)
            for g in range(GROUPS):
                if g >= 2:
                    sp.wait_ge(ld_x[g % 2], 16 * (g // 2))
                    sp.sem_inc(x_in, 1)
                sp.dma_start(xs[:, g * GB:(g + 1) * GB], x_v[:, g * GB:(g + 1) * GB]).then_inc(ld_x[g % 2], 16)
            for g in range(GROUPS - 2, GROUPS):
                sp.wait_ge(ld_x[g % 2], 16 * (g // 2 + 1))
                sp.sem_inc(x_in, 1)
            sp.dma_start(chebs[:], cheb).then_inc(ld_w, 16)
            sp.dma_start(vs[:], vst).then_inc(ld_w, 16)
            sp.dma_start(bs[:], bst).then_inc(ld_w, 16)
            for dst, src in ((w13, w13t), (w2, w2t)):
                sp.dma_start(dst[:], src).then_inc(ld_m, 16)
            if stop_after == "B":
                sp.wait_ge(s["b_x1"], done(B - 1))
                sp.dma_start(out_v, xs[:]).then_inc(d_st[0], 16)
                sp.wait_ge(d_st[0], 16)
                return
            sp.wait_ge(fill_ready, 1)
            sp.dma_start(xrows[E * CAP:E * CAP + P, :], fill[:]).then_inc(fill_done, 16)
            sp.wait_ge(tables, 1)
            for e in range(E):
                r = sp.value_load(filli[0:1, e:e + 1], min_val=e * CAP, max_val=e * CAP + TOKENS)
                sp.dma_start(xrows[bass.ds(r, P), :], fill[:]).then_inc(fill_done, 16)
            sp.wait_ge(fill_done, 16 * (E + 1))
            for q in range(2):
                sp.wait_ge(sc_done[q], 16 * 2 * TT * (B // 2))

            def load_tile(t, q):
                r = sp.value_load(itab[0:1, 1, bass.ds(t, 1)], min_val=0, max_val=E * CAP)
                sp.dma_start(xt[:, q], xrows[bass.ds(r, P), :]).then_inc(c_ld[q], 16)

            load_tile(0, 0)
            load_tile(1, 1)
            with sp.Fori(0, TILES // 2 - 1) as i:
                for q in range(2):
                    sp.wait_ge(c_ld[q], 16 * (i + 1))
                    sp.sem_inc(c_in, 1)
                    sp.wait_ge(c_tr, 2 * i + (q + 1))
                    sp.wait_ge(c_de, 2 * i + (q + 1))
                    load_tile(2 * i + (q + 2), q)
            for q in range(2):
                sp.wait_ge(c_ld[q], 16 * (TILES // 2))
                sp.sem_inc(c_in, 1)

            for q in range(2):
                sp.wait_ge(c_st[q], 16 * (TILES // 2))
            def load_d(b, q):
                sp.dma_start(yy[:, q, 0], y_v[:, 0, b]).then_inc(d_ld[q], 16)
                sp.dma_start(yy[:, q, 1], y_v[:, 1, b]).then_inc(d_ld[q], 16)

            load_d(0, 0)
            load_d(1, 1)
            with sp.Fori(0, B // 2 - 1) as i:
                for q in range(2):
                    sp.wait_ge(d_ld[q], 32 * (i + 1))
                    sp.sem_inc(d_in, 1)
                    sp.wait_ge(d_s, 2 * i + (q + 1))
                    load_d(2 * i + (q + 2), q)
            for q in range(2):
                sp.wait_ge(d_ld[q], 32 * (B // 2))
                sp.sem_inc(d_in, 1)

        @block.tensor
        def _(pe):
            mm = nc.tensor.matmul
            for n in "b_gh b_pr b_L b_tr b_z b_main b_conv b_g1 b_g2 b_tk b_pf".split():
                pe.sem_inc(s[n], START)
            for c in (a_tr, c_up, c_dn, c_ht):
                pe.sem_inc(c, START)
            pe.wait_ge(consts_ready, 1)

            with pe.Fori(0, GROUPS) as g:
                pe.wait_ge(a_stat, g + 1)
                mm(bank[0][:, 0:GB * C], cs(GRP, P), mv[:, :, 0], start=True, stop=True).then_inc(a_mean, 1)
                pe.wait_ge(a_q, g + 1)
                mm(bank[0][:, 0:GB * C], cs(GRP, P), gd[:, 2], start=True, stop=True).then_inc(a_var, 1)
                for j in range(GB):
                    pe.wait_ge(a_xn, GB * g + (j + 1))
                    pe.wait_ge(a_xT, GB * g + (j + 1))
                    for h in range(H):
                        for c in range(C):
                            last = nc.tensor.transpose(bank[1 + j % 2][:, (h * C + c) * P:(h * C + c + 1) * P],
                                                       xn[:, j, c, h * P:(h + 1) * P], ident)
                    last.then_inc(a_tr, 1)
                pe.wait_ge(a_xT, GB * g + (GB + START))
                pe.wait_ge(a_rn, g + START)
                for j in range(GB):
                    for h in range(H):
                        for c in range(C):
                            mm(bank[3][:, j * H + h:j * H + h + 1], xn[:, j, c, h * P:(h + 1) * P],
                               sm("u1")[:, c:c + 1], start=(c == 0), stop=(c == C - 1))
                    for h in range(H):
                        for c in range(C):
                            o = 16 + (c * GB + j) * T + h * TH
                            last = mm(bank[3][:, o:o + TH], xTg[:, j, h, c * P:(c + 1) * P], u3bd[:],
                                      start=True, stop=True)
                last.then_inc(a_av, 1)
                pe.wait_ge(a_rn, g + (1 + START))
                for c in range(C):
                    last = mm(bank[4][:, 0:GB * T], u2rep[:, c].rearrange("p t f -> p (t f)"),
                              rn[:, c].rearrange("p b t -> p (b t)"), start=(c == 0), stop=(c == C - 1))
                last.then_inc(a_cr, 1)
                pe.wait_ge(a_ai, g + 1)
                for j in range(GB):
                    last = mm(bank[5][0:T, j * T:(j + 1) * T], crep[:, j], aind[:, j].rearrange("p h t -> p (h t)"),
                              start=True, stop=True)
                last.then_inc(a_pr, 1)
                pe.wait_ge(a_th, g + 1)
                pe.nop(nofuse=True)
                mm(bank[5][0:T, 0:GB * T], sml[0:T, COL["vet"]:COL["vet"] + T],
                   eb[0:T, 1].rearrange("p b t -> p (b t)"), start=True, stop=True).then_inc(a_er, 1)
                pe.wait_ge(a_et, g + 1)
                for j in range(GB):
                    for h in range(H):
                        o = (j * H + h) * (T + 1)
                        last = mm(bank[6][:, o:o + T + 1],
                                  erep[0:T, j, h * TH:(h + 1) * TH].rearrange("p t f -> p (t f)"), i16w1[0:T, :],
                                  start=True, stop=True)
                last.then_inc(a_rep, 1)

            def mix(b, p):
                pe.wait_ge(s["b_lr"], done(b - 1))
                if not isinstance(b, int) or b >= 5:
                    pe.wait_ge(s["b_tkc"], done(b - 5))
                pe.wait_ge(s["b_gb"], done(b))
                for q in range(2):
                    for h in range(H):
                        last = mm(bank[0][0:T, q * N:(q + 1) * N], ghb[:, p, h, q], xT[:, b, h],
                                  start=(h == 0), stop=(h == H - 1))
                last.then_inc(s["b_gh"], 1)

            def product(b, p):
                pe.wait_ge(s["b_lr"], done(b))
                pe.wait_ge(s["b_exp"], done(b - 1))
                for c in range(C):
                    last = mm(bank[1][:, c * N:(c + 1) * N], lr[0:T, p, N + c * P:N + (c + 1) * P],
                              lr[0:T, p, 0:N], start=True, stop=True)
                last.then_inc(s["b_pr"], 1)

            def logits(b, p):
                pe.wait_ge(s["b_th"], done(b))
                for c in range(C):
                    for j in range(C):
                        last = mm(bank[1][:, c * N:(c + 1) * N], vs[:, j, c * P:(c + 1) * P], sg[:, p, j],
                                  start=(j == 0), stop=(j == C - 1))
                last.then_inc(s["b_L"], 1)

            def turn_softmax(b, p):
                pe.wait_ge(s["b_pn"], done(b))
                pe.wait_ge(s["b_A"], done(b - 1))
                for m in range(C):
                    for n in range(C):
                        last = nc.tensor.transpose(bank[3][:, m * N + n * P:m * N + (n + 1) * P],
                                                   pn[:, n, m * P:(m + 1) * P], ident)
                last.then_inc(s["b_tr"], 1)

            def features(b, p, c):
                pe.wait_ge(s["b_xb"], done(b))
                for h in range(H):
                    pe.wait_ge(s["b_zc"], (b * 4 + (c * H + h)) + (START - 1))
                    mm(bank[4 + h][:, 0:K * P], xTb[:, p, h, c * P:(c + 1) * P],
                       thetabd[:].rearrange("p k t o -> p (k t o)"), start=True, stop=True).then_inc(s["b_z"], 1)

            def graph(b, p, h):
                if h == 0:
                    pe.wait_ge(s["b_A"], done(b))
                    pe.wait_ge(s["b_zc"], (b * 4 + 4) + START)
                    pe.wait_ge(s["b_relu"], done(b - 1))
                for c in range(C):
                    for k in range(K):
                        last = mm(bank[6][:, h * N:(h + 1) * N], z[:, p, c, k, h], A[:, c, k],
                                  start=(c == 0 and k == 0), stop=(c == C - 1 and k == K - 1))
                if h == H - 1:
                    last.then_inc(s["b_main"], 1)

            def conv(b, p):
                pe.wait_ge(s["b_relu"], done(b))
                pe.wait_ge(s["b_y"], done(b - 1))
                for c in range(C):
                    o = bank[7][:, c * FT:(c + 1) * FT]
                    for h in range(H):
                        mm(o[:, h * P:(h + 1) * P], xTb[:, p, h, c * P:(c + 1) * P],
                           rwbd[:].rearrange("p t o -> p (t o)"), start=(c == 0 and h == 0), stop=False,
                           skip_group_check=True)
                    for h in range(H):
                        a = h * (FT - BAND)
                        last = mm(o[:, a:a + BAND], sgT[:, h, c * P:(c + 1) * P], convm[:, h],
                                  start=False, stop=(c == C - 1 and h == H - 1), skip_group_check=True)
                last.then_inc(s["b_conv"], 1)

            def gn_mean(b, p):
                pe.wait_ge(s["b_st"], done(b))
                pe.wait_ge(s["b_slot"], done(b - 1))
                mm(bank[2][:, 0:C], cs(GRP, P), mv2[:, :, 0], start=True, stop=True).then_inc(s["b_g1"], 1)

            def gn_var(b, p):
                pe.wait_ge(s["b_q"], done(b))
                mm(bank[2][:, 0:C], cs(GRP, P), gd2[:, 2], start=True, stop=True).then_inc(s["b_g2"], 1)

            def tokens(b, p):
                pe.wait_ge(s["b_xn"], done(b))
                pe.wait_ge(s["b_lr"], done(min(b + 4, B - 1) if isinstance(b, int) else b + 4))
                for k in range(TT):
                    for c in range(C):
                        mm(bank[2][:, 16 + k * E:16 + (k + 1) * E], xn2[:, c, k * P:(k + 1) * P],
                           sm("gate")[:, c * E:(c + 1) * E], start=(c == 0), stop=(c == C - 1))
                for k in range(TT):
                    for c in range(C):
                        last = nc.tensor.transpose(bank[0][:, k * N + c * P:k * N + (c + 1) * P],
                                                   xn2[:, c, k * P:(k + 1) * P], ident)
                last.then_inc(s["b_tk"], 1)

            def prefix(b, p):
                pe.wait_ge(s["b_M"], done(b))
                tri, one = cs(TRI, P), cs(ONE, P)
                M = rt[:, 9]
                mm(bank[2][:, 64:64 + E], tri, M[:, 0], start=True, stop=True)
                mm(bank[2][:, 72:72 + E], tri, M[:, 1], start=True, stop=False)
                mm(bank[2][:, 72:72 + E], one, M[:, 0], start=False, stop=True)
                mm(bank[2][:, 80:80 + E], one, M[:, 0], start=True, stop=False)
                mm(bank[2][:, 80:80 + E], one, M[:, 1], start=False, stop=True).then_inc(s["b_pf"], 1)

            def turn(i, q, ahead2, ahead1, now, back1, back2):
                if now:
                    graph(i, q, 0)
                if ahead1:
                    logits(i + 1, 1 - q)
                if back2:
                    gn_mean(i - 2, q)
                if now:
                    graph(i, q, 1)
                if back2:
                    gn_var(i - 2, q)
                if ahead2:
                    mix(i + 2, q)
                if ahead1:
                    features(i + 1, 1 - q, 0)
                    turn_softmax(i + 1, 1 - q)
                if back2:
                    tokens(i - 2, q)
                if ahead2:
                    product(i + 2, q)
                if ahead1:
                    features(i + 1, 1 - q, 1)
                if now:
                    conv(i, q)
                if back2:
                    prefix(i - 2, q)

            pe.wait_ge(ld_w, 48)
            pe.wait_ge(a_gh, GROUPS)
            schedule(pe, turn)

            if stop_after == "B":
                return
            pe.wait_ge(ld_m, 32)
            pe.wait_ge(tables, 1)

            def transpose_rows(t, q):
                pe.wait_ge(c_in, t + 1)
                pe.wait_ge(c_xc, t + START - 1)
                for c in range(C):
                    last = nc.tensor.transpose(bank[q][:, c * P:(c + 1) * P], xt[:, q, c * P:(c + 1) * P], ident)
                last.then_inc(c_tr, 1)

            def up(t, q):
                e = pe.value_load(itab[0:1, 0, bass.ds(t, 1)], min_val=0, max_val=E - 1)
                pe.wait_ge(c_xc, t + (1 + START))
                pe.wait_ge(c_h, t + START - 1)
                for c in range(C):
                    last = mm(bank[2 + q][:, :], xc[:, q, c], w13[:, e, c].rearrange("p w n -> p (w n)"),
                              start=(c == 0), stop=(c == C - 1))
                last.then_inc(c_up, 1)

            def turn_hidden(t, q):
                pe.wait_ge(c_h, t + (1 + START))
                pe.wait_ge(c_hc, t + START - 1)
                for f in range(C):
                    last = nc.tensor.transpose(bank[6 + q][:, f * P:(f + 1) * P], hh[:, q, f], ident)
                last.then_inc(c_ht, 1)

            def down(t, q):
                e = pe.value_load(itab[0:1, 0, bass.ds(t, 1)], min_val=0, max_val=E - 1)
                pe.wait_ge(c_hc, t + (1 + START))
                pe.wait_ge(c_y, t + START - 1)
                for f in range(C):
                    last = mm(bank[4 + q][:, 0:N], hT[:, q, f], w2[:, e, f], start=(f == 0), stop=(f == C - 1))
                last.then_inc(c_dn, 1)

            transpose_rows(0, 0)
            up(0, 0)
            transpose_rows(1, 1)
            with pe.Fori(0, TILES // 2 - 1) as i:
                for q in range(2):
                    t = 2 * i + q
                    up(t + 1, 1 - q)
                    turn_hidden(t, q)
                    transpose_rows(t + 2, q)
                    down(t, q)
            up(TILES - 1, 1)
            turn_hidden(TILES - 2, 0)
            down(TILES - 2, 0)
            turn_hidden(TILES - 1, 1)
            down(TILES - 1, 1)

            with pe.Fori(0, B // 2) as i:
                for q in range(2):
                    b = 2 * i + q
                    pe.wait_ge(d_s, b + 1)
                    pe.wait_ge(d_o, b + START - 1)
                    for c in range(C):
                        for k in range(TT):
                            last = nc.tensor.transpose(bank[6 + q][:, c * FT + k * P:c * FT + (k + 1) * P],
                                                       ys[:, q, k, c * P:(c + 1) * P], ident)
                    last.then_inc(d_tr, 1)

        @block.scalar
        def _(act):
            for n in "b_lr b_th b_exp b_relu b_sq b_xn b_ex b_zc".split():
                act.sem_inc(s[n], START)
            act.sem_inc(a_xT, START)
            nc.scalar.preload_act_table(ACT.Exp)

            with act.Fori(0, GROUPS) as g:
                act.wait_ge(a_nb, g + 1)
                for j in range(GB):
                    for c in range(C):
                        ins = nc.scalar.activation(
                            xn[:, j, c].rearrange("p (t f) -> p f t", f=F),
                            xs[:, GB * g + j, c].rearrange("p (f t) -> p f t", t=T), ACT.Identity,
                            bias=gr[:, 1, j * C + c:j * C + c + 1], scale=gr[:, 0, j * C + c:j * C + c + 1])
                    ins.then_inc(a_xn, 1)
                for j in range(GB):
                    act.wait_ge(a_tr, GB * g + (j + 1 + START))
                    act.wait_ge(a_cp, g + 1)
                    nc.scalar.copy(xTg[:, j].rearrange("p h n -> p (h n)"), bank[1 + j % 2][:, :]).then_inc(a_xT, 1)
                act.wait_ge(a_pb, g + 1)
                nc.scalar.activation(eb[0:T, 1], eb[0:T, 0], ACT.Tanh, scale=0.5).then_inc(a_th, 1)
                act.wait_ge(a_es, g + 1)
                nc.scalar.activation(eb[0:T, 2], eb[0:T, 0], ACT.Exp, scale=0.5).then_inc(a_ex, 1)

            def copy_mix(b, p):
                act.wait_ge(s["b_gh"], done(b))
                act.wait_ge(s["b_pr"], done(b - 2))
                nc.scalar.copy(lr[0:T, p], bank[0][0:T, :]).then_inc(s["b_lr"], 1)

            def tanh(b, p):
                act.wait_ge(s["b_bs"], done(b))
                nc.scalar.activation(sg[:, p], sg[:, p], ACT.Tanh, scale=0.5).then_inc(s["b_th"], 1)

            def exps(b, p):
                act.wait_ge(s["b_max"], done(b))
                act.wait_ge(s["b_pn"], done(b - 1))
                for c in range(C):
                    ins = nc.scalar.activation(pe_[:, c], bank[1][:, c * N:(c + 1) * N], ACT.Exp,
                                               bias=nmx[:, p, 1, c:c + 1], scale=0.5,
                                               accum_out=es2[:, p, 0, c:c + 1])
                ins.then_inc(s["b_exp"], 1)

            def copy_features(b, p, c):
                for h in range(H):
                    act.wait_ge(s["b_z"], (b * 4 + (c * H + h + 1)) + START)
                    nc.scalar.copy(z[:, p, c, :, h], bank[4 + h][:, 0:K * P].rearrange("p (k o) -> p k o", k=K)
                                   ).then_inc(s["b_zc"], 1)

            def relu(b, p):
                act.wait_ge(s["b_main"], done(b))
                act.wait_ge(s["b_conv"], done(b - 1))
                nc.scalar.activation(sgT[:], bank[6][:, :].rearrange("p (h n) -> p h n", h=H), ACT.Relu
                                     ).then_inc(s["b_relu"], 1)

            def square(b, p):
                act.wait_ge(s["b_cen"], done(b))
                act.wait_ge(s["b_var"], done(b - 1))
                nc.scalar.activation(sq[:], y[:], ACT.Square).then_inc(s["b_sq"], 1)

            def normalise(b, p):
                act.wait_ge(s["b_nb"], done(b))
                act.wait_ge(s["b_tk"], done(b - 1))
                for c in range(C):
                    ins = nc.scalar.activation(xn2[:, c], xs[:, b, c], ACT.Identity, bias=gr2[:, 1, c:c + 1],
                                               scale=gr2[:, 0, c:c + 1])
                ins.then_inc(s["b_xn"], 1)

            def route_exp(b, p):
                act.wait_ge(s["b_sh"], done(b))
                nc.scalar.activation(rt[:, 1], rt[:, 0], ACT.Exp).then_inc(s["b_ex"], 1)

            def turn(i, q, ahead2, ahead1, now, back1, back2):
                if back1:
                    square(i - 1, 1 - q)
                if ahead1:
                    exps(i + 1, 1 - q)
                if ahead2:
                    copy_mix(i + 2, q)
                if now:
                    relu(i, q)
                if back2:
                    normalise(i - 2, q)
                if ahead1:
                    copy_features(i + 1, 1 - q, 0)
                if back2:
                    route_exp(i - 2, q)
                if ahead2:
                    tanh(i + 2, q)
                if ahead1:
                    copy_features(i + 1, 1 - q, 1)

            schedule(act, turn)

            if stop_after == "B":
                return
            act.sem_inc(c_y, START)
            act.sem_inc(c_hc, START)
            nc.scalar.preload_act_table(ACT.Gelu)

            def gelu(t, q):
                act.wait_ge(c_up, t + (1 + START))
                act.wait_ge(c_h, t + START - 1)
                nc.scalar.activation(gl[:, q].rearrange("p f k -> p (f k)"), bank[2 + q][:, 0:C * P], ACT.Gelu
                                     ).then_inc(c_gl, 1)

            def copy_y(t, q):
                act.wait_ge(c_dn, t + (1 + START))
                act.wait_ge(c_out, t + 3)
                nc.scalar.copy(yo[:, q], bank[4 + q][:, 0:N]).then_inc(c_y, 1)

            def copy_hidden(t, q):
                act.wait_ge(c_ht, t + (1 + START))
                act.wait_ge(c_dn, t + START - 1)
                nc.scalar.copy(hT[:, q].rearrange("p f k -> p (f k)"), bank[6 + q][:, 0:C * P]).then_inc(c_hc, 1)

            gelu(0, 0)
            with act.Fori(0, TILES // 2 - 1) as i:
                for q in range(2):
                    t = 2 * i + q
                    copy_hidden(t, q)
                    gelu(t + 1, 1 - q)
                    copy_y(t, q)
            copy_hidden(TILES - 2, 0)
            gelu(TILES - 1, 1)
            copy_y(TILES - 2, 0)
            copy_hidden(TILES - 1, 1)
            copy_y(TILES - 1, 1)

            with act.Fori(0, B // 2) as i:
                for q in range(2):
                    act.wait_ge(d_o, 2 * i + (q + 1 + START))
                    act.dma_start(out_v[:, 2 * i + q], oo[:, q]).then_inc(d_st[q], 16)
            for q in range(2):
                act.wait_ge(d_st[q], 16 * (B // 2))

        @block.gpsimd
        def _(pool):
            for n in "b_pn b_rs b_x1 b_rstd b_sc b_gb b_xb".split():
                pool.sem_inc(s[n], START)
            pool.sem_inc(c_out, 4)
            pool.sem_inc(a_cp, 1)
            nc.gpsimd.memset(half[:], -0.5).then_inc(wkp, 1)
            nc.gpsimd.memset(cnt[:], 0.0).then_inc(wkp, 1)
            nc.gpsimd.memset(fill[:], 0.0).then_inc(wkp, 1)
            pool.wait_ge(ld_c, 32)
            pool.wait_ge(wkp, 3)
            nc.gpsimd.tensor_scalar(fill[:, N:N + 1], cs(PCOL, 1), float(TOKENS), None, ALU.add).then_inc(wkp, 1)
            nc.gpsimd.tensor_scalar(fill[:, N + 1:N + 2], cs(PCOL, 1), 0.0, -1.0, ALU.mult, ALU.add).then_inc(wkp, 1)
            for k in range(TT):
                ins = nc.gpsimd.tensor_scalar(tok[:, k:k + 1], cs(PCOL, 1), float(k * P), None, ALU.add)
                ins.then_inc(wkp, 1)
            pool.wait_ge(wkp, 5 + TT)
            pool.sem_inc(fill_ready, 1)
            pool.sem_inc(zeros_ready, 1)

            with pool.Fori(0, GROUPS) as g:
                pool.wait_ge(a_ve, g + 1)
                nc.gpsimd.tensor_tensor(gr[:, 0], gd[:, 3], half[:, 0:GB * C], ALU.pow).then_inc(a_rstd, 1)
                pool.wait_ge(a_xT, GB * g + (GB + START))
                nc.gpsimd.tensor_copy(xT[:, bass.ds(GB * g, GB)], xTg[:]).then_inc(a_cp, 1)

            def fetch_mix(b, p):
                pool.wait_ge(s["b_gh"], done(b - 2))
                nc.gpsimd.tensor_copy(ghb[:, p], gh[:, b]).then_inc(s["b_gb"], 1)

            def fetch_xT(b, p):
                pool.wait_ge(s["b_conv"], done(b - 2))
                nc.gpsimd.tensor_copy(xTb[:, p], xT[:, b]).then_inc(s["b_xb"], 1)

            def scale_softmax(b, p):
                pool.wait_ge(s["b_rec"], done(b))
                pool.wait_ge(s["b_tr"], done(b - 1))
                pool.nop(nofuse=True)
                for c in range(C):
                    ins = nc.gpsimd.tensor_scalar(pn[:, c], pe_[:, c], es2[:, p, 1, c:c + 1], None, ALU.mult)
                ins.then_inc(s["b_pn"], 1)

            def ln_rstd(b, p):
                pool.wait_ge(s["b_var"], done(b))
                pool.nop(nofuse=True)
                step = Steps(pool, p_rs, b, 1)
                step(nc.gpsimd.tensor_scalar(s1[:, 2], s1[:, 1], 1.0 / T, EPS, ALU.mult, ALU.add))
                step.close()
                nc.gpsimd.tensor_tensor(rs[:].rearrange("p c o -> p (c o)"), s1[:, 2].rearrange("p c o -> p (c o)"),
                                        half[:], ALU.pow).then_inc(s["b_rs"], 1)

            def ln_out(b, p):
                pool.wait_ge(s["b_dn"], done(b))
                step = Steps(pool, p_x1, b, 2 * C)
                over = lambda a: a.rearrange("p (u t) -> p u t", u=1).to_broadcast([P, 16, T])
                for c in range(C):
                    step(nc.gpsimd.tensor_tensor(yg[:, c].rearrange("p (o t) -> p o t", t=T),
                                                 y[:, c].rearrange("p (t o) -> p o t", o=16), over(sm("gamma")), ALU.mult))
                    step(nc.gpsimd.tensor_tensor(yg[:, c].rearrange("p (o t) -> p o t", t=T),
                                                 yg[:, c].rearrange("p (o t) -> p o t", t=T), over(sm("beta")), ALU.add))
                step.close()
                nc.gpsimd.tensor_tensor(xs[:, b], xs[:, b], yg[:], ALU.add).then_inc(s["b_x1"], 1)

            def gn_rstd(b, p):
                pool.wait_ge(s["b_ve"], done(b))
                nc.gpsimd.tensor_tensor(gr2[:, 0], gd2[:, 3], half[:, 0:C], ALU.pow).then_inc(s["b_rstd"], 1)

            def scatter(b, q):
                pool.wait_ge(s["b_slot"], done(b))
                pool.wait_ge(s["b_tkc"], done(b))
                pool.nop(nofuse=True)
                for w in range(2):
                    for k in range(TT):
                        pool.indirect_dma_start(
                            xrows, bass.IndirectOffsetOnAxis(ap=slot[:, q, w, k:k + 1], axis=0),
                            xtok[:, q, k], None).then_inc(sc_done[q], 16)

            def turn(i, q, ahead2, ahead1, now, back1, back2):
                if ahead2:
                    fetch_mix(i + 2, q)
                if ahead1:
                    fetch_xT(i + 1, 1 - q)
                if back1:
                    ln_rstd(i - 1, 1 - q)
                if ahead1:
                    scale_softmax(i + 1, 1 - q)
                if back2:
                    gn_rstd(i - 2, q)
                if back1:
                    ln_out(i - 1, 1 - q)

            def landed(q, pairs):
                pool.wait_ge(sc_done[q], pairs * (16 * 2 * TT))
                pool.sem_inc(s["b_sc"], 1)

            pool.wait_ge(a_gh, GROUPS)
            schedule_pool(pool, turn, scatter, landed)

            if stop_after == "B":
                return
            def put_rows(t, q):
                pool.wait_ge(c_y, t + (1 + START))
                pool.wait_ge(c_de, t + 1)
                nc.gpsimd.tensor_copy(dest[:, q], dn[:, 1, t % 4]).then_inc(c_di, 1)
                pool.wait_ge(c_di, t + 1)
                pool.nop(nofuse=True)
                pool.indirect_dma_start(yrows, bass.IndirectOffsetOnAxis(ap=dest[:, q], axis=0),
                                        yo[:, q], None, bounds_check=2 * TOKENS - 1, oob_is_err=False
                                        ).then_inc(c_st[q], 16)

            put_rows(0, 0)
            with pool.Fori(0, TILES // 2 - 1) as i:
                put_rows(2 * i + 1, 1)
                pool.wait_ge(c_st[0], 16 * (i + 1))
                pool.sem_inc(c_out, 1)
                put_rows(2 * i + 2, 0)
                pool.wait_ge(c_st[1], 16 * (i + 1))
                pool.sem_inc(c_out, 1)
            put_rows(TILES - 1, 1)
            for q in range(2):
                pool.wait_ge(c_st[q], 16 * (TILES // 2))

        @block.vector
        def _(dve):
            V = nc.vector
            for n in "b_bs b_max b_rec b_A b_y b_cen b_var b_dn b_st b_q b_ve b_nb b_tkc b_sh b_M b_slot".split():
                dve.sem_inc(s[n], START)
            dve.sem_inc(a_rn, START)
            dve.wait_ge(ld_c, 32)
            blk3 = lambda n: blk.rearrange("p (t u) -> p t u", u=1).to_broadcast([P, TH, n])
            over_t = lambda a: a.rearrange("p (u n) -> p u n", u=1).to_broadcast([P, TH, a.shape[1]])
            for k in range(K):
                V.tensor_tensor(thetabd[:, k], over_t(sm("theta")[:, k * 16:(k + 1) * 16]), blk3(16), ALU.mult)
            V.tensor_tensor(rwbd[:], over_t(sm("rw")), blk3(16), ALU.mult)
            V.tensor_scalar(u3bd[:], blk, sm("u3"), None, ALU.mult)
            for c in range(C):
                V.tensor_copy(u2rep[:, c], over_t(sm("u2")[:, c * F:(c + 1) * F]))
            V.tensor_copy(i16w1[0:T, 0:T], cst[0:T, ID:ID + T])
            V.tensor_copy(i16w1[0:T, T:T + 1], sml[0:T, COL["w1"]:COL["w1"] + 1])
            step = Steps(dve, wk, 0, H * 4 + 2)
            step(V.tensor_tensor(negb[:], sm("tb"), sm("rb"), ALU.add))
            step(V.tensor_scalar(negb[:], negb[:], -1.0, None, ALU.mult))
            for h in range(H):
                def band(out_, dt):
                    q = BLK + dt + (1 - h)
                    on = cst[:, q:q + TH + 1].rearrange("p (t u) -> p t u", u=1).to_broadcast([P, TH + 1, 16])
                    w = sm("tw")[:, dt * 16:(dt + 1) * 16].rearrange("p (u n) -> p u n", u=1).to_broadcast([P, TH + 1, 16])
                    return V.tensor_tensor(out_.rearrange("p (t o) -> p t o", o=16), w, on, ALU.mult)
                band(convm[:, h], 0)
                step(band(convt[:, 0], 1))
                step(V.tensor_tensor(convm[:, h], convm[:, h], convt[:, 0], ALU.add))
                step(band(convt[:, 1], 2))
                step(V.tensor_tensor(convm[:, h], convm[:, h], convt[:, 1], ALU.add))
            step.close()
            dve.sem_inc(consts_ready, 1)
            dve.wait_ge(zeros_ready, 1)

            with dve.Fori(0, GROUPS) as g:
                step = Steps(dve, a_v, g, 9)
                dve.wait_ge(x_in, g + 1)
                for j in range(GB * C):
                    ins = V.bn_stats(st6[:, j], xs[:, GB * g + j // C, j % C])
                step(ins)
                dve.nop(nofuse=True)
                for j in range(GB * C):
                    ins = V.bn_aggr(mv[:, j], st6[:, j])
                ins.then_inc(a_stat, 1)
                dve.wait_ge(a_mean, g + 1)
                step(V.tensor_tensor(gd[:, 0], mv[:, :, 0], bank[0][:, 0:GB * C], ALU.subtract))
                V.tensor_copy(gd[:, 1], bank[0][:, 0:GB * C])
                step(V.tensor_tensor(gd[:, 0], gd[:, 0], gd[:, 0], ALU.mult))
                V.tensor_tensor(gd[:, 2], gd[:, 0], mv[:, :, 1], ALU.add).then_inc(a_q, 1)
                dve.wait_ge(a_var, g + 1)
                V.tensor_scalar(gd[:, 3], bank[0][:, 0:GB * C], EPS, None, ALU.add).then_inc(a_ve, 1)
                dve.wait_ge(a_rstd, g + 1)
                V.scalar_tensor_tensor(out=gr[:, 1], in0=gd[:, 1], scalar=-1.0, in1=gr[:, 0], op0=ALU.mult,
                                       op1=ALU.mult).then_inc(a_nb, 1)
                dve.wait_ge(a_av, g + 1)
                a3 = bank[3][:, 0:GB * H].rearrange("p (j u) -> p j u", u=1).to_broadcast([P, GB * H, TH])
                b3 = blk.rearrange("p (u t) -> p u t", u=1).to_broadcast([P, GB * H, TH])
                V.tensor_tensor(aind[:].rearrange("p b h t -> p (b h) t"), a3, b3, ALU.mult)
                V.tensor_copy(rn[:].rearrange("p c b t -> p (c b t)"), bank[3][:, 16:16 + C * GB * T]).then_inc(a_rn, 1)
                dve.wait_ge(a_cr, g + 1)
                V.tensor_copy(crep[:].rearrange("p b t -> p (b t)"), bank[4][:, 0:GB * T]).then_inc(a_ai, 1)
                dve.wait_ge(a_pr, g + 1)
                bet = sml[0:T, COL["bet"]:COL["bet"] + T].rearrange("p (u t) -> p u t", u=1).to_broadcast([T, GB, T])
                V.tensor_tensor(eb[0:T, 0], bank[5][0:T, 0:GB * T].rearrange("p (b t) -> p b t", b=GB), bet,
                                ALU.add).then_inc(a_pb, 1)
                dve.wait_ge(a_er, g + 1)
                e5 = bank[5][0:T, 0:GB * T].rearrange("p (b t) -> p b t", b=GB)
                wide = lambda a: a.rearrange("p (b u) -> p b u", u=1).to_broadcast([T, GB, T])
                step(V.tensor_reduce(es[0:T, 0], e5, AX, ALU.max))
                V.tensor_tensor(eb[0:T, 0], e5, wide(es[0:T, 0]), ALU.subtract).then_inc(a_es, 1)
                dve.wait_ge(a_ex, g + 1)
                step(V.tensor_reduce(es[0:T, 1], eb[0:T, 2], AX, ALU.add))
                step(V.reciprocal(es[0:T, 2], es[0:T, 1]))
                step(V.tensor_tensor(eb[0:T, 0], eb[0:T, 2], wide(es[0:T, 2]), ALU.mult))
                src = eb[0:T, 0].rearrange("p b (t u) -> p (b t) u", u=1).to_broadcast([T, GB * T, F])
                V.tensor_copy(erep[0:T].rearrange("p b t f -> p (b t) f"), src).then_inc(a_et, 1)
                dve.wait_ge(a_rep, g + 1)
                r6 = bank[6][:, 0:GB * H * (T + 1)].rearrange("p (j t) -> p j t", t=T + 1)
                gg = gh[:, bass.ds(GB * g, GB)].rearrange("p b h q t -> p (b h) q t")
                step(V.tensor_copy(aind[:].rearrange("p b h t -> p (b h) t")[:, :, 0], r6[:, :, T]))
                step(V.tensor_tensor(gg[:, :, 0], sm("w2").rearrange("p (u t) -> p u t", u=1).to_broadcast([P, GB * H, T]),
                                     aind[:].rearrange("p b h t -> p (b h) t")[:, :, 0:1].to_broadcast([P, GB * H, T]), ALU.mult))
                V.tensor_scalar(gg[:, :, 1], r6[:, :, 0:T], sm("w3"), None, ALU.mult).then_inc(a_gh, 1)
                step.close()

            def add_bs(b, p):
                dve.wait_ge(s["b_pr"], done(b))
                dve.wait_ge(s["b_L"], done(b - 2))
                V.tensor_tensor(sg[:, p].rearrange("p c n -> p (c n)"), bank[1][:, :],
                                bs[:].rearrange("p c n -> p (c n)"), ALU.add).then_inc(s["b_bs"], 1)

            def row_max(b, p):
                dve.wait_ge(s["b_L"], done(b))
                step = Steps(dve, v_mx, b, 1)
                step(V.tensor_reduce(nmx[:, p, 0], bank[1][:, :].rearrange("p (c n) -> p c n", c=C), AX, ALU.max))
                step.close()
                V.tensor_scalar(nmx[:, p, 1], nmx[:, p, 0], -0.5, None, ALU.mult).then_inc(s["b_max"], 1)

            def recip(b, p):
                dve.wait_ge(s["b_exp"], done(b))
                V.reciprocal(es2[:, p, 1], es2[:, p, 0]).then_inc(s["b_rec"], 1)

            def weigh(b, p):
                dve.wait_ge(s["b_tr"], done(b))
                dve.wait_ge(s["b_main"], done(b - 1))
                for c in range(C):
                    p3 = bank[3][:, c * N:(c + 1) * N].rearrange("p (u n) -> p u n", u=1).to_broadcast([P, K, N])
                    ins = V.tensor_tensor(A[:, c], p3, chebs[:, c], ALU.mult)
                ins.then_inc(s["b_A"], 1)

            y_ot = y[:].rearrange("p c (t o) -> p c o t", o=16)
            thin = lambda a: a.rearrange("p c (o u) -> p (c o) u", u=1).to_broadcast([P, C * 16, T])
            yv = [y[:, c].rearrange("p (t o) -> p o t", o=16) for c in range(C)]
            th = lambda a, c: a[:, c].rearrange("p (o u) -> p o u", u=1).to_broadcast([P, 16, T])

            def ln_a(b, p):
                dve.wait_ge(s["b_conv"], done(b))
                dve.wait_ge(s["b_x1"], done(b - 1))
                step = Steps(dve, v_ln, b, 2)
                nb = negb[:].rearrange("p (u o) -> p u o", u=1).to_broadcast([P, C * T, 16])
                ins = V.tensor_tensor(y[:].rearrange("p c (t o) -> p (c t) o", o=16),
                                      bank[7][:, :].rearrange("p (k o) -> p k o", o=16), nb, ALU.max)
                ins.then_inc(s["b_y"], 1)
                dve.wait_ge(s["b_y"], done(b))
                for c in range(C):
                    ins = V.tensor_reduce(s1[:, 0, c], yv[c], AX, ALU.add)
                step(ins)
                for c in range(C):
                    ins = V.scalar_tensor_tensor(out=yv[c], in0=th(s1[:, 0], c), scalar=-1.0 / T, in1=yv[c],
                                                 op0=ALU.mult, op1=ALU.add)
                step(ins)
                step.close()
                dve.sem_inc(s["b_cen"], 1)

            def ln_b(b, p):
                dve.wait_ge(s["b_sq"], done(b))
                for c in range(C):
                    ins = V.tensor_reduce(s1[:, 1, c], sq[:, c].rearrange("p (t o) -> p o t", o=16), AX, ALU.add)
                ins.then_inc(s["b_var"], 1)

            def ln_c(b, p):
                dve.wait_ge(s["b_rs"], done(b))
                for c in range(C):
                    ins = V.tensor_tensor(yv[c], yv[c], th(rs[:], c), ALU.mult)
                ins.then_inc(s["b_dn"], 1)

            def gn_stats(b, p):
                dve.wait_ge(s["b_x1"], done(b))
                step = Steps(dve, v_gn, b, 3)
                for c in range(C):
                    ins = V.bn_stats(st62[:, c], xs[:, b, c])
                step(ins)
                dve.nop(nofuse=True)
                for c in range(C):
                    ins = V.bn_aggr(mv2[:, c], st62[:, c])
                ins.then_inc(s["b_st"], 1)
                dve.wait_ge(s["b_g1"], done(b))
                step(V.tensor_tensor(gd2[:, 0], mv2[:, :, 0], bank[2][:, 0:C], ALU.subtract))
                V.tensor_copy(gd2[:, 1], bank[2][:, 0:C])
                step(V.tensor_tensor(gd2[:, 0], gd2[:, 0], gd2[:, 0], ALU.mult))
                V.tensor_tensor(gd2[:, 2], gd2[:, 0], mv2[:, :, 1], ALU.add).then_inc(s["b_q"], 1)
                step.close()

            def gn_scale(b, p):
                dve.wait_ge(s["b_g2"], done(b))
                V.tensor_scalar(gd2[:, 3], bank[2][:, 0:C], EPS, None, ALU.add).then_inc(s["b_ve"], 1)
                dve.wait_ge(s["b_rstd"], done(b))
                V.scalar_tensor_tensor(out=gr2[:, 1], in0=gd2[:, 1], scalar=-1.0, in1=gr2[:, 0], op0=ALU.mult,
                                       op1=ALU.mult).then_inc(s["b_nb"], 1)

            wide8 = lambda a: a.rearrange("p (k u) -> p k u", u=1).to_broadcast([P, TT, E])
            row8 = lambda a: a.rearrange("p (u e) -> p u e", u=1).to_broadcast([P, TT, E])

            def route_a(b, p):
                dve.wait_ge(s["b_tk"], done(b))
                dve.wait_ge(s["b_sc"], done(b - 2))
                V.tensor_copy(xtok[:, p, :, 0:N], bank[0][:, :].rearrange("p (k n) -> p k n", k=TT)).then_inc(s["b_tkc"], 1)
                V.tensor_copy(xtok[:, p, :, N], tok[:])
                step = Steps(dve, v_rt, b, 3)
                lg = bank[2][:, 16:16 + TT * E].rearrange("p (k e) -> p k e", k=TT)
                step(V.tensor_reduce(r2[:, 0], lg, AX, ALU.max))
                step(V.tensor_scalar(tok[:], tok[:], float(FT), None, ALU.add))
                step(V.tensor_tensor(rt[:, 0], lg, wide8(r2[:, 0]), ALU.subtract))
                step.close()
                dve.sem_inc(s["b_sh"], 1)

            def route_b(b, p):
                dve.wait_ge(s["b_ex"], done(b))
                step = Steps(dve, v_rt2, b, 27)
                step(V.tensor_reduce(r2[:, 1], rt[:, 1], AX, ALU.add))
                step(V.reciprocal(r2[:, 2], r2[:, 1]))
                step(V.tensor_tensor(rt[:, 2], rt[:, 1], wide8(r2[:, 2]), ALU.mult))
                src = rt[:, 2]
                for w in range(2):
                    step(V.tensor_reduce(r2[:, 3 + w], src, AX, ALU.max))
                    step(V.tensor_tensor(rt[:, 3], src, wide8(r2[:, 3 + w]), ALU.is_equal))
                    step(V.tensor_tensor(rt[:, 4], rt[:, 3], row8(cs(DSC, E)), ALU.mult))
                    step(V.tensor_reduce(r2[:, 5 + w], rt[:, 4], AX, ALU.max))
                    step(V.tensor_tensor(rt[:, 7 + w], rt[:, 4], wide8(r2[:, 5 + w]), ALU.is_equal))
                    if w == 0:
                        step(V.scalar_tensor_tensor(out=rt[:, 5], in0=rt[:, 7], scalar=-2.0, in1=rt[:, 2],
                                                    op0=ALU.mult, op1=ALU.add))
                        src = rt[:, 5]
                step(V.tensor_tensor(rt[:, 9], rt[:, 7], rt[:, 8], ALU.add))
                dve.sem_inc(s["b_M"], 1)
                step(V.tensor_scalar(xtok[:, p, :, N + 1], r2[:, 5], -1.0, float(E), ALU.mult, ALU.add))
                step(V.tensor_tensor(r2[:, 7], r2[:, 3], r2[:, 4], ALU.add))
                step(V.reciprocal(r2[:, 8], r2[:, 7]))
                wb = wts[:, b]
                V.tensor_tensor(wb[:, 0], r2[:, 3], r2[:, 8], ALU.mult)
                step(V.tensor_tensor(wb[:, 1], r2[:, 4], r2[:, 8], ALU.mult))
                dve.wait_ge(s["b_pf"], done(b))
                pf = bank[2][:, 64:64 + TT * E].rearrange("p (k e) -> p k e", k=TT)
                step(V.tensor_tensor(rt[:, 10], pf, row8(cnt[:]), ALU.add))
                step(V.tensor_tensor(cnt[:], cnt[:], bank[2][:, 80:80 + E], ALU.add))
                step(V.tensor_tensor(rt[:, 10], rt[:, 10], row8(cs(EBASE, E)), ALU.add))
                for w in range(2):
                    step(V.tensor_tensor(rt[:, 3 + w], rt[:, 10], rt[:, 7 + w], ALU.mult))
                    step(V.tensor_reduce(slotf[:, w], rt[:, 3 + w], AX, ALU.add))
                step(V.tensor_copy(slot[:, p].rearrange("p w k -> p (w k)"), slotf[:].rearrange("p w k -> p (w k)")))
                step.close()
                dve.sem_inc(s["b_slot"], 1)

            def turn(i, q, ahead2, ahead1, now, back1, back2):
                if back1:
                    ln_a(i - 1, 1 - q)
                if ahead1:
                    row_max(i + 1, 1 - q)
                if back2:
                    gn_stats(i - 2, q)
                if back1:
                    ln_b(i - 1, 1 - q)
                if ahead1:
                    recip(i + 1, 1 - q)
                if back2:
                    gn_scale(i - 2, q)
                if back1:
                    ln_c(i - 1, 1 - q)
                if ahead1:
                    weigh(i + 1, 1 - q)
                if back2:
                    route_a(i - 2, q)
                if ahead2:
                    add_bs(i + 2, q)
                if back2:
                    route_b(i - 2, q)

            dve.wait_ge(ld_w, 48)
            schedule(dve, turn)

            if stop_after == "B":
                return
            step = Steps(dve, v_tb, 0, 16)
            step(V.tensor_scalar(nt[:, 0], cnt[:], float(P - 1), None, ALU.add))
            step(V.tensor_copy(ci[:, 0], nt[:, 0]))
            step(V.tensor_scalar(ci[:, 1], ci[:, 0], 7, None, ALU.arith_shift_right))
            step(V.tensor_copy(nt[:, 1], ci[:, 1]))
            step(V.tensor_tensor_scan(nt[:, 2], cst[:, ONE:ONE + E], nt[:, 1], 0.0, ALU.mult, ALU.add))
            tl = lambda a: a.rearrange("p (u e) -> p u e", u=1).to_broadcast([P, TILES, E])
            ti = cs(TIDX, TILES)
            step(V.tensor_tensor(ge[:, 0], tl(nt[:, 2]), ti.rearrange("p (t u) -> p t u", u=1).to_broadcast([P, TILES, E]),
                                 ALU.is_le))
            step(V.tensor_reduce(tb3[:, 0], ge[:, 0], AX, ALU.add))
            step(V.tensor_tensor(ge[:, 1], ge[:, 0], tl(nt[:, 1]), ALU.mult))
            step(V.tensor_reduce(tb3[:, 1], ge[:, 1], AX, ALU.add))
            step(V.tensor_tensor(tb3[:, 2], ti, tb3[:, 1], ALU.subtract))
            step(V.tensor_scalar(tb3[:, 3], tb3[:, 0], float(CAP), None, ALU.mult))
            step(V.scalar_tensor_tensor(out=tb3[:, 4], in0=tb3[:, 2], scalar=float(P), in1=tb3[:, 3], op0=ALU.mult,
                                        op1=ALU.add))
            step(V.tensor_scalar(itab[:, 1], tb3[:, 4], float(E * CAP), None, ALU.min))
            step(V.tensor_scalar(itab[:, 0], tb3[:, 0], float(E - 1), None, ALU.min))
            step(V.tensor_tensor(fillf[:], cnt[:], cs(EBASE, E), ALU.add))
            step(V.tensor_copy(filli[:], fillf[:]))
            step.close()
            dve.sem_inc(tables, 1)

            dve.sem_inc(c_xc, START)
            dve.sem_inc(c_h, START)

            def copy_x(t, q):
                dve.wait_ge(c_tr, t + 1)
                dve.wait_ge(c_up, t + START - 1)
                V.tensor_copy(xc[:, q].rearrange("p c k -> p (c k)"), bank[q][:, 0:C * P]).then_inc(c_xc, 1)
                dve.wait_ge(c_out, t + 1)
                V.tensor_scalar(dn[:, 0, t % 4], xt[:, q, N + 1:N + 2], tb3[:, 0, bass.ds(t, 1)], float(TOKENS),
                                ALU.not_equal, ALU.mult).then_inc(c_dd, 1)
                dve.wait_ge(c_dd, t + 1)
                V.tensor_tensor(dn[:, 1, t % 4], dn[:, 0, t % 4], xt[:, q, N:N + 1], ALU.add).then_inc(c_de, 1)

            def gate(t, q):
                dve.wait_ge(c_gl, t + 1)
                dve.wait_ge(c_ht, t + START - 1)
                V.tensor_tensor(hh[:, q].rearrange("p f k -> p (f k)"), bank[2 + q][:, C * P:2 * C * P],
                                gl[:, q].rearrange("p f k -> p (f k)"), ALU.mult).then_inc(c_h, 1)

            copy_x(0, 0)
            copy_x(1, 1)
            gate(0, 0)
            with dve.Fori(0, TILES // 2 - 1) as i:
                for q in range(2):
                    t = 2 * i + q
                    copy_x(t + 2, q)
                    gate(t + 1, 1 - q)
            gate(TILES - 1, 1)

            dve.sem_inc(d_o, START)
            def combine(b, q, stored):
                dve.wait_ge(d_in, b + 1)
                for k in range(TT):
                    ins = V.tensor_scalar(ys[:, q, k], yy[:, q, 0, k], wts[:, b, 0, k:k + 1], None, ALU.mult)
                ins.then_inc(d_m, 1)
                dve.wait_ge(d_m, b + 1)
                for k in range(TT):
                    ins = V.scalar_tensor_tensor(out=ys[:, q, k], in0=yy[:, q, 1, k], scalar=wts[:, b, 1, k:k + 1],
                                                 in1=ys[:, q, k], op0=ALU.mult, op1=ALU.add)
                ins.then_inc(d_s, 1)
                dve.wait_ge(d_tr, b + 1)
                if stored is not None:
                    dve.wait_ge(d_st[q], stored)
                V.tensor_tensor(oo[:, q].rearrange("p c n -> p (c n)"), bank[6 + q][:, :],
                                xs[:, b].rearrange("p c n -> p (c n)"), ALU.add).then_inc(d_o, 1)

            for q in range(2):
                combine(q, q, None)
            with dve.Fori(1, B // 2) as i:
                for q in range(2):
                    combine(2 * i + q, q, 16 * i)


def constants():
    import numpy as np

    a = np.zeros((P, NCONST), np.float32)
    p = np.arange(P)
    a[:, ID:ID + P] = np.eye(P)
    a[:, TRI:TRI + P] = p[:, None] < p[None, :]
    a[:, ONE:ONE + P] = 1.0
    a[:, GRP:GRP + P] = (p[:, None] // 8 == p[None, :] // 8) / 8.0
    a[:, BLK:BLK + TH + 4] = np.arange(TH + 4)[None, :] == p[:, None] // F + 2
    a[:, DSC:DSC + E] = E - np.arange(E)
    a[:, EBASE:EBASE + E] = np.arange(E) * CAP
    a[:, TIDX:TIDX + TILES] = np.arange(TILES)
    a[:, PCOL] = p
    return a


def kernel(**inputs):
    import numpy as np
    import concourse.bacc as bacc
    from concourse.bass_utils import run_bass_kernel_spmd as run

    g = {k: np.asarray(v) for k, v in inputs.items()}
    c = {k[8:]: v for k, v in g.items() if k.startswith("L0_conv_")}
    m = {k[8:]: v for k, v in g.items() if k.startswith("L1_conv_")}
    small = np.zeros((P, NSMALL), np.float32)

    def put(name, a):
        small[:a.shape[0], COL[name]:COL[name] + SIZES[name]] = a

    down = lambda a: np.tile(a, (TH, 1))
    every = lambda a: np.tile(a.reshape(1, -1), (P, 1))
    rows = lambda a: np.moveaxis(a.reshape(a.shape[:-2] + (C, P, a.shape[-1])), -2, 0)
    put("theta", down(c["Theta"].transpose(1, 0, 2).reshape(F, K * 16)))
    put("rw", down(c["rw"].T))
    put("tw", down(c["tw"][:, :, 0, :].transpose(1, 2, 0).reshape(16, 48)))
    put("w2", down(c["W2"]))
    put("u3", down(c["U3"].reshape(F, 1)))
    put("w3", down(c["W3"].reshape(F, 1)))
    put("tb", every(c["tb"]))
    put("rb", every(c["rb"]))
    put("gamma", every(c["gamma"]))
    put("beta", every(c["beta"]))
    put("u1", c["U1"].reshape(C, P).T)
    put("u2", c["U2"].reshape(F, C, P).transpose(2, 1, 0).reshape(P, C * F))
    put("gate", m["gate_w"].reshape(E, C, P).transpose(2, 1, 0).reshape(P, C * E))
    put("vet", c["V_e"].T)
    put("bet", c["b_e"][0].T)
    put("w1", c["W1"].reshape(T, 1))
    arrays = dict(x=g["x"], consts=constants(), small=small, cheb=c["cheb"].reshape(K, C, P, N).transpose(2, 1, 0, 3),
                  vst=rows(c["V_s"].T), bst=rows(c["b_s"][0].T), 
                  w13t=rows(np.concatenate([m["w1"].transpose(0, 2, 1), m["w3"].transpose(0, 2, 1)], -1)
                            ).reshape(P, E, C, 2, N), w2t=rows(m["w2"].transpose(0, 2, 1)))
    arrays = {k: np.ascontiguousarray(v) for k, v in arrays.items()}

    nc = bacc.Bacc("TRN2", target_bir_lowering=False, num_devices=1)
    args = {k: nc.dram_tensor(f"{k}_in", v.shape, F32, kind="ExternalInput").ap() for k, v in arrays.items()}
    xrows = nc.dram_tensor("xrows", (E * CAP + P, ROW), F32, kind="Internal").ap()
    yrows = nc.dram_tensor("yrows", (2 * TOKENS + P, N), F32, kind="Internal").ap()
    out = nc.dram_tensor("out", (B, N, F, T), F32, kind="ExternalOutput").ap()
    build(nc, xrows=xrows, yrows=yrows, out=out, **args)
    r = run(nc, [{f"{k}_in": v for k, v in arrays.items()}], core_ids=[0])
    return r.results[0]["out"]
```

```python
from contextlib import ExitStack

import concourse.bass as bass
from concourse import mybir

F32 = mybir.dt.float32
I32 = mybir.dt.int32
BF16 = mybir.dt.bfloat16
ALU = mybir.AluOpType
ACT = mybir.ActivationFunctionType
AX = mybir.AxisListType.X

P = 128
B, N, F, T = 16, 256, 16, 16
C = N // P
FT = F * T
TH = P // F
H = FT // P
K = 3
BAND = (TH + 1) * F
GB = 4
GROUPS = B // GB
E = 8
TT = FT // P
TOKENS = B * FT
CAP = TOKENS + P
ROW = N + 2
TILES = 2 * TOKENS // P + E
EPS = 1e-5
START = 2

ID, TRI, ONE, GRP = 0, P, 2 * P, 3 * P
BLK = 4 * P
DSC = BLK + TH + 4
EBASE = DSC + E
TIDX = EBASE + E
PCOL = TIDX + TILES
REP = PCOL + 1
NCONST = REP + FT

SIZES = dict(theta=K * 16, rw=16, tw=3 * 16, w2=T, w3=1, tb=16, rb=16, gamma=T, beta=T,
             u3=F, uu=C * 48, gate=C * E, vet=T, bet=T, w1=1)
COL, NSMALL = {}, 0
for _name, _size in SIZES.items():
    COL[_name] = NSMALL
    NSMALL += _size


NV = C * 16 + C
MAGIC = 1597463007.0


def done(b):
    return b + (1 + START)


class Steps:

    def __init__(self, eng, sem, turn, per_turn):
        self.eng, self.sem, self.base, self.per, self.n = eng, sem, turn * per_turn, per_turn, 0

    def __call__(self, ins):
        ins.then_inc(self.sem, 1)
        self.n += 1
        self.eng.wait_ge(self.sem, self.base + self.n)

    def then(self, ins):
        ins.then_inc(self.sem, 1)
        self.n += 1
        yield
        self.eng.wait_ge(self.sem, self.base + self.n)

    def close(self):
        assert self.n == self.per, (self.n, self.per)


def weave(*chains, along=()):
    chains = list(chains)
    while chains:
        for chain in tuple(chains):
            if next(chain, chains) is chains:
                chains.remove(chain)
        for chain in along:
            next(chain, None)


def schedule(eng, turn):
    for i in range(-2, 4):
        turn(i, i % 2, True, i + 1 >= 0, i >= 0, i >= 1, i >= 2, i >= 3)
    with eng.Fori(0, (B - 6) // 2) as j:
        for q in range(2):
            turn(2 * j + (4 + q), q, *(True,) * 6)
    for i in range(B - 2, B + 3):
        turn(i, i % 2, False, i + 1 < B, i < B, i - 1 < B, i - 2 < B, True)


def build(nc, x, consts, small, cheb, vst, bst, w13t, w2t, xrows, yrows, out, stop_after=None):
    with ExitStack() as ctx:
        def sb(name, shape, dt=F32):
            return ctx.enter_context(nc.sbuf_tensor(name, [P] + shape, dt))

        def sem(name):
            return ctx.enter_context(nc.semaphore(name))

        bank = [ctx.enter_context(nc.psum_tensor(f"bank{i}", [P, 512], F32)) for i in range(8)]

        cst = sb("cst", [NCONST])
        sml = sb("sml", [NSMALL])
        xs = sb("xs", [B, C, FT])
        xT = sb("xT", [B, H, N])
        xTb = sb("xTb", [2, H, N])
        ghb = sb("ghb", [2, H, 48])
        chebs = sb("chebs", [C, K, N])
        vs = sb("vs", [C, N])
        bs = sb("bs", [C, N])
        w13 = sb("w13", [E, C, 2, N])
        w2 = sb("w2", [E, C, N])
        thetabd = sb("thetabd", [K, TH, 16])
        rwbd = sb("rwbd", [TH, 16])
        convm = sb("convm", [H, BAND])
        convt = sb("convt", [2, BAND])
        negb = sb("negb", [16])
        tri = sb("tri", [P], BF16)
        one = sb("one", [P], BF16)
        vr = sb("vr", [NV])
        vq = sb("vq", [5, NV])
        i16w1 = sb("i16w1", [T + 1])
        zs, As, xs1 = 2 * C * K * H * P, 2 * C * K * N, GB * C * FT
        work = sb("work", [zs + As + 2 * C * FT])
        z = work[:, 0:zs].rearrange("p (b c k h n) -> p b c k h n", b=2, c=C, k=K, h=H)
        A = work[:, zs:zs + As].rearrange("p (b c k n) -> p b c k n", b=2, c=C, k=K)
        y = work[:, zs + As:].rearrange("p (b c n) -> p b c n", b=2, c=C)
        xn = work[:, 0:xs1].rearrange("p (b c n) -> p b c n", b=GB, c=C)
        uq = work[:, xs1:xs1 + GB * FT].rearrange("p (j f) -> p j f", f=F)
        st6 = sb("st6", [GB * C, 6])
        mv = sb("mv", [GB * C, 2])
        gd = sb("gd", [4, GB * C])
        gr = sb("gr", [2, GB * C])
        ca = sb("ca", [2, GB, T])
        ej = sb("ej", [GB, T + 1])
        eb = sb("eb", [3, GB, T])
        es = sb("es", [4, GB])
        mk = sb("mk", [F])
        gh = sb("gh", [B, H, 48])
        lr = sb("lr", [2, 2 * N])
        sg = sb("sg", [2, C, N])
        nmx = sb("nmx", [2, 2, C])
        es2 = sb("es2", [2, 2, C])
        pe_ = sb("pe_", [C, N])
        pn = sb("pn", [C, N])
        sgT = sb("sgT", [H, N])
        sq = sb("sq", [C, FT])
        s1 = sb("s1", [C, 16])
        yg = sb("yg", [C, FT])
        st62 = sb("st62", [C, 6])
        mv2 = sb("mv2", [C, 2])
        gd2 = sb("gd2", [4, C])
        gr2 = sb("gr2", [2, C])
        xn2 = sb("xn2", [C, FT])
        xtok = sb("xtok", [2, TT, ROW])
        tok = sb("tok", [TT])
        lgT = sb("lgT", [FT])
        mb = sb("mb", [TT, E], BF16)
        rt = sb("rt", [12, TT, E])
        r2 = sb("r2", [10, TT])
        wts = sb("wts", [B, 2, TT])
        cnt = sb("cnt", [E])
        slotf = sb("slotf", [2, TT])
        slot = sb("slot", [2, 2, TT], I32)
        ci = sb("ci", [2, E], I32)
        nt = sb("nt", [3, E])
        ge = sb("ge", [2, TILES, E])
        tb3 = sb("tb3", [5, TILES])
        itab = sb("itab", [2, TILES], I32)
        filli = sb("filli", [E], I32)
        fillf = sb("fillf", [E])
        fill = sb("fill", [ROW])
        dest = sb("dest", [4, 1], I32)
        room = xT[:].rearrange("p b h n -> p (b h n)")
        used = [0]

        def over_xT(*shape):
            size = 1
            for d in shape:
                size *= d
            a = room[:, used[0]:used[0] + size]
            used[0] += size
            names = " ".join("abcd"[:len(shape)])
            return a.rearrange(f"p ({names}) -> p {names}", **dict(zip(names.split(), shape)))

        xt = over_xT(2, ROW)
        xc = over_xT(2, C, P)
        gl = over_xT(2, C, P)
        hh = over_xT(2, C, P)
        hT = over_xT(2, C, P)
        yo = over_xT(4, N)
        dn = over_xT(2, 4, 1)
        used[0] = 0
        yy = over_xT(4, 2, TT, N)
        ym = over_xT(2, TT, N)
        ys = over_xT(2, TT, N)
        oo = over_xT(2, C, FT)

        ld_c = sem("ld_c"); ld_w = sem("ld_w"); ld_m = sem("ld_m")
        ld_x = [sem(f"ld_x{i}") for i in range(2)]
        x_in = sem("x_in")
        wk = sem("wk"); wkp = sem("wkp"); consts_ready = sem("consts_ready"); zeros_ready = sem("zeros_ready")
        a_v = sem("a_v"); a_rq = sem("a_rq"); a_w = sem("a_w")
        a_stat = sem("a_stat"); a_mean = sem("a_mean"); a_q = sem("a_q"); a_var = sem("a_var"); a_nb = sem("a_nb")
        a_xnv = sem("a_xnv"); a_xna = sem("a_xna"); a_tr = sem("a_tr"); a_xT = sem("a_xT"); a_uq = sem("a_uq")
        a_uc = sem("a_uc"); a_ca = sem("a_ca"); a_pr = sem("a_pr"); a_pb = sem("a_pb"); a_th = sem("a_th")
        a_er = sem("a_er"); a_es = sem("a_es"); a_ex = sem("a_ex"); a_et = sem("a_et"); a_ej = sem("a_ej")
        a_ec = sem("a_ec"); a_rep = sem("a_rep"); a_gh = sem("a_gh")
        names = ("b_gh b_lr b_pr b_bs b_th b_L b_max b_exp b_rec b_pn b_tr b_A b_z b_zc b_main b_relu b_conv "
                 "b_y b_cen b_sq b_var b_dn b_x1 b_st b_g1 b_q b_g2 b_nb b_xn b_tk b_tkc b_gt b_gtc b_lg "
                 "b_sh b_ex b_M b_pf b_slot b_sc b_gb b_xb").split()
        s = {n: sem(n) for n in names}
        v_ln = sem("v_ln"); v_gn = sem("v_gn"); v_rt = sem("v_rt"); v_rt2 = sem("v_rt2"); v_rt3 = sem("v_rt3"); v_lq = sem("v_lq"); v_gq = sem("v_gq"); v_sc = sem("v_sc"); z_gh = sem("z_gh")
        p_x1 = sem("p_x1"); v_mx = sem("v_mx"); tok_ready = sem("tok_ready")
        sc_done = [sem("sc_done0"), sem("sc_done1")]
        v_tb = sem("v_tb"); tables = sem("tables"); fill_ready = sem("fill_ready"); fill_done = sem("fill_done")
        rows_ready = sem("rows_ready")
        d_ym = sem("d_ym"); c_ld = [sem("c_ld0"), sem("c_ld1")]; c_in = sem("c_in"); c_tr = sem("c_tr"); c_xc = sem("c_xc"); c_up = sem("c_up")
        c_gl = sem("c_gl"); c_h = sem("c_h"); c_ht = sem("c_ht"); c_hc = sem("c_hc"); c_dn = sem("c_dn"); c_y = sem("c_y"); c_dd = sem("c_dd")
        c_de = sem("c_de"); c_di = sem("c_di")
        c_st = [sem(f"c_st{i}") for i in range(4)]; c_out = sem("c_out")
        d_ld = [sem(f"d_ld{i}") for i in range(4)]; d_in = sem("d_in"); d_m = sem("d_m"); d_s = sem("d_s"); d_tr = sem("d_tr")
        d_o = sem("d_o"); d_st = [sem("d_st0"), sem("d_st1")]; d_out = sem("d_out")

        cs = lambda a, n: cst[:, a:a + n]
        sm = lambda name: sml[:, COL[name]:COL[name] + SIZES[name]]
        ident = cs(ID, P)
        blk = cs(BLK + 2, TH)

        x_v = x.rearrange("b (c p) f t -> p b c (f t)", p=P)
        out_v = out.rearrange("b (c p) f t -> p b c (f t)", p=P)
        y_v = yrows[0:2 * TOKENS, :].rearrange("(w b k p) n -> p w b k n", w=2, b=B, k=TT)

        block = ctx.enter_context(nc.Block())

        @block.sync
        def _(sp):
            sp.dma_start(cst[:], consts).then_inc(ld_c, 16)
            sp.dma_start(sml[:], small).then_inc(ld_c, 16)
            for g in range(GROUPS):
                if g >= 2:
                    sp.wait_ge(ld_x[g % 2], 16 * (g // 2))
                    sp.sem_inc(x_in, 1)
                sp.dma_start(xs[:, g * GB:(g + 1) * GB], x_v[:, g * GB:(g + 1) * GB]).then_inc(ld_x[g % 2], 16)
            for g in range(GROUPS - 2, GROUPS):
                sp.wait_ge(ld_x[g % 2], 16 * (g // 2 + 1))
                sp.sem_inc(x_in, 1)
            sp.dma_start(chebs[:], cheb).then_inc(ld_w, 16)
            sp.dma_start(vs[:], vst).then_inc(ld_w, 16)
            sp.dma_start(bs[:], bst).then_inc(ld_w, 16)
            for dst, src in ((w13, w13t), (w2, w2t)):
                sp.dma_start(dst[:], src).then_inc(ld_m, 16)
            if stop_after == "B":
                sp.wait_ge(s["b_x1"], done(B - 1))
                sp.dma_start(out_v, xs[:]).then_inc(d_st[0], 16)
                sp.wait_ge(d_st[0], 16)
                return
            sp.wait_ge(fill_ready, 1)
            sp.dma_start(xrows[E * CAP:E * CAP + P, :], fill[:]).then_inc(fill_done, 16)
            sp.wait_ge(tables, 1)
            for e in range(E):
                r = sp.value_load(filli[0:1, e:e + 1], min_val=e * CAP, max_val=e * CAP + TOKENS)
                sp.dma_start(xrows[bass.ds(r, P), :], fill[:]).then_inc(fill_done, 16)
            sp.wait_ge(fill_done, 16 * (E + 1))
            for q in range(2):
                sp.wait_ge(sc_done[q], 16 * 2 * TT * (B // 2))

            def load_tile(t, q):
                r = sp.value_load(itab[0:1, 1, bass.ds(t, 1)], min_val=0, max_val=E * CAP)
                sp.dma_start(xt[:, q], xrows[bass.ds(r, P), :]).then_inc(c_ld[q], 16)

            load_tile(0, 0)
            load_tile(1, 1)
            with sp.Fori(0, TILES // 2 - 1) as i:
                for q in range(2):
                    sp.wait_ge(c_ld[q], 16 * (i + 1))
                    sp.sem_inc(c_in, 1)
                    sp.wait_ge(c_tr, 2 * i + (q + 1))
                    sp.wait_ge(c_de, 2 * i + (q + 1))
                    load_tile(2 * i + (q + 2), q)
            for q in range(2):
                sp.wait_ge(c_ld[q], 16 * (TILES // 2))
                sp.sem_inc(c_in, 1)

            for q in range(4):
                sp.wait_ge(c_st[q], 16 * (TILES // 4))
            def load_d(b, q):
                sp.dma_start(yy[:, q, 0], y_v[:, 0, b]).then_inc(d_ld[q], 16)
                sp.dma_start(yy[:, q, 1], y_v[:, 1, b]).then_inc(d_ld[q], 16)

            for q in range(4):
                load_d(q, q)
            with sp.Fori(0, B // 4 - 1) as i:
                for q in range(4):
                    sp.wait_ge(d_ld[q], 32 * (i + 1))
                    sp.sem_inc(d_in, 1)
                    sp.wait_ge(d_s, 4 * i + (q + 1 + START))
                    load_d(4 * i + (q + 4), q)
            for q in range(4):
                sp.wait_ge(d_ld[q], 32 * (B // 4))
                sp.sem_inc(d_in, 1)

        @block.tensor
        def _(pe):
            mm = nc.tensor.matmul
            for n in "b_gh b_pr b_L b_tr b_z b_main b_conv b_g1 b_g2 b_tk b_gt b_lg b_pf".split():
                pe.sem_inc(s[n], START)
            for c in (a_tr, c_up, c_dn, c_ht):
                pe.sem_inc(c, START)
            pe.wait_ge(consts_ready, 1)

            with pe.Fori(0, GROUPS) as g:
                pe.wait_ge(a_stat, g + 1)
                mm(bank[0][:, 0:GB * C], cs(GRP, P), mv[:, :, 0], start=True, stop=True).then_inc(a_mean, 1)
                pe.wait_ge(a_q, g + 1)
                mm(bank[0][:, 0:GB * C], cs(GRP, P), gd[:, 2], start=True, stop=True).then_inc(a_var, 1)
                for j in range(GB):
                    pe.wait_ge(a_xnv, GB * g + (j + 1))
                    pe.wait_ge(a_xna, GB * g + (j + 1))
                    pe.wait_ge(a_xT, GB * g + (j + 1))
                    for h in range(H):
                        for c in range(C):
                            last = nc.tensor.transpose(bank[1 + j % 2][:, (h * C + c) * P:(h * C + c + 1) * P],
                                                       xn[:, j, c, h * P:(h + 1) * P], ident)
                    last.then_inc(a_tr, 1)
                pe.wait_ge(a_ca, g + START)
                for jj in range(GB // 2):
                    for c in range(C):
                        last = mm(bank[3 + jj][0:48, :], sm("uu")[:, c * 48:(c + 1) * 48], xn[:, 2 * jj:2 * jj + 2, c],
                                  start=(c == 0), stop=(c == C - 1))
                last.then_inc(a_uq, 1)
                pe.wait_ge(a_ca, g + (1 + START))
                pe.nop(nofuse=True)
                for j in range(GB):
                    last = mm(bank[5][0:T, j * T:(j + 1) * T], ca[0:T, 0, j], ca[0:T, 1, j], start=True, stop=True)
                last.then_inc(a_pr, 1)
                pe.wait_ge(a_th, g + 1)
                pe.nop(nofuse=True)
                mm(bank[5][0:T, 0:GB * T], sml[0:T, COL["vet"]:COL["vet"] + T],
                   eb[0:T, 1].rearrange("p b t -> p (b t)"), start=True, stop=True).then_inc(a_er, 1)
                pe.wait_ge(a_et, g + 1)
                pe.nop(nofuse=True)
                for j in range(GB):
                    last = mm(bank[6][0:T, j * (T + 1):(j + 1) * (T + 1)], eb[0:T, 0, j], i16w1[0:T, :],
                              start=True, stop=True)
                last.then_inc(a_ej, 1)
                pe.wait_ge(a_ec, g + 1)
                for h in range(H):
                    last = mm(bank[7][:, h * GB * (T + 1):(h + 1) * GB * (T + 1)],
                              cst[0:T, REP + h * P:REP + (h + 1) * P], ej[0:T].rearrange("p b t -> p (b t)"),
                              start=True, stop=True)
                last.then_inc(a_rep, 1)

            def mix(b, p):
                pe.wait_ge(s["b_lr"], done(b - 1))
                if not isinstance(b, int) or b >= 5:
                    pe.wait_ge(s["b_tkc"], done(b - 5))
                pe.wait_ge(s["b_gb"], done(b))
                for h in range(H):
                    last = mm(bank[0][0:48, 0:N], ghb[:, p, h], xT[:, b, h], start=(h == 0), stop=(h == H - 1))
                last.then_inc(s["b_gh"], 1)

            def product(b, p):
                pe.wait_ge(s["b_lr"], done(b))
                pe.wait_ge(s["b_exp"], done(b - 1))
                for c in range(C):
                    last = mm(bank[1][:, c * N:(c + 1) * N], lr[0:T, p, N + c * P:N + (c + 1) * P],
                              lr[0:T, p, 0:N], start=True, stop=True)
                last.then_inc(s["b_pr"], 1)

            def logits(b, p):
                pe.wait_ge(s["b_th"], done(b))
                for c in range(C):
                    for j in range(C):
                        last = mm(bank[1][:, c * N:(c + 1) * N], vs[:, j, c * P:(c + 1) * P], sg[:, p, j],
                                  start=(j == 0), stop=(j == C - 1))
                last.then_inc(s["b_L"], 1)

            def turn_softmax(b, p):
                pe.wait_ge(s["b_pn"], done(b))
                pe.wait_ge(s["b_A"], done(b - 1))
                if not isinstance(b, int) or b >= 4:
                    pe.wait_ge(s["b_sh"], done(b - 4))
                for m in range(C):
                    for n in range(C):
                        last = nc.tensor.transpose(bank[3][:, m * N + n * P:m * N + (n + 1) * P],
                                                   pn[:, n, m * P:(m + 1) * P], ident)
                last.then_inc(s["b_tr"], 1)

            def features(b, p, c):
                pe.wait_ge(s["b_xb"], done(b))
                for h in range(H):
                    pe.wait_ge(s["b_zc"], (b * 4 + (c * H + h)) + (START - 1))
                    mm(bank[4 + h][:, 0:K * P], xTb[:, p, h, c * P:(c + 1) * P],
                       thetabd[:].rearrange("p k t o -> p (k t o)"), start=True, stop=True).then_inc(s["b_z"], 1)

            def graph(b, p, h, c):
                if h == 0 and c == 0:
                    pe.wait_ge(s["b_A"], done(b))
                    pe.wait_ge(s["b_zc"], (b * 4 + 4) + START)
                    pe.wait_ge(s["b_relu"], done(b - 1))
                for k in range(K):
                    last = mm(bank[6][:, h * N:(h + 1) * N], z[:, p, c, k, h], A[:, p, c, k],
                              start=(c == 0 and k == 0), stop=(c == C - 1 and k == K - 1))
                if h == H - 1 and c == C - 1:
                    last.then_inc(s["b_main"], 1)

            def conv(b, p):
                pe.wait_ge(s["b_relu"], done(b))
                pe.wait_ge(s["b_y"], done(b - 1))
                for c in range(C):
                    o = bank[7][:, c * FT:(c + 1) * FT]
                    for h in range(H):
                        mm(o[:, h * P:(h + 1) * P], xTb[:, p, h, c * P:(c + 1) * P],
                           rwbd[:].rearrange("p t o -> p (t o)"), start=(c == 0 and h == 0), stop=False,
                           skip_group_check=True)
                    for h in range(H):
                        a = h * (FT - BAND)
                        last = mm(o[:, a:a + BAND], sgT[:, h, c * P:(c + 1) * P], convm[:, h],
                                  start=False, stop=(c == C - 1 and h == H - 1), skip_group_check=True)
                last.then_inc(s["b_conv"], 1)

            def gn_mean(b, p):
                pe.wait_ge(s["b_st"], done(b))
                pe.wait_ge(s["b_slot"], done(b - 2))
                mm(bank[2][:, 0:C], cs(GRP, P), mv2[:, :, 0], start=True, stop=True).then_inc(s["b_g1"], 1)

            def gn_var(b, p):
                pe.wait_ge(s["b_q"], done(b))
                mm(bank[2][:, 0:C], cs(GRP, P), gd2[:, 2], start=True, stop=True).then_inc(s["b_g2"], 1)

            def tokens(b, p):
                pe.wait_ge(s["b_xn"], done(b))
                pe.wait_ge(s["b_lr"], done(min(b + 4, B - 1) if isinstance(b, int) else b + 4))
                pe.wait_ge(s["b_A"], done(min(b + 3, B - 1) if isinstance(b, int) else b + 3))
                for c in range(C):
                    last = mm(bank[3][0:E, 0:FT], sm("gate")[:, c * E:(c + 1) * E], xn2[:, c], start=(c == 0),
                              stop=(c == C - 1))
                last.then_inc(s["b_gt"], 1)
                for k in range(TT):
                    for c in range(C):
                        last = nc.tensor.transpose(bank[0][:, k * N + c * P:k * N + (c + 1) * P],
                                                   xn2[:, c, k * P:(k + 1) * P], ident)
                last.then_inc(s["b_tk"], 1)

            def turn_logits(b, p):
                pe.wait_ge(s["b_gtc"], done(b))
                pe.nop(nofuse=True)
                for k in range(TT):
                    last = nc.tensor.transpose(bank[3][:, FT + k * E:FT + (k + 1) * E], lgT[0:E, k * P:(k + 1) * P],
                                               cst[0:E, ID:ID + E])
                last.then_inc(s["b_lg"], 1)

            def prefix(b, p):
                pe.wait_ge(s["b_nb"], done(min(b + 1, B - 1) if isinstance(b, int) else b + 1))
                pe.wait_ge(s["b_M"], done(b))
                mm(bank[2][:, 64:64 + E], tri[:], mb[:, 0], start=True, stop=True)
                mm(bank[2][:, 72:72 + E], tri[:], mb[:, 1], start=True, stop=False)
                mm(bank[2][:, 72:72 + E], one[:], mb[:, 0], start=False, stop=True)
                mm(bank[2][:, 80:80 + E], one[:], mb[:, 0], start=True, stop=False)
                mm(bank[2][:, 80:80 + E], one[:], mb[:, 1], start=False, stop=True).then_inc(s["b_pf"], 1)

            def turn(i, q, ahead2, ahead1, now, back1, back2, back3):
                if ahead1:
                    logits(i + 1, 1 - q)
                if now:
                    graph(i, q, 0, 0)
                    graph(i, q, 0, 1)
                if ahead2:
                    mix(i + 2, q)
                if back2:
                    gn_mean(i - 2, q)
                if ahead1:
                    turn_softmax(i + 1, 1 - q)
                if now:
                    graph(i, q, 1, 0)
                if back2:
                    gn_var(i - 2, q)
                if now:
                    graph(i, q, 1, 1)
                if ahead1:
                    features(i + 1, 1 - q, 0)
                if ahead2:
                    product(i + 2, q)
                if now:
                    conv(i, q)
                if ahead1:
                    features(i + 1, 1 - q, 1)
                if back3:
                    prefix(i - 3, 1 - q)
                if back2:
                    tokens(i - 2, q)
                if back2:
                    turn_logits(i - 2, q)

            pe.wait_ge(ld_w, 48)
            pe.wait_ge(a_gh, GROUPS)
            schedule(pe, turn)

            if stop_after == "B":
                return
            pe.wait_ge(ld_m, 32)
            pe.wait_ge(tables, 1)

            def transpose_rows(t, q):
                pe.wait_ge(c_in, t + 1)
                pe.wait_ge(c_xc, t + START - 1)
                for c in range(C):
                    last = nc.tensor.transpose(bank[q][:, c * P:(c + 1) * P], xt[:, q, c * P:(c + 1) * P], ident)
                last.then_inc(c_tr, 1)

            def up(t, q):
                e = pe.value_load(itab[0:1, 0, bass.ds(t, 1)], min_val=0, max_val=E - 1)
                pe.wait_ge(c_xc, t + (1 + START))
                pe.wait_ge(c_h, t + START - 1)
                for c in range(C):
                    last = mm(bank[2 + q][:, :], xc[:, q, c], w13[:, e, c].rearrange("p w n -> p (w n)"),
                              start=(c == 0), stop=(c == C - 1))
                last.then_inc(c_up, 1)

            def turn_hidden(t, q):
                pe.wait_ge(c_h, t + (1 + START))
                pe.wait_ge(c_hc, t + START - 1)
                for f in range(C):
                    last = nc.tensor.transpose(bank[6 + q][:, f * P:(f + 1) * P], hh[:, q, f], ident)
                last.then_inc(c_ht, 1)

            def down(t, q):
                e = pe.value_load(itab[0:1, 0, bass.ds(t, 1)], min_val=0, max_val=E - 1)
                pe.wait_ge(c_hc, t + (1 + START))
                pe.wait_ge(c_y, t + START - 1)
                for f in range(C):
                    last = mm(bank[4 + q][:, 0:N], hT[:, q, f], w2[:, e, f], start=(f == 0), stop=(f == C - 1))
                last.then_inc(c_dn, 1)

            def step_c(t, q, more=True):
                if more:
                    up(t + 1, 1 - q)
                    transpose_rows(t + 2, q)
                down(t - 1, 1 - q)
                turn_hidden(t, q)

            transpose_rows(0, 0)
            up(0, 0)
            transpose_rows(1, 1)
            up(1, 1)
            transpose_rows(2, 0)
            turn_hidden(0, 0)
            with pe.Fori(0, (TILES - 4) // 2) as i:
                step_c(2 * i + 1, 1)
                step_c(2 * i + 2, 0)
            step_c(TILES - 3, 1)
            up(TILES - 1, 1)
            step_c(TILES - 2, 0, False)
            step_c(TILES - 1, 1, False)
            down(TILES - 1, 1)

            with pe.Fori(0, B // 2) as i:
                for q in range(2):
                    b = 2 * i + q
                    pe.wait_ge(d_s, b + (1 + START))
                    pe.wait_ge(d_o, b + START - 1)
                    for c in range(C):
                        for k in range(TT):
                            last = nc.tensor.transpose(bank[6 + q][:, c * FT + k * P:c * FT + (k + 1) * P],
                                                       ys[:, q, k, c * P:(c + 1) * P], ident)
                    last.then_inc(d_tr, 1)

        @block.scalar
        def _(act):
            for n in "b_lr b_th b_exp b_relu b_sq b_xn b_ex b_zc b_xb b_tkc b_gtc".split():
                act.sem_inc(s[n], START)
            act.sem_inc(a_xT, START)
            nc.scalar.preload_act_table(ACT.Exp)

            with act.Fori(0, GROUPS) as g:
                act.wait_ge(a_nb, g + 1)
                for j in range(GB):
                    nc.scalar.activation(
                        xn[:, j, 1].rearrange("p (t f) -> p f t", f=F),
                        xs[:, GB * g + j, 1].rearrange("p (f t) -> p f t", t=T), ACT.Identity,
                        bias=gr[:, 1, j * C + 1:j * C + 2], scale=gr[:, 0, j * C + 1:j * C + 2]).then_inc(a_xna, 1)
                for j in range(GB):
                    act.wait_ge(a_tr, GB * g + (j + 1 + START))
                    nc.scalar.copy(xT[:, GB * g + j].rearrange("p h n -> p (h n)"), bank[1 + j % 2][:, :]).then_inc(a_xT, 1)
                act.wait_ge(a_pb, g + 1)
                nc.scalar.activation(eb[0:T, 1], eb[0:T, 0], ACT.Tanh, scale=0.5).then_inc(a_th, 1)
                act.wait_ge(a_es, g + 1)
                nc.scalar.activation(eb[0:T, 2], eb[0:T, 0], ACT.Exp, scale=0.5).then_inc(a_ex, 1)

            def copy_mix(b, p):
                act.wait_ge(s["b_gh"], done(b))
                act.wait_ge(s["b_pr"], done(b - 2))
                nc.scalar.copy(lr[0:T, p, 0:N], bank[0][0:T, 0:N])
                nc.scalar.copy(lr[0:T, p, N:2 * N], bank[0][32:32 + T, 0:N]).then_inc(s["b_lr"], 1)

            def fetch_xT(b, p):
                act.wait_ge(s["b_conv"], done(b - 2))
                nc.scalar.copy(xTb[:, p], xT[:, b]).then_inc(s["b_xb"], 1)

            def copy_tokens(b, p):
                act.wait_ge(s["b_gt"], done(b))
                nc.scalar.copy(lgT[0:E], bank[3][0:E, 0:FT]).then_inc(s["b_gtc"], 1)
                act.wait_ge(s["b_tk"], done(b))
                act.wait_ge(s["b_sc"], done(b - 2))
                nc.scalar.copy(xtok[:, p, :, 0:N], bank[0][:, :].rearrange("p (k n) -> p k n", k=TT)
                               ).then_inc(s["b_tkc"], 1)

            def tanh(b, p):
                act.wait_ge(s["b_bs"], done(b))
                nc.scalar.activation(sg[:, p], sg[:, p], ACT.Tanh, scale=0.5).then_inc(s["b_th"], 1)

            def exps(b, p):
                act.wait_ge(s["b_max"], done(b))
                act.wait_ge(s["b_pn"], done(b - 1))
                for c in range(C):
                    ins = nc.scalar.activation(pe_[:, c], bank[1][:, c * N:(c + 1) * N], ACT.Exp,
                                               bias=nmx[:, p, 1, c:c + 1], scale=0.5,
                                               accum_out=es2[:, p, 0, c:c + 1])
                ins.then_inc(s["b_exp"], 1)

            def copy_features(b, p, c):
                for h in range(H):
                    act.wait_ge(s["b_z"], (b * 4 + (c * H + h + 1)) + START)
                    nc.scalar.copy(z[:, p, c, :, h], bank[4 + h][:, 0:K * P].rearrange("p (k o) -> p k o", k=K)
                                   ).then_inc(s["b_zc"], 1)

            def relu(b, p):
                act.wait_ge(s["b_main"], done(b))
                act.wait_ge(s["b_conv"], done(b - 1))
                nc.scalar.activation(sgT[:], bank[6][:, :].rearrange("p (h n) -> p h n", h=H), ACT.Relu
                                     ).then_inc(s["b_relu"], 1)

            def square(b, p):
                act.wait_ge(s["b_cen"], done(b))
                act.wait_ge(s["b_var"], done(b - 1))
                nc.scalar.activation(sq[:], y[:, p], ACT.Square).then_inc(s["b_sq"], 1)

            def normalise(b, p):
                act.wait_ge(s["b_nb"], done(b))
                act.wait_ge(s["b_tk"], done(b - 1))
                for c in range(C):
                    ins = nc.scalar.activation(xn2[:, c], xs[:, b, c], ACT.Identity, bias=gr2[:, 1, c:c + 1],
                                               scale=gr2[:, 0, c:c + 1])
                ins.then_inc(s["b_xn"], 1)

            def route_exp(b, p):
                act.wait_ge(s["b_sh"], done(b))
                nc.scalar.activation(rt[:, 1], rt[:, 0], ACT.Exp).then_inc(s["b_ex"], 1)

            def turn(i, q, ahead2, ahead1, now, back1, back2, back3):
                if ahead1:
                    fetch_xT(i + 1, 1 - q)
                if back3:
                    route_exp(i - 3, 1 - q)
                if ahead1:
                    exps(i + 1, 1 - q)
                if back1:
                    square(i - 1, 1 - q)
                if ahead2:
                    copy_mix(i + 2, q)
                if now:
                    relu(i, q)
                if ahead1:
                    copy_features(i + 1, 1 - q, 0)
                if back2:
                    normalise(i - 2, q)
                if ahead2:
                    tanh(i + 2, q)
                if ahead1:
                    copy_features(i + 1, 1 - q, 1)
                if back2:
                    copy_tokens(i - 2, q)

            schedule(act, turn)

            if stop_after == "B":
                return
            act.sem_inc(c_y, START)
            act.sem_inc(c_hc, START)
            nc.scalar.preload_act_table(ACT.Gelu)

            def gelu(t, q):
                act.wait_ge(c_up, t + (1 + START))
                act.wait_ge(c_h, t + START - 1)
                nc.scalar.activation(gl[:, q].rearrange("p f k -> p (f k)"), bank[2 + q][:, 0:C * P], ACT.Gelu
                                     ).then_inc(c_gl, 1)

            def copy_y(t, q):
                act.wait_ge(c_dn, t + (1 + START))
                act.wait_ge(c_out, t + 1)
                nc.scalar.copy(yo[:, t % 4], bank[4 + q][:, 0:N]).then_inc(c_y, 1)

            def copy_hidden(t, q):
                act.wait_ge(c_ht, t + (1 + START))
                act.wait_ge(c_dn, t + START - 1)
                nc.scalar.copy(hT[:, q].rearrange("p f k -> p (f k)"), bank[6 + q][:, 0:C * P]).then_inc(c_hc, 1)

            def step_c(t, q):
                gelu(t + 1, 1 - q)
                copy_y(t - 1, 1 - q)
                copy_hidden(t, q)

            gelu(0, 0)
            gelu(1, 1)
            copy_hidden(0, 0)
            with act.Fori(0, (TILES - 2) // 2) as i:
                step_c(2 * i + 1, 1)
                step_c(2 * i + 2, 0)
            copy_y(TILES - 2, 0)
            copy_hidden(TILES - 1, 1)
            copy_y(TILES - 1, 1)

            def weigh_first(b, q):
                act.wait_ge(d_in, b + 1)
                act.wait_ge(d_s, b + (START - 1))
                for k in range(TT):
                    ins = nc.scalar.mul(ym[:, q, k], yy[:, b % 4, 0, k], wts[:, b, 0, k:k + 1])
                ins.then_inc(d_ym, 1)

            def store(b, q):
                act.wait_ge(d_o, b + (1 + START))
                act.dma_start(out_v[:, b], oo[:, q]).then_inc(d_st[q], 16)

            weigh_first(0, 0)
            with act.Fori(0, B // 2 - 1) as i:
                weigh_first(2 * i + 1, 1)
                store(2 * i, 0)
                weigh_first(2 * i + 2, 0)
                store(2 * i + 1, 1)
            weigh_first(B - 1, 1)
            store(B - 2, 0)
            store(B - 1, 1)
            for q in range(2):
                act.wait_ge(d_st[q], 16 * (B // 2))

        @block.gpsimd
        def _(pool):
            for n in "b_x1 b_sc".split():
                pool.sem_inc(s[n], START)
            pool.sem_inc(c_out, 4)
            nc.gpsimd.memset(gh[:], 0.0).then_inc(wkp, 1)
            nc.gpsimd.memset(cnt[:], 0.0).then_inc(wkp, 1)
            nc.gpsimd.memset(fill[:], 0.0).then_inc(wkp, 1)
            pool.wait_ge(ld_c, 32)
            pool.wait_ge(wkp, 3)
            nc.gpsimd.tensor_scalar(fill[:, N:N + 1], cs(PCOL, 1), float(TOKENS), None, ALU.add).then_inc(wkp, 1)
            nc.gpsimd.tensor_scalar(fill[:, N + 1:N + 2], cs(PCOL, 1), 0.0, -1.0, ALU.mult, ALU.add).then_inc(wkp, 1)
            for k in range(TT):
                ins = nc.gpsimd.tensor_scalar(tok[:, k:k + 1], cs(PCOL, 1), float(k * P), None, ALU.add)
                ins.then_inc(wkp, 1)
            pool.wait_ge(wkp, 5 + TT)
            pool.sem_inc(fill_ready, 1)
            pool.sem_inc(zeros_ready, 1)

            def ln_out(b, p):
                pool.wait_ge(s["b_dn"], done(b))
                step = Steps(pool, p_x1, b, 2 * C)
                over = lambda a: a.rearrange("p (u t) -> p u t", u=1).to_broadcast([P, 16, T])
                for c in range(C):
                    step(nc.gpsimd.tensor_tensor(yg[:, c].rearrange("p (o t) -> p o t", t=T),
                                                 y[:, p, c].rearrange("p (t o) -> p o t", o=16), over(sm("gamma")), ALU.mult))
                    step(nc.gpsimd.tensor_tensor(yg[:, c].rearrange("p (o t) -> p o t", t=T),
                                                 yg[:, c].rearrange("p (o t) -> p o t", t=T), over(sm("beta")), ALU.add))
                step.close()
                nc.gpsimd.tensor_tensor(xs[:, b], xs[:, b], yg[:], ALU.add).then_inc(s["b_x1"], 1)

            def scatter(b, q):
                pool.wait_ge(s["b_slot"], done(b))
                pool.wait_ge(s["b_tkc"], done(b))
                pool.nop(nofuse=True)
                for w in range(2):
                    for k in range(TT):
                        pool.indirect_dma_start(
                            xrows, bass.IndirectOffsetOnAxis(ap=slot[:, q, w, k:k + 1], axis=0),
                            xtok[:, q, k], None).then_inc(sc_done[q], 16)

            def landed(q, b):
                pool.wait_ge(sc_done[q], (b + (2 - q)) * (16 * TT))
                pool.sem_inc(s["b_sc"], 1)

            def turn(i, q, ahead2, ahead1, now, back1, back2, back3):
                if not isinstance(i, int) or i >= 4:
                    landed(q, i - 4)
                if back1:
                    ln_out(i - 1, 1 - q)
                if back3:
                    scatter(i - 3, 1 - q)

            pool.wait_ge(a_gh, GROUPS)
            schedule(pool, turn)
            landed((B - 1) % 2, B - 1)

            if stop_after == "B":
                return
            pool.sem_inc(c_di, 4)

            def put_rows(t, q):
                pool.wait_ge(c_de, t + 1)
                pool.nop(nofuse=True)
                nc.gpsimd.tensor_copy(dest[:, q], dn[:, 1, q]).then_inc(c_di, 1)
                pool.wait_ge(c_y, t + (1 + START))
                pool.wait_ge(c_di, t + (1 + 4))
                pool.nop(nofuse=True)
                pool.indirect_dma_start(yrows, bass.IndirectOffsetOnAxis(ap=dest[:, q], axis=0),
                                        yo[:, q], None, bounds_check=2 * TOKENS - 1, oob_is_err=False
                                        ).then_inc(c_st[q], 16)

            for q in range(3):
                put_rows(q, q)
            with pool.Fori(0, TILES // 4 - 1) as i:
                for q in range(4):
                    put_rows(4 * i + (q + 3), (q + 3) % 4)
                    pool.wait_ge(c_st[q], 16 * (i + 1))
                    pool.sem_inc(c_out, 1)
            put_rows(TILES - 1, 3)
            for q in range(4):
                pool.wait_ge(c_st[q], 16 * (TILES // 4))

        @block.vector
        def _(dve):
            V = nc.vector
            for n in "b_gb b_bs b_max b_rec b_A b_y b_cen b_var b_dn b_st b_q b_nb b_sh b_M b_slot b_pn".split():
                dve.sem_inc(s[n], START)
            dve.sem_inc(a_ca, START)
            dve.wait_ge(ld_c, 32)
            blk3 = lambda n: blk.rearrange("p (t u) -> p t u", u=1).to_broadcast([P, TH, n])
            over_t = lambda a: a.rearrange("p (u n) -> p u n", u=1).to_broadcast([P, TH, a.shape[1]])
            for k in range(K):
                V.tensor_tensor(thetabd[:, k], over_t(sm("theta")[:, k * 16:(k + 1) * 16]), blk3(16), ALU.mult)
            V.tensor_tensor(rwbd[:], over_t(sm("rw")), blk3(16), ALU.mult)
            V.tensor_copy(tri[:], cs(TRI, P))
            V.tensor_copy(one[:], cs(ONE, P))
            V.tensor_copy(mk[0:32], sml[0:32, COL["u3"]:COL["u3"] + F])
            V.tensor_copy(mk[32:48], cst[32:48, ID + 32:ID + 48])
            V.tensor_copy(i16w1[0:T, 0:T], cst[0:T, ID:ID + T])
            V.tensor_copy(i16w1[0:T, T:T + 1], sml[0:T, COL["w1"]:COL["w1"] + 1])
            step = Steps(dve, wk, 0, H * 4 + 2)
            step(V.tensor_tensor(negb[:], sm("tb"), sm("rb"), ALU.add))
            step(V.tensor_scalar(negb[:], negb[:], -1.0, None, ALU.mult))
            for h in range(H):
                def band(out_, dt):
                    q = BLK + dt + (1 - h)
                    on = cst[:, q:q + TH + 1].rearrange("p (t u) -> p t u", u=1).to_broadcast([P, TH + 1, 16])
                    w = sm("tw")[:, dt * 16:(dt + 1) * 16].rearrange("p (u n) -> p u n", u=1).to_broadcast([P, TH + 1, 16])
                    return V.tensor_tensor(out_.rearrange("p (t o) -> p t o", o=16), w, on, ALU.mult)
                band(convm[:, h], 0)
                step(band(convt[:, 0], 1))
                step(V.tensor_tensor(convm[:, h], convm[:, h], convt[:, 0], ALU.add))
                step(band(convt[:, 1], 2))
                step(V.tensor_tensor(convm[:, h], convm[:, h], convt[:, 1], ALU.add))
            step.close()
            dve.sem_inc(consts_ready, 1)
            dve.wait_ge(zeros_ready, 1)

            def reciprocal_root(step, v, out_):
                bits, guess = v[:, 1].bitcast(I32), out_
                yield from step.then(V.tensor_scalar(bits, v[:, 0].bitcast(I32), 1, None, ALU.arith_shift_right))
                yield from step.then(V.tensor_scalar(guess.bitcast(I32), bits, -1.0, MAGIC, ALU.mult, ALU.add))
                for last in (False, False, True):
                    yield from step.then(V.tensor_tensor(v[:, 2], v[:, 0], guess, ALU.mult))
                    yield from step.then(V.scalar_tensor_tensor(out=v[:, 3], in0=v[:, 2], scalar=-0.5, in1=guess, op0=ALU.mult,
                                                op1=ALU.mult))
                    if last:
                        yield from step.then(V.scalar_tensor_tensor(out=v[:, 3], in0=v[:, 3], scalar=0.5, in1=guess, op0=ALU.add,
                                                    op1=ALU.mult))
                        yield from step.then(V.tensor_tensor(guess, guess, v[:, 3], ALU.add))
                    else:
                        yield from step.then(V.scalar_tensor_tensor(out=guess, in0=v[:, 3], scalar=1.5, in1=guess, op0=ALU.add,
                                                    op1=ALU.mult))

            def run(chain):
                for _ in chain:
                    pass

            GC = GB * C
            mask = mk[0:48].rearrange("p (u f) -> p u f", u=1).to_broadcast([48, 2 * T, F])
            wide = lambda a: a.rearrange("p (b u) -> p b u", u=1).to_broadcast([T, GB, T])

            def stats(g, js):
                for j in js:
                    ins = V.bn_stats(st6[:, j], xs[:, GB * g + j // C, j % C])
                return ins

            def close_stats(g, ins):
                step = Steps(dve, a_w, g, 1)
                step(ins)
                step.close()
                dve.nop(nofuse=True)
                for j in range(GC):
                    ins = V.bn_aggr(mv[:, j], st6[:, j])
                ins.then_inc(a_stat, 1)

            def group(g, more):
                step = Steps(dve, a_v, g, 24)
                dve.wait_ge(a_mean, g + 1)
                step(V.tensor_tensor(gd[:, 0], mv[:, :, 0], bank[0][:, 0:GC], ALU.subtract))
                V.tensor_copy(gd[:, 1], bank[0][:, 0:GC])
                step(V.tensor_tensor(gd[:, 0], gd[:, 0], gd[:, 0], ALU.mult))
                V.tensor_tensor(gd[:, 2], gd[:, 0], mv[:, :, 1], ALU.add).then_inc(a_q, 1)
                dve.wait_ge(a_var, g + 1)
                step(V.tensor_scalar(vq[:, 0, 0:GC], bank[0][:, 0:GC], EPS, None, ALU.add))
                run(reciprocal_root(step, vq[:, :, 0:GC], gr[:, 0]))
                step(V.scalar_tensor_tensor(out=gr[:, 1], in0=gd[:, 1], scalar=-1.0, in1=gr[:, 0], op0=ALU.mult,
                                            op1=ALU.mult))
                dve.sem_inc(a_nb, 1)
                for j in range(GB):
                    V.tensor_scalar(xn[:, j, 0].rearrange("p (t f) -> p f t", f=F),
                                    xs[:, GB * g + j, 0].rearrange("p (f t) -> p f t", t=T),
                                    gr[:, 0, j * C:j * C + 1], gr[:, 1, j * C:j * C + 1], ALU.mult, ALU.add
                                    ).then_inc(a_xnv, 1)
                if more:
                    dve.wait_ge(x_in, g + 2)
                    stats(g + 1, range(0, 4))
                dve.wait_ge(a_uq, g + 1)
                for jj in range(GB // 2):
                    ins = V.tensor_tensor(uq[0:48, jj * 2 * T:(jj + 1) * 2 * T],
                                          bank[3 + jj][0:48, :].rearrange("p (j f) -> p j f", f=F), mask, ALU.mult)
                step(ins)
                flat = lambda a: a.rearrange("p b t -> p (b t)")
                V.tensor_reduce(flat(ca[0:T, 0]), uq[0:T], AX, ALU.add)
                V.tensor_reduce(flat(ca[0:T, 1]), uq[32:32 + T], AX, ALU.add).then_inc(a_ca, 1)
                if more:
                    last = stats(g + 1, range(4, 5))
                dve.wait_ge(a_pr, g + 1)
                bet = sml[0:T, COL["bet"]:COL["bet"] + T].rearrange("p (u t) -> p u t", u=1).to_broadcast([T, GB, T])
                e5 = bank[5][0:T, 0:GB * T].rearrange("p (b t) -> p b t", b=GB)
                V.tensor_tensor(eb[0:T, 0], e5, bet, ALU.add).then_inc(a_pb, 1)
                if more:
                    last = stats(g + 1, range(5, 7))
                dve.wait_ge(a_er, g + 1)
                step(V.tensor_reduce(es[0:T, 0], e5, AX, ALU.max))
                V.tensor_tensor(eb[0:T, 0], e5, wide(es[0:T, 0]), ALU.subtract).then_inc(a_es, 1)
                if more:
                    last = stats(g + 1, range(7, 8))
                    close_stats(g + 1, last)
                dve.wait_ge(a_ex, g + 1)
                step(V.tensor_reduce(es[0:T, 1], eb[0:T, 2], AX, ALU.add))
                step(V.reciprocal(es[0:T, 2], es[0:T, 1]))
                V.tensor_tensor(eb[0:T, 0], eb[0:T, 2], wide(es[0:T, 2]), ALU.mult).then_inc(a_et, 1)
                dve.wait_ge(a_ej, g + 1)
                V.tensor_copy(ej[0:T].rearrange("p b t -> p (b t)"), bank[6][0:T, 0:GB * (T + 1)]).then_inc(a_ec, 1)
                dve.wait_ge(a_rep, g + 1)
                for h in range(H):
                    r7 = bank[7][:, h * GB * (T + 1):(h + 1) * GB * (T + 1)].rearrange("p (b t) -> p b t", b=GB)
                    gg = gh[:, bass.ds(GB * g, GB), h]
                    step(V.tensor_copy(es[:, 3], r7[:, :, T]))
                    V.tensor_tensor(gg[:, :, 0:T], sm("w2").rearrange("p (u t) -> p u t", u=1).to_broadcast([P, GB, T]),
                                    es[:, 3].rearrange("p (b u) -> p b u", u=1).to_broadcast([P, GB, T]), ALU.mult)
                    step(V.tensor_scalar(gg[:, :, 32:32 + T], r7[:, :, 0:T], sm("w3"), None, ALU.mult))
                step.close()
                dve.sem_inc(a_gh, 1)

            dve.wait_ge(x_in, 1)
            close_stats(0, stats(0, range(GC)))
            with dve.Fori(0, GROUPS - 1) as g:
                group(g, True)
            group(GROUPS - 1, False)

            def fetch_mix(b, p):
                dve.wait_ge(s["b_gh"], done(b - 2))
                V.tensor_copy(ghb[:, p], gh[:, b]).then_inc(s["b_gb"], 1)

            def add_bs(b, p):
                dve.wait_ge(s["b_pr"], done(b))
                dve.wait_ge(s["b_L"], done(b - 2))
                V.tensor_tensor(sg[:, p].rearrange("p c n -> p (c n)"), bank[1][:, :],
                                bs[:].rearrange("p c n -> p (c n)"), ALU.add).then_inc(s["b_bs"], 1)
                yield

            def row_max(b, p):
                dve.wait_ge(s["b_L"], done(b))
                step = Steps(dve, v_mx, b, 1)
                yield from step.then(V.tensor_reduce(nmx[:, p, 0], bank[1][:, :].rearrange("p (c n) -> p c n", c=C),
                                                     AX, ALU.max))
                step.close()
                V.tensor_scalar(nmx[:, p, 1], nmx[:, p, 0], -0.5, None, ALU.mult).then_inc(s["b_max"], 1)
                yield

            def recip(b, p):
                dve.wait_ge(s["b_exp"], done(b))
                step = Steps(dve, v_sc, b, 1)
                yield from step.then(V.reciprocal(es2[:, p, 1], es2[:, p, 0]))
                step.close()
                dve.wait_ge(s["b_tr"], done(b - 1))
                V.tensor_scalar(pn[:, 0], pe_[:, 0], es2[:, p, 1, 0:1], None, ALU.mult)
                yield
                V.tensor_scalar(pn[:, 1], pe_[:, 1], es2[:, p, 1, 1:2], None, ALU.mult).then_inc(s["b_pn"], 1)
                yield

            def weigh(b, p):
                dve.wait_ge(s["b_tr"], done(b))
                dve.wait_ge(s["b_main"], done(b - 2))
                for c in range(C):
                    p3 = bank[3][:, c * N:(c + 1) * N].rearrange("p (u n) -> p u n", u=1).to_broadcast([P, K, N])
                    ins = V.tensor_tensor(A[:, p, c], p3, chebs[:, c], ALU.mult)
                    if c == C - 1:
                        ins.then_inc(s["b_A"], 1)
                    yield

            yvs = [[y[:, p, c].rearrange("p (t o) -> p o t", o=16) for c in range(C)] for p in range(2)]
            th = lambda a, c: a[:, c].rearrange("p (o u) -> p o u", u=1).to_broadcast([P, 16, T])

            def ln_a(b, p):
                dve.wait_ge(s["b_conv"], done(b))
                dve.wait_ge(s["b_x1"], done(b - 2))
                yv = yvs[p]
                step = Steps(dve, v_ln, b, 2)
                nb = negb[:].rearrange("p (u o) -> p u o", u=1).to_broadcast([P, C * T, 16])
                V.tensor_tensor(y[:, p].rearrange("p c (t o) -> p (c t) o", o=16),
                                bank[7][:, :].rearrange("p (k o) -> p k o", o=16), nb, ALU.max).then_inc(s["b_y"], 1)
                yield
                dve.wait_ge(s["b_y"], done(b))
                V.tensor_reduce(s1[:, 0], yv[0], AX, ALU.add)
                yield
                yield from step.then(V.tensor_reduce(s1[:, 1], yv[1], AX, ALU.add))
                V.scalar_tensor_tensor(out=yv[0], in0=th(s1, 0), scalar=-1.0 / T, in1=yv[0], op0=ALU.mult, op1=ALU.add)
                yield
                yield from step.then(V.scalar_tensor_tensor(out=yv[1], in0=th(s1, 1), scalar=-1.0 / T, in1=yv[1],
                                                            op0=ALU.mult, op1=ALU.add))
                step.close()
                dve.sem_inc(s["b_cen"], 1)

            def ln_b(b, p):
                dve.wait_ge(s["b_sq"], done(b))
                for c in range(C):
                    ins = V.tensor_reduce(vq[:, 4, c * 16:(c + 1) * 16], sq[:, c].rearrange("p (t o) -> p o t", o=16),
                                          AX, ALU.add)
                    if c == C - 1:
                        ins.then_inc(s["b_var"], 1)
                    yield

            LN, GN = slice(0, C * 16), slice(C * 16, NV)

            def ln_roots(b, p):
                dve.wait_ge(s["b_var"], done(b))
                step = Steps(dve, v_lq, b, 13)
                yield from step.then(V.tensor_scalar(vq[:, 0, LN], vq[:, 4, LN], 1.0 / T, EPS, ALU.mult, ALU.add))
                yield from reciprocal_root(step, vq[:, :, LN], vr[:, LN])
                step.close()

            def gn_roots(b, p):
                dve.wait_ge(s["b_g2"], done(b))
                step = Steps(dve, v_gq, b, 13)
                yield from step.then(V.tensor_scalar(vq[:, 0, GN], bank[2][:, 0:C], EPS, None, ALU.add))
                yield from reciprocal_root(step, vq[:, :, GN], vr[:, GN])
                step.close()

            def ln_c(b, p):
                yv = yvs[p]
                for c in range(C):
                    ins = V.tensor_tensor(yv[c], yv[c], vr[:, c * 16:(c + 1) * 16].rearrange("p (o u) -> p o u", u=1)
                                          .to_broadcast([P, 16, T]), ALU.mult)
                    if c == C - 1:
                        ins.then_inc(s["b_dn"], 1)
                    yield

            def gn_stats(b, p, step):
                dve.wait_ge(s["b_x1"], done(b))
                V.bn_stats(st62[:, 0], xs[:, b, 0])
                yield
                yield from step.then(V.bn_stats(st62[:, 1], xs[:, b, 1]))
                dve.nop(nofuse=True)
                for c in range(C):
                    ins = V.bn_aggr(mv2[:, c], st62[:, c])
                ins.then_inc(s["b_st"], 1)
                yield

            def gn_moments(b, p, step):
                dve.wait_ge(s["b_g1"], done(b))
                dve.wait_ge(s["b_st"], done(b))
                V.tensor_copy(gd2[:, 1], bank[2][:, 0:C])
                yield from step.then(V.tensor_tensor(gd2[:, 0], mv2[:, :, 0], bank[2][:, 0:C], ALU.subtract))
                yield from step.then(V.tensor_tensor(gd2[:, 0], gd2[:, 0], gd2[:, 0], ALU.mult))
                V.tensor_tensor(gd2[:, 2], gd2[:, 0], mv2[:, :, 1], ALU.add).then_inc(s["b_q"], 1)
                step.close()
                yield

            def gn_scale(b, p):
                dve.wait_ge(s["b_xn"], done(b - 1))
                V.tensor_copy(gr2[:, 0], vr[:, C * 16:NV])
                V.scalar_tensor_tensor(out=gr2[:, 1], in0=gd2[:, 1], scalar=-1.0, in1=vr[:, C * 16:NV], op0=ALU.mult,
                                       op1=ALU.mult).then_inc(s["b_nb"], 1)
                yield

            wide8 = lambda a: a.rearrange("p (k u) -> p k u", u=1).to_broadcast([P, TT, E])
            row8 = lambda a: a.rearrange("p (u e) -> p u e", u=1).to_broadcast([P, TT, E])

            def route_a(b, p):
                dve.wait_ge(s["b_lg"], done(b))
                dve.wait_ge(s["b_sc"], done(b - 2))
                V.tensor_copy(xtok[:, p, :, N], tok[:])
                step = Steps(dve, v_rt, b, 3)
                lg = bank[3][:, FT:FT + TT * E].rearrange("p (k e) -> p k e", k=TT)
                yield from step.then(V.tensor_reduce(r2[:, 0], lg, AX, ALU.max))
                yield from step.then(V.tensor_scalar(tok[:], tok[:], float(FT), None, ALU.add))
                yield from step.then(V.tensor_tensor(rt[:, 0], lg, wide8(r2[:, 0]), ALU.subtract))
                step.close()
                dve.sem_inc(s["b_sh"], 1)

            def route_b(b, p):
                dve.wait_ge(s["b_ex"], done(b))
                step = Steps(dve, v_rt2, b, 18)
                yield from step.then(V.tensor_reduce(r2[:, 1], rt[:, 1], AX, ALU.add))
                yield from step.then(V.reciprocal(r2[:, 2], r2[:, 1]))
                yield from step.then(V.tensor_tensor(rt[:, 2], rt[:, 1], wide8(r2[:, 2]), ALU.mult))
                src = rt[:, 2]
                for w in range(2):
                    yield from step.then(V.tensor_reduce(r2[:, 3 + w], src, AX, ALU.max))
                    yield from step.then(V.tensor_tensor(rt[:, 3], src, wide8(r2[:, 3 + w]), ALU.is_equal))
                    yield from step.then(V.tensor_tensor(rt[:, 4], rt[:, 3], row8(cs(DSC, E)), ALU.mult))
                    yield from step.then(V.tensor_reduce(r2[:, 5 + w], rt[:, 4], AX, ALU.max))
                    yield from step.then(V.tensor_tensor(rt[:, 7 + w], rt[:, 4], wide8(r2[:, 5 + w]), ALU.is_equal))
                    if w == 0:
                        yield from step.then(V.scalar_tensor_tensor(out=rt[:, 5], in0=rt[:, 7], scalar=-2.0, in1=rt[:, 2],
                                                                    op0=ALU.mult, op1=ALU.add))
                        src = rt[:, 5]
                yield from step.then(V.tensor_tensor(mb[:], rt[:, 7], rt[:, 8], ALU.add))
                dve.sem_inc(s["b_M"], 1)
                V.tensor_scalar(xtok[:, p, :, N + 1], r2[:, 5], -1.0, float(E), ALU.mult, ALU.add)
                yield from step.then(V.tensor_tensor(r2[:, 7], r2[:, 3], r2[:, 4], ALU.add))
                yield from step.then(V.reciprocal(r2[:, 8], r2[:, 7]))
                wb = wts[:, b]
                V.tensor_tensor(wb[:, 0], r2[:, 3], r2[:, 8], ALU.mult)
                yield from step.then(V.tensor_tensor(wb[:, 1], r2[:, 4], r2[:, 8], ALU.mult))
                step.close()

            def route_c(b, p):
                dve.wait_ge(s["b_pf"], done(b))
                step = Steps(dve, v_rt3, b, 5)
                pf = bank[2][:, 64:64 + TT * E].rearrange("p (k e) -> p k e", k=TT)
                yield from step.then(V.tensor_tensor(rt[:, 10], pf, row8(cnt[:]), ALU.add))
                V.tensor_tensor(cnt[:], cnt[:], bank[2][:, 80:80 + E], ALU.add)
                yield from step.then(V.tensor_tensor(rt[:, 10], rt[:, 10], row8(cs(EBASE, E)), ALU.add))
                V.tensor_tensor(rt[:, 3], rt[:, 10], rt[:, 7], ALU.mult)
                yield from step.then(V.tensor_tensor(rt[:, 4], rt[:, 10], rt[:, 8], ALU.mult))
                V.tensor_reduce(slotf[:, 0], rt[:, 3], AX, ALU.add)
                yield from step.then(V.tensor_reduce(slotf[:, 1], rt[:, 4], AX, ALU.add))
                yield from step.then(V.tensor_copy(slot[:, p].rearrange("p w k -> p (w k)"),
                                                   slotf[:].rearrange("p w k -> p (w k)")))
                step.close()
                dve.sem_inc(s["b_slot"], 1)

            def turn(i, q, ahead2, ahead1, now, back1, back2, back3):
                step = Steps(dve, v_gn, i - 2, 3)

                def pause(n):
                    for _ in range(n):
                        yield

                def statistics():
                    if back2:
                        yield from gn_stats(i - 2, q, step)

                def attention():
                    if ahead1:
                        yield from row_max(i + 1, 1 - q)
                        yield from pause(6)
                        yield from recip(i + 1, 1 - q)

                def centre():
                    if back1:
                        yield from ln_a(i - 1, 1 - q)

                def layer_norm():
                    if back1:
                        yield from ln_b(i - 1, 1 - q)
                        yield from ln_roots(i - 1, 1 - q)
                        yield from ln_c(i - 1, 1 - q)

                def group_norm():
                    if back2:
                        yield from gn_moments(i - 2, q, step)
                        yield from pause(2)
                        yield from gn_roots(i - 2, q)
                        yield from gn_scale(i - 2, q)

                def matrices():
                    if ahead1:
                        yield from pause(8)
                        yield from weigh(i + 1, 1 - q)
                    if ahead2:
                        yield from add_bs(i + 2, q)

                def router(part):
                    if back3:
                        yield from part(i - 3, 1 - q)

                choice = router(route_b)
                if ahead2:
                    fetch_mix(i + 2, q)
                weave(centre())
                weave(router(route_a), statistics())
                weave(attention(), along=(choice,))
                weave(layer_norm(), group_norm(), matrices(), choice)
                weave(router(route_c))

            dve.wait_ge(ld_w, 48)
            schedule(dve, turn)

            if stop_after == "B":
                return
            step = Steps(dve, v_tb, 0, 16)
            step(V.tensor_scalar(nt[:, 0], cnt[:], float(P - 1), None, ALU.add))
            step(V.tensor_copy(ci[:, 0], nt[:, 0]))
            step(V.tensor_scalar(ci[:, 1], ci[:, 0], 7, None, ALU.arith_shift_right))
            step(V.tensor_copy(nt[:, 1], ci[:, 1]))
            step(V.tensor_tensor_scan(nt[:, 2], cst[:, ONE:ONE + E], nt[:, 1], 0.0, ALU.mult, ALU.add))
            tl = lambda a: a.rearrange("p (u e) -> p u e", u=1).to_broadcast([P, TILES, E])
            ti = cs(TIDX, TILES)
            step(V.tensor_tensor(ge[:, 0], tl(nt[:, 2]), ti.rearrange("p (t u) -> p t u", u=1).to_broadcast([P, TILES, E]),
                                 ALU.is_le))
            step(V.tensor_reduce(tb3[:, 0], ge[:, 0], AX, ALU.add))
            step(V.tensor_tensor(ge[:, 1], ge[:, 0], tl(nt[:, 1]), ALU.mult))
            step(V.tensor_reduce(tb3[:, 1], ge[:, 1], AX, ALU.add))
            step(V.tensor_tensor(tb3[:, 2], ti, tb3[:, 1], ALU.subtract))
            step(V.tensor_scalar(tb3[:, 3], tb3[:, 0], float(CAP), None, ALU.mult))
            step(V.scalar_tensor_tensor(out=tb3[:, 4], in0=tb3[:, 2], scalar=float(P), in1=tb3[:, 3], op0=ALU.mult,
                                        op1=ALU.add))
            step(V.tensor_scalar(itab[:, 1], tb3[:, 4], float(E * CAP), None, ALU.min))
            step(V.tensor_scalar(itab[:, 0], tb3[:, 0], float(E - 1), None, ALU.min))
            step(V.tensor_tensor(fillf[:], cnt[:], cs(EBASE, E), ALU.add))
            step(V.tensor_copy(filli[:], fillf[:]))
            step.close()
            dve.sem_inc(tables, 1)

            dve.sem_inc(c_xc, START)
            dve.sem_inc(c_h, START)

            def copy_x(t, q):
                dve.wait_ge(c_tr, t + 1)
                dve.wait_ge(c_up, t + START - 1)
                V.tensor_copy(xc[:, q].rearrange("p c k -> p (c k)"), bank[q][:, 0:C * P]).then_inc(c_xc, 1)
                dve.wait_ge(c_di, t + 1)
                V.tensor_scalar(dn[:, 0, t % 4], xt[:, q, N + 1:N + 2], tb3[:, 0, bass.ds(t, 1)], float(TOKENS),
                                ALU.not_equal, ALU.mult).then_inc(c_dd, 1)
                dve.wait_ge(c_dd, t + 1)
                V.tensor_tensor(dn[:, 1, t % 4], dn[:, 0, t % 4], xt[:, q, N:N + 1], ALU.add).then_inc(c_de, 1)

            def gate(t, q):
                dve.wait_ge(c_gl, t + 1)
                dve.wait_ge(c_ht, t + START - 1)
                V.tensor_tensor(hh[:, q].rearrange("p f k -> p (f k)"), bank[2 + q][:, C * P:2 * C * P],
                                gl[:, q].rearrange("p f k -> p (f k)"), ALU.mult).then_inc(c_h, 1)

            copy_x(0, 0)
            copy_x(1, 1)
            gate(0, 0)
            with dve.Fori(0, TILES // 2 - 1) as i:
                for q in range(2):
                    t = 2 * i + q
                    copy_x(t + 2, q)
                    gate(t + 1, 1 - q)
            gate(TILES - 1, 1)

            dve.sem_inc(d_o, START)
            dve.sem_inc(d_s, START)
            def combine(b, q, stored):
                dve.wait_ge(d_in, b + 1)
                dve.wait_ge(d_ym, b + 1)
                for k in range(TT):
                    ins = V.scalar_tensor_tensor(out=ys[:, q, k], in0=yy[:, b % 4, 1, k], scalar=wts[:, b, 1, k:k + 1],
                                                 in1=ym[:, q, k], op0=ALU.mult, op1=ALU.add)
                ins.then_inc(d_s, 1)
                dve.wait_ge(d_tr, b + 1)
                if stored is not None:
                    dve.wait_ge(d_st[q], stored)
                V.tensor_tensor(oo[:, q].rearrange("p c n -> p (c n)"), bank[6 + q][:, :],
                                xs[:, b].rearrange("p c n -> p (c n)"), ALU.add).then_inc(d_o, 1)

            for q in range(2):
                combine(q, q, None)
            with dve.Fori(1, B // 2) as i:
                for q in range(2):
                    combine(2 * i + q, q, 16 * i)


def constants():
    import numpy as np

    a = np.zeros((P, NCONST), np.float32)
    p = np.arange(P)
    a[:, ID:ID + P] = np.eye(P)
    a[:, TRI:TRI + P] = p[:, None] < p[None, :]
    a[:, ONE:ONE + P] = 1.0
    a[:, GRP:GRP + P] = (p[:, None] // 8 == p[None, :] // 8) / 8.0
    a[:, BLK:BLK + TH + 4] = np.arange(TH + 4)[None, :] == p[:, None] // F + 2
    a[:, DSC:DSC + E] = E - np.arange(E)
    a[:, EBASE:EBASE + E] = np.arange(E) * CAP
    a[:, TIDX:TIDX + TILES] = np.arange(TILES)
    a[:, PCOL] = p
    a[0:T, REP:REP + FT] = np.arange(FT)[None, :] // F == np.arange(T)[:, None]
    return a


def kernel(**inputs):
    import numpy as np
    import concourse.bacc as bacc
    from concourse.bass_utils import run_bass_kernel_spmd as run

    g = {k: np.asarray(v) for k, v in inputs.items()}
    c = {k[8:]: v for k, v in g.items() if k.startswith("L0_conv_")}
    m = {k[8:]: v for k, v in g.items() if k.startswith("L1_conv_")}
    small = np.zeros((P, NSMALL), np.float32)

    def put(name, a):
        small[:a.shape[0], COL[name]:COL[name] + SIZES[name]] = a

    down = lambda a: np.tile(a, (TH, 1))
    every = lambda a: np.tile(a.reshape(1, -1), (P, 1))
    rows = lambda a: np.moveaxis(a.reshape(a.shape[:-2] + (C, P, a.shape[-1])), -2, 0)
    put("theta", down(c["Theta"].transpose(1, 0, 2).reshape(F, K * 16)))
    put("rw", down(c["rw"].T))
    put("tw", down(c["tw"][:, :, 0, :].transpose(1, 2, 0).reshape(16, 48)))
    put("w2", down(c["W2"]))
    put("w3", down(c["W3"].reshape(F, 1)))
    put("tb", every(c["tb"]))
    put("rb", every(c["rb"]))
    put("gamma", every(c["gamma"]))
    put("beta", every(c["beta"]))
    put("u3", every(c["U3"]))
    uu = np.zeros((C, P, 48), np.float32)
    uu[:, :, 0:F] = c["U2"].reshape(F, C, P).transpose(1, 2, 0)
    uu[:, :, 32:48] = c["U1"].reshape(C, P, 1)
    put("uu", uu.transpose(1, 0, 2).reshape(P, C * 48))
    put("gate", m["gate_w"].reshape(E, C, P).transpose(2, 1, 0).reshape(P, C * E))
    put("vet", c["V_e"].T)
    put("bet", c["b_e"][0].T)
    put("w1", c["W1"].reshape(T, 1))
    arrays = dict(x=g["x"], consts=constants(), small=small, cheb=c["cheb"].reshape(K, C, P, N).transpose(2, 1, 0, 3),
                  vst=rows(c["V_s"].T), bst=rows(c["b_s"][0].T), 
                  w13t=rows(np.concatenate([m["w1"].transpose(0, 2, 1), m["w3"].transpose(0, 2, 1)], -1)
                            ).reshape(P, E, C, 2, N), w2t=rows(m["w2"].transpose(0, 2, 1)))
    arrays = {k: np.ascontiguousarray(v) for k, v in arrays.items()}

    nc = bacc.Bacc("TRN2", target_bir_lowering=False, num_devices=1)
    args = {k: nc.dram_tensor(f"{k}_in", v.shape, F32, kind="ExternalInput").ap() for k, v in arrays.items()}
    xrows = nc.dram_tensor("xrows", (E * CAP + P, ROW), F32, kind="Internal").ap()
    yrows = nc.dram_tensor("yrows", (2 * TOKENS + P, N), F32, kind="Internal").ap()
    out = nc.dram_tensor("out", (B, N, F, T), F32, kind="ExternalOutput").ap()
    build(nc, xrows=xrows, yrows=yrows, out=out, **args)
    r = run(nc, [{f"{k}_in": v for k, v in arrays.items()}], core_ids=[0])
    return r.results[0]["out"]
```

```python
from contextlib import ExitStack

import concourse.bass as bass
from concourse import mybir

F32 = mybir.dt.float32
I32 = mybir.dt.int32
BF16 = mybir.dt.bfloat16
ALU = mybir.AluOpType
ACT = mybir.ActivationFunctionType
AX = mybir.AxisListType.X

P = 128
B, N, F, T = 16, 256, 16, 16
C = N // P
FT = F * T
TH = P // F
H = FT // P
K = 3
BAND = (TH + 1) * F
GB = 4
GROUPS = B // GB
E = 8
TT = FT // P
TOKENS = B * FT
CAP = TOKENS + P
ROW = N + 2
TILES = 2 * TOKENS // P + E
EPS = 1e-5
BITS = E.bit_length() - 1
AHEAD = 6
START = 2

ID, TRI, ONE, GRP = 0, P, 2 * P, 3 * P
BLK = 4 * P
DSC = BLK + TH + 4
EBASE = DSC + E
TIDX = EBASE + E
PCOL = TIDX + TILES
REP = PCOL + 1
NCONST = REP + FT

SIZES = dict(theta=K * 16, rw=16, tw=3 * 16, w2=T, w3=1, tb=16, rb=16, gamma=T, beta=T,
             u3=F, uu=C * 48, gate=C * E, vet=T, bet=T, w1=1)
COL, NSMALL = {}, 0
for _name, _size in SIZES.items():
    COL[_name] = NSMALL
    NSMALL += _size


NV = C * 16 + C
MAGIC = 1597463007.0


def done(b):
    return b + (1 + START)


class Steps:

    def __init__(self, eng, sem, turn, per_turn):
        self.eng, self.sem, self.base, self.per, self.n = eng, sem, turn * per_turn, per_turn, 0

    def __call__(self, ins):
        ins.then_inc(self.sem, 1)
        self.n += 1
        self.eng.wait_ge(self.sem, self.base + self.n)

    def then(self, ins):
        ins.then_inc(self.sem, 1)
        self.n += 1
        yield
        self.eng.wait_ge(self.sem, self.base + self.n)

    def close(self):
        assert self.n == self.per, (self.n, self.per)


def weave(*chains, along=()):
    chains = list(chains)
    while chains:
        for chain in tuple(chains):
            if next(chain, chains) is chains:
                chains.remove(chain)
        for chain in along:
            next(chain, None)


def schedule(eng, turn):
    for i in range(-2, 4):
        turn(i, i % 2, True, i + 1 >= 0, i >= 0, i >= 1, i >= 2, i >= 3)
    with eng.Fori(0, (B - 6) // 2) as j:
        for q in range(2):
            turn(2 * j + (4 + q), q, *(True,) * 6)
    for i in range(B - 2, B + 3):
        turn(i, i % 2, False, i + 1 < B, i < B, i - 1 < B, i - 2 < B, True)


def build(nc, x, consts, small, cheb, vst, bst, w13t, w2t, xrows, yrows, out):
    with ExitStack() as ctx:
        def sb(name, shape, dt=F32):
            return ctx.enter_context(nc.sbuf_tensor(name, [P] + shape, dt))

        def sem(name):
            return ctx.enter_context(nc.semaphore(name))

        bank = [ctx.enter_context(nc.psum_tensor(f"bank{i}", [P, 512], F32)) for i in range(8)]

        cst = sb("cst", [NCONST])
        sml = sb("sml", [NSMALL])
        xs = sb("xs", [B, C, FT])
        xT = sb("xT", [B, H, N])
        xTb = sb("xTb", [2, H, N])
        ghb = sb("ghb", [2, H, 48])
        chebs = sb("chebs", [C, K, N])
        vs = sb("vs", [C, N])
        bs = sb("bs", [C, N])
        w13 = sb("w13", [E, C, 2, N])
        w2 = sb("w2", [E, C, N])
        thetabd = sb("thetabd", [K, TH, 16])
        rwbd = sb("rwbd", [TH, 16])
        convm = sb("convm", [H, BAND])
        convt = sb("convt", [2, BAND])
        negb = sb("negb", [16])
        tri = sb("tri", [P], BF16)
        one = sb("one", [P], BF16)
        vq = sb("vq", [5, NV])
        vr = sb("vr", [NV])
        i16w1 = sb("i16w1", [T + 1])
        zs, As, xs1 = 2 * C * K * H * P, 2 * C * K * N, GB * C * FT
        work = sb("work", [zs + As + 2 * C * FT])
        z = work[:, 0:zs].rearrange("p (b c k h n) -> p b c k h n", b=2, c=C, k=K, h=H)
        A = work[:, zs:zs + As].rearrange("p (b c k n) -> p b c k n", b=2, c=C, k=K)
        y = work[:, zs + As:].rearrange("p (b c n) -> p b c n", b=2, c=C)
        xn = work[:, 0:xs1].rearrange("p (b c n) -> p b c n", b=GB, c=C)
        uq = work[:, xs1:xs1 + GB * FT].rearrange("p (j f) -> p j f", f=F)
        st6 = sb("st6", [GB * C, 6])
        mv = sb("mv", [GB * C, 2])
        gd = sb("gd", [4, GB * C])
        gr = sb("gr", [2, GB * C])
        ca = sb("ca", [2, GB, T])
        ej = sb("ej", [GB, T + 1])
        eb = sb("eb", [3, GB, T])
        es = sb("es", [4, GB])
        mk = sb("mk", [F])
        gh = sb("gh", [B, H, 48])
        lr = sb("lr", [2, 2 * N])
        sg = sb("sg", [2, C, N])
        nmx = sb("nmx", [2, 2, C])
        es2 = sb("es2", [2, 2, C])
        pe_ = sb("pe_", [C, N])
        pn = sb("pn", [C, N])
        sgT = sb("sgT", [H, N])
        sq = sb("sq", [C, FT])
        s1 = sb("s1", [C, 16])
        yg = sb("yg", [C, FT])
        st62 = sb("st62", [C, 6])
        mv2 = sb("mv2", [C, 2])
        gd2 = sb("gd2", [4, C])
        gr2 = sb("gr2", [2, C])
        xn2 = sb("xn2", [C, FT])
        xtok = sb("xtok", [2, TT, ROW])
        tok = sb("tok", [TT])
        lgT = sb("lgT", [FT])
        mb = sb("mb", [TT, E], BF16)
        rt = sb("rt", [12, TT, E])
        r2 = sb("r2", [10, TT])
        wts = sb("wts", [B, 2, TT])
        cnt = sb("cnt", [E])
        slotf = sb("slotf", [2, TT])
        slot = sb("slot", [2, 2, TT], I32)
        ci = sb("ci", [2, E], I32)
        nt = sb("nt", [3, E])
        ge = work[:, 0:2 * TILES * E].rearrange("p (a t e) -> p a t e", a=2, t=TILES)
        pk = work[:, 2 * TILES * E:2 * TILES * E + 3 * TILES].rearrange("p (a t) -> p a t", a=3)
        tb3 = sb("tb3", [5, TILES])
        itab = sb("itab", [2, TILES], I32)
        filli = sb("filli", [E], I32)
        fillf = sb("fillf", [E])
        fill = sb("fill", [ROW])
        dest = sb("dest", [4, 1], I32)
        room = xT[:].rearrange("p b h n -> p (b h n)")
        used = [0]

        def over_xT(*shape):
            size = 1
            for d in shape:
                size *= d
            a = room[:, used[0]:used[0] + size]
            used[0] += size
            names = " ".join("abcd"[:len(shape)])
            return a.rearrange(f"p ({names}) -> p {names}", **dict(zip(names.split(), shape)))

        xt = over_xT(2, ROW)
        xc = over_xT(2, C, P)
        gl = over_xT(2, C, P)
        hh = over_xT(2, C, P)
        hT = over_xT(2, C, P)
        yo = over_xT(4, N)
        dn = over_xT(2, 4, 1)
        used[0] = 0
        yy = over_xT(4, 2, TT, N)
        ym = over_xT(4, TT, N)
        ys = over_xT(2, TT, N)
        oo = over_xT(2, C, FT)

        ld_c = sem("ld_c"); ld_w = sem("ld_w"); ld_m = sem("ld_m")
        ld_x = [sem(f"ld_x{i}") for i in range(2)]
        x_in = sem("x_in")
        wk = sem("wk"); wkp = sem("wkp"); consts_ready = sem("consts_ready"); zeros_ready = sem("zeros_ready")
        a_v = sem("a_v"); a_hv = sem("a_hv"); a_w = sem("a_w")
        a_stat = sem("a_stat"); a_mean = sem("a_mean"); a_q = sem("a_q"); a_var = sem("a_var"); a_nb = sem("a_nb")
        a_xnv = sem("a_xnv"); a_xna = sem("a_xna"); a_tr = sem("a_tr"); a_xT = sem("a_xT"); a_uq = sem("a_uq")
        a_ca = sem("a_ca"); a_pr = sem("a_pr"); a_pb = sem("a_pb"); a_th = sem("a_th")
        a_er = sem("a_er"); a_es = sem("a_es"); a_ex = sem("a_ex"); a_et = sem("a_et"); a_ej = sem("a_ej")
        a_ec = sem("a_ec"); a_rep = sem("a_rep"); a_gh = sem("a_gh")
        names = ("b_gh b_lr b_pr b_bs b_th b_L b_max b_exp b_rec b_pn b_tr b_A b_z b_zc b_main b_relu b_conv "
                 "b_y b_cen b_sq b_var b_dn b_x1 b_st b_g1 b_q b_g2 b_nb b_xn b_tk b_tkc b_gt b_gtc b_lg "
                 "b_sh b_ex b_M b_pf b_slot b_sc b_gb b_xb").split()
        s = {n: sem(n) for n in names}
        v_ln = sem("v_ln"); v_gn = sem("v_gn"); v_rt = sem("v_rt"); v_rt2 = sem("v_rt2"); v_rt3 = sem("v_rt3"); v_lq = sem("v_lq"); v_gq = sem("v_gq")
        p_x1 = sem("p_x1"); v_mx = sem("v_mx")
        sc_done = [sem("sc_done0"), sem("sc_done1")]
        v_tb = sem("v_tb"); tables = sem("tables"); fill_rows = sem("fill_rows"); fill_ready = sem("fill_ready"); fill_done = sem("fill_done")
        
        d_ym = sem("d_ym"); c_ld = [sem("c_ld0"), sem("c_ld1")]; c_in = sem("c_in"); c_tr = sem("c_tr"); c_xc = sem("c_xc"); c_up = sem("c_up")
        c_gl = sem("c_gl"); c_h = sem("c_h"); c_ht = sem("c_ht"); c_hc = sem("c_hc"); c_dn = sem("c_dn"); c_y = sem("c_y"); c_dd = sem("c_dd")
        c_de = sem("c_de"); c_di = sem("c_di")
        c_st = [sem(f"c_st{i}") for i in range(4)]; c_out = sem("c_out")
        d_ld = [sem(f"d_ld{i}") for i in range(4)]; d_in = sem("d_in"); d_s = sem("d_s"); d_tr = sem("d_tr")
        d_o = sem("d_o"); d_st = [sem("d_st0"), sem("d_st1")]

        cs = lambda a, n: cst[:, a:a + n]
        sm = lambda name: sml[:, COL[name]:COL[name] + SIZES[name]]
        ident = cs(ID, P)
        blk = cs(BLK + 2, TH)

        x_v = x.rearrange("b (c p) f t -> p b c (f t)", p=P)
        out_v = out.rearrange("b (c p) f t -> p b c (f t)", p=P)
        y_v = yrows[0:2 * TOKENS, :].rearrange("(w b k p) n -> p w b k n", w=2, b=B, k=TT)

        def fill_behind(eng, experts):
            for e in experts:
                r = eng.value_load(filli[0:1, e:e + 1], min_val=e * CAP, max_val=e * CAP + TOKENS)
                eng.dma_start(xrows[bass.ds(r, P), :], fill[:]).then_inc(fill_done, 16)

        block = ctx.enter_context(nc.Block())

        @block.sync
        def _(sp):
            sp.dma_start(cst[:], consts).then_inc(ld_c, 16)
            sp.dma_start(sml[:], small).then_inc(ld_c, 16)
            for g in range(GROUPS):
                if g >= 2:
                    sp.wait_ge(ld_x[g % 2], 16 * (g // 2))
                    sp.sem_inc(x_in, 1)
                sp.dma_start(xs[:, g * GB:(g + 1) * GB], x_v[:, g * GB:(g + 1) * GB]).then_inc(ld_x[g % 2], 16)
            for g in range(GROUPS - 2, GROUPS):
                sp.wait_ge(ld_x[g % 2], 16 * (g // 2 + 1))
                sp.sem_inc(x_in, 1)
            sp.dma_start(chebs[:], cheb).then_inc(ld_w, 16)
            sp.dma_start(vs[:], vst).then_inc(ld_w, 16)
            sp.dma_start(bs[:], bst).then_inc(ld_w, 16)
            for dst, src in ((w13, w13t), (w2, w2t)):
                sp.dma_start(dst[:], src).then_inc(ld_m, 16)
            sp.wait_ge(fill_ready, 1)
            sp.dma_start(xrows[E * CAP:E * CAP + P, :], fill[:]).then_inc(fill_done, 16)
            sp.wait_ge(fill_rows, 1)
            fill_behind(sp, range(E // 2))
            sp.wait_ge(tables, 1)
            sp.wait_ge(fill_done, 16 * (E + 1))
            for q in range(2):
                sp.wait_ge(sc_done[q], 16 * 2 * TT * (B // 2))

            def load_tile(t, q):
                r = sp.value_load(itab[0:1, 1, bass.ds(t, 1)], min_val=0, max_val=E * CAP)
                sp.dma_start(xt[:, q], xrows[bass.ds(r, P), :]).then_inc(c_ld[q], 16)

            load_tile(0, 0)
            load_tile(1, 1)
            with sp.Fori(0, TILES // 2 - 1) as i:
                for q in range(2):
                    sp.wait_ge(c_ld[q], 16 * (i + 1))
                    sp.sem_inc(c_in, 1)
                    sp.wait_ge(c_tr, 2 * i + (q + 1))
                    sp.wait_ge(c_de, 2 * i + (q + 1))
                    load_tile(2 * i + (q + 2), q)
            for q in range(2):
                sp.wait_ge(c_ld[q], 16 * (TILES // 2))
                sp.sem_inc(c_in, 1)

            for q in range(4):
                sp.wait_ge(c_st[q], 16 * (TILES // 4))
            def load_d(b, q):
                sp.dma_start(yy[:, q, 0], y_v[:, 0, b]).then_inc(d_ld[q], 16)
                sp.dma_start(yy[:, q, 1], y_v[:, 1, b]).then_inc(d_ld[q], 16)

            def landed(q, pairs):
                sp.wait_ge(d_ld[q], 32 * pairs)
                sp.sem_inc(d_in, 1)

            for q in range(4):
                load_d(q, q)
            landed(0, 1)
            landed(1, 1)
            with sp.Fori(0, B // 4 - 1) as i:
                for q in range(4):
                    landed((q + 2) % 4, i + (1 if q < 2 else 2))
                    sp.wait_ge(d_s, 4 * i + (q + 1 + START))
                    load_d(4 * i + (q + 4), q)
            landed(2, B // 4)
            landed(3, B // 4)

        @block.tensor
        def _(pe):
            mm = nc.tensor.matmul
            for n in "b_gh b_pr b_L b_tr b_z b_main b_conv b_g1 b_g2 b_tk b_gt b_lg b_pf".split():
                pe.sem_inc(s[n], START)
            for c in (a_tr, c_up, c_dn, c_ht):
                pe.sem_inc(c, START)
            pe.wait_ge(consts_ready, 1)

            def norm_mean(g):
                pe.wait_ge(a_stat, g + 1)
                mm(bank[0][:, 0:GB * C], cs(GRP, P), mv[:, :, 0], start=True, stop=True).then_inc(a_mean, 1)

            def norm_var(g):
                pe.wait_ge(a_q, g + 1)
                mm(bank[0][:, 0:GB * C], cs(GRP, P), gd[:, 2], start=True, stop=True).then_inc(a_var, 1)

            def turn_x(g, j):
                pe.wait_ge(a_xnv, GB * g + (j + 1))
                pe.wait_ge(a_xna, GB * g + (j + 1))
                pe.wait_ge(a_xT, GB * g + (j + 1))
                for h in range(H):
                    for c in range(C):
                        last = nc.tensor.transpose(bank[1 + j % 2][:, (h * C + c) * P:(h * C + c + 1) * P],
                                                   xn[:, j, c, h * P:(h + 1) * P], ident)
                last.then_inc(a_tr, 1)

            def through_u(g, jj):
                pe.wait_ge(a_ca, g + START)
                for c in range(C):
                    last = mm(bank[3 + jj][0:48, :], sm("uu")[:, c * 48:(c + 1) * 48], xn[:, 2 * jj:2 * jj + 2, c],
                              start=(c == 0), stop=(c == C - 1))
                last.then_inc(a_uq, 1)

            def temporal_product(g):
                pe.wait_ge(a_ca, g + (1 + START))
                pe.nop(nofuse=True)
                for j in range(GB):
                    last = mm(bank[5][0:T, j * T:(j + 1) * T], ca[0:T, 0, j], ca[0:T, 1, j], start=True, stop=True)
                last.then_inc(a_pr, 1)

            def temporal_logits(g):
                pe.wait_ge(a_th, g + 1)
                pe.nop(nofuse=True)
                mm(bank[5][0:T, 0:GB * T], sml[0:T, COL["vet"]:COL["vet"] + T],
                   eb[0:T, 1].rearrange("p b t -> p (b t)"), start=True, stop=True).then_inc(a_er, 1)

            def turn_attention(g):
                pe.wait_ge(a_et, g + 1)
                pe.nop(nofuse=True)
                for j in range(GB):
                    last = mm(bank[6][0:T, j * (T + 1):(j + 1) * (T + 1)], eb[0:T, 0, j], i16w1[0:T, :],
                              start=True, stop=True)
                last.then_inc(a_ej, 1)

            def spread(g):
                pe.wait_ge(a_ec, g + 1)
                for h in range(H):
                    last = mm(bank[7][:, h * GB * (T + 1):(h + 1) * GB * (T + 1)],
                              cst[0:T, REP + h * P:REP + (h + 1) * P], ej[0:T].rearrange("p b t -> p (b t)"),
                              start=True, stop=True)
                last.then_inc(a_rep, 1)

            norm_mean(0)
            norm_var(0)
            for j in range(GB):
                turn_x(0, j)
            with pe.Fori(0, GROUPS - 1) as g:
                through_u(g, 0)
                norm_mean(g + 1)
                through_u(g, 1)
                norm_var(g + 1)
                temporal_product(g)
                turn_x(g + 1, 0)
                temporal_logits(g)
                turn_x(g + 1, 1)
                turn_x(g + 1, 2)
                turn_attention(g)
                turn_x(g + 1, 3)
                spread(g)
            g = GROUPS - 1
            through_u(g, 0)
            through_u(g, 1)
            temporal_product(g)
            temporal_logits(g)
            turn_attention(g)
            spread(g)

            def mix(b, p):
                pe.wait_ge(s["b_lr"], done(b - 1))
                if not isinstance(b, int) or b >= 5:
                    pe.wait_ge(s["b_tkc"], done(b - 5))
                pe.wait_ge(s["b_gb"], done(b))
                for h in range(H):
                    last = mm(bank[0][0:48, 0:N], ghb[:, p, h], xT[:, b, h], start=(h == 0), stop=(h == H - 1))
                last.then_inc(s["b_gh"], 1)

            def product(b, p):
                pe.wait_ge(s["b_lr"], done(b))
                pe.wait_ge(s["b_exp"], done(b - 1))
                for c in range(C):
                    last = mm(bank[1][:, c * N:(c + 1) * N], lr[0:T, p, N + c * P:N + (c + 1) * P],
                              lr[0:T, p, 0:N], start=True, stop=True)
                last.then_inc(s["b_pr"], 1)

            def logits(b, p):
                pe.wait_ge(s["b_th"], done(b))
                for c in range(C):
                    for j in range(C):
                        last = mm(bank[1][:, c * N:(c + 1) * N], vs[:, j, c * P:(c + 1) * P], sg[:, p, j],
                                  start=(j == 0), stop=(j == C - 1))
                last.then_inc(s["b_L"], 1)

            def turn_softmax(b, p):
                pe.wait_ge(s["b_pn"], done(b))
                pe.wait_ge(s["b_A"], done(b - 1))
                if not isinstance(b, int) or b >= 4:
                    pe.wait_ge(s["b_sh"], done(b - 4))
                for m in range(C):
                    for n in range(C):
                        last = nc.tensor.transpose(bank[3][:, m * N + n * P:m * N + (n + 1) * P],
                                                   pn[:, n, m * P:(m + 1) * P], ident)
                last.then_inc(s["b_tr"], 1)

            def features(b, p, c):
                pe.wait_ge(s["b_xb"], done(b))
                for h in range(H):
                    pe.wait_ge(s["b_zc"], (b * 4 + (c * H + h)) + (START - 1))
                    mm(bank[4 + h][:, 0:K * P], xTb[:, p, h, c * P:(c + 1) * P],
                       thetabd[:].rearrange("p k t o -> p (k t o)"), start=True, stop=True).then_inc(s["b_z"], 1)

            def graph(b, p, h, c):
                if h == 0 and c == 0:
                    pe.wait_ge(s["b_A"], done(b))
                    pe.wait_ge(s["b_zc"], (b * 4 + 4) + START)
                    pe.wait_ge(s["b_relu"], done(b - 1))
                for k in range(K):
                    last = mm(bank[6][:, h * N:(h + 1) * N], z[:, p, c, k, h], A[:, p, c, k],
                              start=(c == 0 and k == 0), stop=(c == C - 1 and k == K - 1))
                if h == H - 1 and c == C - 1:
                    last.then_inc(s["b_main"], 1)

            def conv(b, p):
                pe.wait_ge(s["b_relu"], done(b))
                pe.wait_ge(s["b_y"], done(b - 1))
                for c in range(C):
                    o = bank[7][:, c * FT:(c + 1) * FT]
                    for h in range(H):
                        mm(o[:, h * P:(h + 1) * P], xTb[:, p, h, c * P:(c + 1) * P],
                           rwbd[:].rearrange("p t o -> p (t o)"), start=(c == 0 and h == 0), stop=False,
                           skip_group_check=True)
                    for h in range(H):
                        a = h * (FT - BAND)
                        last = mm(o[:, a:a + BAND], sgT[:, h, c * P:(c + 1) * P], convm[:, h],
                                  start=False, stop=(c == C - 1 and h == H - 1), skip_group_check=True)
                last.then_inc(s["b_conv"], 1)

            def gn_mean(b, p):
                pe.wait_ge(s["b_st"], done(b))
                pe.wait_ge(s["b_slot"], done(b - 2))
                mm(bank[2][:, 0:C], cs(GRP, P), mv2[:, :, 0], start=True, stop=True).then_inc(s["b_g1"], 1)

            def gn_var(b, p):
                pe.wait_ge(s["b_q"], done(b))
                mm(bank[2][:, 0:C], cs(GRP, P), gd2[:, 2], start=True, stop=True).then_inc(s["b_g2"], 1)

            def tokens(b, p):
                pe.wait_ge(s["b_xn"], done(b))
                pe.wait_ge(s["b_lr"], done(min(b + 4, B - 1) if isinstance(b, int) else b + 4))
                pe.wait_ge(s["b_A"], done(min(b + 3, B - 1) if isinstance(b, int) else b + 3))
                for c in range(C):
                    last = mm(bank[3][0:E, 0:FT], sm("gate")[:, c * E:(c + 1) * E], xn2[:, c], start=(c == 0),
                              stop=(c == C - 1))
                last.then_inc(s["b_gt"], 1)
                for k in range(TT):
                    for c in range(C):
                        last = nc.tensor.transpose(bank[0][:, k * N + c * P:k * N + (c + 1) * P],
                                                   xn2[:, c, k * P:(k + 1) * P], ident)
                last.then_inc(s["b_tk"], 1)

            def turn_logits(b, p):
                pe.wait_ge(s["b_gtc"], done(b))
                pe.nop(nofuse=True)
                for k in range(TT):
                    last = nc.tensor.transpose(bank[3][:, FT + k * E:FT + (k + 1) * E], lgT[0:E, k * P:(k + 1) * P],
                                               cst[0:E, ID:ID + E])
                last.then_inc(s["b_lg"], 1)

            def prefix(b, p):
                pe.wait_ge(s["b_nb"], done(min(b + 1, B - 1) if isinstance(b, int) else b + 1))
                pe.wait_ge(s["b_M"], done(b))
                mm(bank[2][:, 64:64 + E], tri[:], mb[:, 0], start=True, stop=True)
                mm(bank[2][:, 72:72 + E], tri[:], mb[:, 1], start=True, stop=False)
                mm(bank[2][:, 72:72 + E], one[:], mb[:, 0], start=False, stop=True)
                mm(bank[2][:, 80:80 + E], one[:], mb[:, 0], start=True, stop=False)
                mm(bank[2][:, 80:80 + E], one[:], mb[:, 1], start=False, stop=True).then_inc(s["b_pf"], 1)

            def turn(i, q, ahead2, ahead1, now, back1, back2, back3):
                if ahead1:
                    logits(i + 1, 1 - q)
                if now:
                    graph(i, q, 0, 0)
                    graph(i, q, 0, 1)
                if ahead2:
                    mix(i + 2, q)
                if back2:
                    gn_mean(i - 2, q)
                if now:
                    graph(i, q, 1, 0)
                if ahead1:
                    turn_softmax(i + 1, 1 - q)
                if back2:
                    gn_var(i - 2, q)
                if now:
                    graph(i, q, 1, 1)
                if ahead1:
                    features(i + 1, 1 - q, 0)
                if ahead2:
                    product(i + 2, q)
                if now:
                    conv(i, q)
                if ahead1:
                    features(i + 1, 1 - q, 1)
                if back3:
                    prefix(i - 3, 1 - q)
                if back2:
                    tokens(i - 2, q)
                if back2:
                    turn_logits(i - 2, q)

            pe.wait_ge(ld_w, 48)
            pe.wait_ge(a_gh, GROUPS)
            schedule(pe, turn)

            pe.wait_ge(ld_m, 32)
            pe.wait_ge(tables, 1)

            def transpose_rows(t, q):
                pe.wait_ge(c_in, t + 1)
                pe.wait_ge(c_xc, t + START - 1)
                for c in range(C):
                    last = nc.tensor.transpose(bank[q][:, c * P:(c + 1) * P], xt[:, q, c * P:(c + 1) * P], ident)
                last.then_inc(c_tr, 1)

            def experts(t, n):
                v = pe.value_load(itab[0:1, 0, bass.ds(t, 1)], min_val=0, max_val=E ** AHEAD - 1)
                return [(v >> (BITS * k)) & (E - 1) for k in range(n)]

            def up(t, q, e):
                pe.wait_ge(c_xc, t + (1 + START))
                pe.wait_ge(c_h, t + START - 1)
                for c in range(C):
                    last = mm(bank[2 + q][:, :], xc[:, q, c], w13[:, e, c].rearrange("p w n -> p (w n)"),
                              start=(c == 0), stop=(c == C - 1))
                last.then_inc(c_up, 1)

            def turn_hidden(t, q):
                pe.wait_ge(c_h, t + (1 + START))
                pe.wait_ge(c_hc, t + START - 1)
                for f in range(C):
                    last = nc.tensor.transpose(bank[6 + q][:, f * P:(f + 1) * P], hh[:, q, f], ident)
                last.then_inc(c_ht, 1)

            def down(t, q, e):
                pe.wait_ge(c_hc, t + (1 + START))
                pe.wait_ge(c_y, t + START - 1)
                for f in range(C):
                    last = mm(bank[4 + q][:, 0:N], hT[:, q, f], w2[:, e, f], start=(f == 0), stop=(f == C - 1))
                last.then_inc(c_dn, 1)

            def step_c(t, q, e_up, e_down):
                if e_up is not None:
                    up(t + 1, 1 - q, e_up)
                    transpose_rows(t + 2, q)
                down(t - 1, 1 - q, e_down)
                turn_hidden(t, q)

            transpose_rows(0, 0)
            e = experts(0, 2)
            up(0, 0, e[0])
            transpose_rows(1, 1)
            up(1, 1, e[1])
            transpose_rows(2, 0)
            turn_hidden(0, 0)
            with pe.Fori(0, TILES // 4 - 1) as i:
                e = experts(4 * i, AHEAD)
                for k in range(4):
                    step_c(4 * i + (k + 1), (k + 1) % 2, e[k + 2], e[k])
            e = experts(TILES - 4, 4)
            step_c(TILES - 3, 1, e[2], e[0])
            up(TILES - 1, 1, e[3])
            step_c(TILES - 2, 0, None, e[1])
            step_c(TILES - 1, 1, None, e[2])
            down(TILES - 1, 1, e[3])

            with pe.Fori(0, B // 2) as i:
                for q in range(2):
                    b = 2 * i + q
                    pe.wait_ge(d_s, b + (1 + START))
                    pe.wait_ge(d_o, b + START - 1)
                    for c in range(C):
                        for k in range(TT):
                            last = nc.tensor.transpose(bank[6 + q][:, c * FT + k * P:c * FT + (k + 1) * P],
                                                       ys[:, q, k, c * P:(c + 1) * P], ident)
                    last.then_inc(d_tr, 1)

        @block.scalar
        def _(act):
            for n in "b_lr b_th b_exp b_relu b_sq b_xn b_ex b_zc b_xb b_tkc b_gtc b_pn".split():
                act.sem_inc(s[n], START)
            act.sem_inc(a_xT, START)
            nc.scalar.preload_act_table(ACT.Exp)

            def normalise_x(g):
                act.wait_ge(a_nb, g + 1)
                if not isinstance(g, int):
                    act.wait_ge(a_uq, 2 * g)
                for j in range(GB):
                    nc.scalar.activation(
                        xn[:, j, 1].rearrange("p (t f) -> p f t", f=F),
                        xs[:, GB * g + j, 1].rearrange("p (f t) -> p f t", t=T), ACT.Identity,
                        bias=gr[:, 1, j * C + 1:j * C + 2], scale=gr[:, 0, j * C + 1:j * C + 2]).then_inc(a_xna, 1)

            def copy_x(g, j):
                act.wait_ge(a_tr, GB * g + (j + 1 + START))
                nc.scalar.copy(xT[:, GB * g + j].rearrange("p h n -> p (h n)"), bank[1 + j % 2][:, :]).then_inc(a_xT, 1)

            def temporal_tanh(g):
                act.wait_ge(a_pb, g + 1)
                nc.scalar.activation(eb[0:T, 1], eb[0:T, 0], ACT.Tanh, scale=0.5).then_inc(a_th, 1)

            def temporal_exp(g):
                act.wait_ge(a_es, g + 1)
                nc.scalar.activation(eb[0:T, 2], eb[0:T, 0], ACT.Exp, scale=0.5).then_inc(a_ex, 1)

            normalise_x(0)
            for j in range(GB):
                copy_x(0, j)
            with act.Fori(0, GROUPS - 1) as g:
                normalise_x(g + 1)
                temporal_tanh(g)
                copy_x(g + 1, 0)
                copy_x(g + 1, 1)
                temporal_exp(g)
                copy_x(g + 1, 2)
                copy_x(g + 1, 3)
            temporal_tanh(GROUPS - 1)
            temporal_exp(GROUPS - 1)

            def copy_mix(b, p):
                act.wait_ge(s["b_gh"], done(b))
                act.wait_ge(s["b_pr"], done(b - 2))
                nc.scalar.copy(lr[0:T, p, 0:N], bank[0][0:T, 0:N])
                nc.scalar.copy(lr[0:T, p, N:2 * N], bank[0][32:32 + T, 0:N]).then_inc(s["b_lr"], 1)

            def fetch_xT(b, p):
                act.wait_ge(s["b_conv"], done(b - 2))
                nc.scalar.copy(xTb[:, p], xT[:, b]).then_inc(s["b_xb"], 1)

            def copy_tokens(b, p):
                act.wait_ge(s["b_gt"], done(b))
                nc.scalar.copy(lgT[0:E], bank[3][0:E, 0:FT]).then_inc(s["b_gtc"], 1)
                act.wait_ge(s["b_tk"], done(b))
                act.wait_ge(s["b_sc"], done(b - 2))
                nc.scalar.copy(xtok[:, p, :, 0:N], bank[0][:, :].rearrange("p (k n) -> p k n", k=TT)
                               ).then_inc(s["b_tkc"], 1)

            def tanh(b, p):
                act.wait_ge(s["b_bs"], done(b))
                nc.scalar.activation(sg[:, p], sg[:, p], ACT.Tanh, scale=0.5).then_inc(s["b_th"], 1)

            def exps(b, p):
                act.wait_ge(s["b_max"], done(b))
                for c in range(C):
                    ins = nc.scalar.activation(pe_[:, c], bank[1][:, c * N:(c + 1) * N], ACT.Exp,
                                               bias=nmx[:, p, 1, c:c + 1], scale=0.5,
                                               accum_out=es2[:, p, 0, c:c + 1])
                ins.then_inc(s["b_exp"], 1)

            def scale(b, p):
                act.wait_ge(s["b_rec"], done(b))
                act.wait_ge(s["b_tr"], done(b - 1))
                for c in range(C):
                    ins = nc.scalar.mul(pn[:, c], pe_[:, c], es2[:, p, 1, c:c + 1])
                ins.then_inc(s["b_pn"], 1)

            def copy_features(b, p, c):
                for h in range(H):
                    act.wait_ge(s["b_z"], (b * 4 + (c * H + h + 1)) + START)
                    nc.scalar.copy(z[:, p, c, :, h], bank[4 + h][:, 0:K * P].rearrange("p (k o) -> p k o", k=K)
                                   ).then_inc(s["b_zc"], 1)

            def relu(b, p):
                act.wait_ge(s["b_main"], done(b))
                act.wait_ge(s["b_conv"], done(b - 1))
                nc.scalar.activation(sgT[:], bank[6][:, :].rearrange("p (h n) -> p h n", h=H), ACT.Relu
                                     ).then_inc(s["b_relu"], 1)

            def square(b, p):
                act.wait_ge(s["b_cen"], done(b))
                act.wait_ge(s["b_var"], done(b - 1))
                nc.scalar.activation(sq[:], y[:, p], ACT.Square).then_inc(s["b_sq"], 1)

            def normalise(b, p):
                act.wait_ge(s["b_nb"], done(b))
                act.wait_ge(s["b_tk"], done(b - 1))
                for c in range(C):
                    ins = nc.scalar.activation(xn2[:, c], xs[:, b, c], ACT.Identity, bias=gr2[:, 1, c:c + 1],
                                               scale=gr2[:, 0, c:c + 1])
                ins.then_inc(s["b_xn"], 1)

            def route_exp(b, p):
                act.wait_ge(s["b_sh"], done(b))
                nc.scalar.activation(rt[:, 1], rt[:, 0], ACT.Exp).then_inc(s["b_ex"], 1)

            def turn(i, q, ahead2, ahead1, now, back1, back2, back3):
                if ahead1:
                    fetch_xT(i + 1, 1 - q)
                if back1:
                    square(i - 1, 1 - q)
                if back3:
                    route_exp(i - 3, 1 - q)
                if ahead1:
                    exps(i + 1, 1 - q)
                if ahead1:
                    scale(i + 1, 1 - q)
                if ahead2:
                    copy_mix(i + 2, q)
                if now:
                    relu(i, q)
                if ahead1:
                    copy_features(i + 1, 1 - q, 0)
                if back2:
                    normalise(i - 2, q)
                if ahead2:
                    tanh(i + 2, q)
                if ahead1:
                    copy_features(i + 1, 1 - q, 1)
                if back2:
                    copy_tokens(i - 2, q)

            schedule(act, turn)

            act.wait_ge(fill_ready, 1)
            act.wait_ge(fill_rows, 1)
            fill_behind(act, range(E // 2, E))
            act.sem_inc(c_y, START)
            act.sem_inc(c_hc, START)
            nc.scalar.preload_act_table(ACT.Gelu)

            def gelu(t, q):
                act.wait_ge(c_up, t + (1 + START))
                act.wait_ge(c_h, t + START - 1)
                nc.scalar.activation(gl[:, q].rearrange("p f k -> p (f k)"), bank[2 + q][:, 0:C * P], ACT.Gelu
                                     ).then_inc(c_gl, 1)

            def copy_y(t, q):
                act.wait_ge(c_dn, t + (1 + START))
                act.wait_ge(c_out, t + 1)
                nc.scalar.copy(yo[:, t % 4], bank[4 + q][:, 0:N]).then_inc(c_y, 1)

            def copy_hidden(t, q):
                act.wait_ge(c_ht, t + (1 + START))
                act.wait_ge(c_dn, t + START - 1)
                nc.scalar.copy(hT[:, q].rearrange("p f k -> p (f k)"), bank[6 + q][:, 0:C * P]).then_inc(c_hc, 1)

            def step_c(t, q):
                gelu(t + 1, 1 - q)
                copy_y(t - 1, 1 - q)
                copy_hidden(t, q)

            gelu(0, 0)
            gelu(1, 1)
            copy_hidden(0, 0)
            with act.Fori(0, (TILES - 2) // 2) as i:
                step_c(2 * i + 1, 1)
                step_c(2 * i + 2, 0)
            copy_y(TILES - 2, 0)
            copy_hidden(TILES - 1, 1)
            copy_y(TILES - 1, 1)

            def weigh_first(b):
                act.wait_ge(d_in, b + 1)
                if not isinstance(b, int):
                    act.wait_ge(d_s, b + (START - 3))
                for k in range(TT):
                    ins = nc.scalar.mul(ym[:, b % 4, k], yy[:, b % 4, 0, k], wts[:, b, 0, k:k + 1])
                ins.then_inc(d_ym, 1)

            def store(b, q):
                act.wait_ge(d_o, b + (1 + START))
                act.dma_start(out_v[:, b], oo[:, q]).then_inc(d_st[q], 16)

            weigh_first(0)
            weigh_first(1)
            with act.Fori(0, B // 2 - 1) as i:
                for q in range(2):
                    weigh_first(2 * i + (q + 2))
                    store(2 * i + q, q)
            store(B - 2, 0)
            store(B - 1, 1)
            for q in range(2):
                act.wait_ge(d_st[q], 16 * (B // 2))

        @block.gpsimd
        def _(pool):
            for n in "b_x1 b_sc".split():
                pool.sem_inc(s[n], START)
            pool.sem_inc(c_out, 4)
            nc.gpsimd.memset(gh[:], 0.0).then_inc(wkp, 1)
            nc.gpsimd.memset(cnt[:], 0.0).then_inc(wkp, 1)
            nc.gpsimd.memset(fill[:], 0.0).then_inc(wkp, 1)
            pool.wait_ge(ld_c, 32)
            pool.wait_ge(wkp, 3)
            nc.gpsimd.tensor_scalar(fill[:, N:N + 1], cs(PCOL, 1), float(TOKENS), None, ALU.add).then_inc(wkp, 1)
            nc.gpsimd.tensor_scalar(fill[:, N + 1:N + 2], cs(PCOL, 1), 0.0, -1.0, ALU.mult, ALU.add).then_inc(wkp, 1)
            for k in range(TT):
                ins = nc.gpsimd.tensor_scalar(tok[:, k:k + 1], cs(PCOL, 1), float(k * P), None, ALU.add)
                ins.then_inc(wkp, 1)
            pool.wait_ge(wkp, 5 + TT)
            pool.sem_inc(fill_ready, 1)
            pool.sem_inc(zeros_ready, 1)

            def ln_out(b, p):
                pool.wait_ge(s["b_dn"], done(b))
                step = Steps(pool, p_x1, b, 2)
                over = lambda a: a.rearrange("p (u t) -> p u t", u=1).to_broadcast([P, C * 16, T])
                flat = lambda a: a.rearrange("p c (o t) -> p (c o) t", t=T)
                step(nc.gpsimd.tensor_tensor(flat(yg[:]), flat(y[:, p]), over(sm("gamma")), ALU.mult))
                step(nc.gpsimd.tensor_tensor(flat(yg[:]), flat(yg[:]), over(sm("beta")), ALU.add))
                step.close()
                nc.gpsimd.tensor_tensor(xs[:, b], xs[:, b], yg[:], ALU.add).then_inc(s["b_x1"], 1)

            def scatter(b, q):
                pool.wait_ge(s["b_slot"], done(b))
                pool.wait_ge(s["b_tkc"], done(b))
                pool.nop(nofuse=True)
                for w in range(2):
                    for k in range(TT):
                        pool.indirect_dma_start(
                            xrows, bass.IndirectOffsetOnAxis(ap=slot[:, q, w, k:k + 1], axis=0),
                            xtok[:, q, k], None).then_inc(sc_done[q], 16)

            def landed(q, b):
                pool.wait_ge(sc_done[q], (b + (2 - q)) * (16 * TT))
                pool.sem_inc(s["b_sc"], 1)

            def turn(i, q, ahead2, ahead1, now, back1, back2, back3):
                if not isinstance(i, int) or i >= 4:
                    landed(q, i - 4)
                if back1:
                    ln_out(i - 1, 1 - q)
                if back3:
                    scatter(i - 3, 1 - q)

            pool.wait_ge(a_gh, GROUPS)
            schedule(pool, turn)
            landed((B - 1) % 2, B - 1)

            pool.sem_inc(c_di, 4)

            def put_rows(t, q):
                pool.wait_ge(c_de, t + 1)
                pool.nop(nofuse=True)
                nc.gpsimd.tensor_copy(dest[:, q], dn[:, 1, q]).then_inc(c_di, 1)
                pool.wait_ge(c_y, t + (1 + START))
                pool.wait_ge(c_di, t + (1 + 4))
                pool.nop(nofuse=True)
                pool.indirect_dma_start(yrows, bass.IndirectOffsetOnAxis(ap=dest[:, q], axis=0),
                                        yo[:, q], None, bounds_check=2 * TOKENS - 1, oob_is_err=False
                                        ).then_inc(c_st[q], 16)

            for q in range(3):
                put_rows(q, q)
            with pool.Fori(0, TILES // 4 - 1) as i:
                for q in range(4):
                    put_rows(4 * i + (q + 3), (q + 3) % 4)
                    pool.wait_ge(c_st[q], 16 * (i + 1))
                    pool.sem_inc(c_out, 1)
            put_rows(TILES - 1, 3)
            for q in range(4):
                pool.wait_ge(c_st[q], 16 * (TILES // 4))

        @block.vector
        def _(dve):
            V = nc.vector
            for n in "b_gb b_bs b_max b_rec b_A b_y b_cen b_var b_dn b_st b_q b_nb b_sh b_M b_slot".split():
                dve.sem_inc(s[n], START)
            dve.sem_inc(a_ca, START)
            dve.wait_ge(ld_c, 32)
            blk3 = lambda n: blk.rearrange("p (t u) -> p t u", u=1).to_broadcast([P, TH, n])
            over_t = lambda a: a.rearrange("p (u n) -> p u n", u=1).to_broadcast([P, TH, a.shape[1]])
            for k in range(K):
                V.tensor_tensor(thetabd[:, k], over_t(sm("theta")[:, k * 16:(k + 1) * 16]), blk3(16), ALU.mult)
            V.tensor_tensor(rwbd[:], over_t(sm("rw")), blk3(16), ALU.mult)
            V.tensor_copy(tri[:], cs(TRI, P))
            V.tensor_copy(one[:], cs(ONE, P))
            V.tensor_copy(mk[0:32], sml[0:32, COL["u3"]:COL["u3"] + F])
            V.tensor_copy(mk[32:48], cst[32:48, ID + 32:ID + 48])
            V.tensor_copy(i16w1[0:T, 0:T], cst[0:T, ID:ID + T])
            V.tensor_copy(i16w1[0:T, T:T + 1], sml[0:T, COL["w1"]:COL["w1"] + 1])
            step = Steps(dve, wk, 0, H * 4 + 2)
            step(V.tensor_tensor(negb[:], sm("tb"), sm("rb"), ALU.add))
            step(V.tensor_scalar(negb[:], negb[:], -1.0, None, ALU.mult))
            for h in range(H):
                def band(out_, dt):
                    q = BLK + dt + (1 - h)
                    on = cst[:, q:q + TH + 1].rearrange("p (t u) -> p t u", u=1).to_broadcast([P, TH + 1, 16])
                    w = sm("tw")[:, dt * 16:(dt + 1) * 16].rearrange("p (u n) -> p u n", u=1).to_broadcast([P, TH + 1, 16])
                    return V.tensor_tensor(out_.rearrange("p (t o) -> p t o", o=16), w, on, ALU.mult)
                band(convm[:, h], 0)
                step(band(convt[:, 0], 1))
                step(V.tensor_tensor(convm[:, h], convm[:, h], convt[:, 0], ALU.add))
                step(band(convt[:, 1], 2))
                step(V.tensor_tensor(convm[:, h], convm[:, h], convt[:, 1], ALU.add))
            step.close()
            dve.sem_inc(consts_ready, 1)
            dve.wait_ge(zeros_ready, 1)

            def reciprocal_root(step, v, out_):
                bits, guess = v[:, 1].bitcast(I32), out_
                yield from step.then(V.tensor_scalar(bits, v[:, 0].bitcast(I32), 1, None, ALU.arith_shift_right))
                yield from step.then(V.tensor_scalar(guess.bitcast(I32), bits, -1.0, MAGIC, ALU.mult, ALU.add))
                for last in (False, False, True):
                    yield from step.then(V.tensor_tensor(v[:, 2], v[:, 0], guess, ALU.mult))
                    yield from step.then(V.scalar_tensor_tensor(out=v[:, 3], in0=v[:, 2], scalar=-0.5, in1=guess, op0=ALU.mult,
                                                op1=ALU.mult))
                    if last:
                        yield from step.then(V.scalar_tensor_tensor(out=v[:, 3], in0=v[:, 3], scalar=0.5, in1=guess, op0=ALU.add,
                                                    op1=ALU.mult))
                        yield from step.then(V.tensor_tensor(guess, guess, v[:, 3], ALU.add))
                    else:
                        yield from step.then(V.scalar_tensor_tensor(out=guess, in0=v[:, 3], scalar=1.5, in1=guess, op0=ALU.add,
                                                    op1=ALU.mult))

            def run(chain):
                for _ in chain:
                    pass

            GC = GB * C
            mask = mk[0:48].rearrange("p (u f) -> p u f", u=1).to_broadcast([48, 2 * T, F])
            wide = lambda a: a.rearrange("p (b u) -> p b u", u=1).to_broadcast([T, GB, T])

            def stats(g):
                step = Steps(dve, a_w, g, 1)
                dve.wait_ge(x_in, g + 1)
                for j in range(GC - 1):
                    V.bn_stats(st6[:, j], xs[:, GB * g + j // C, j % C])
                    yield
                yield from step.then(V.bn_stats(st6[:, GC - 1], xs[:, GB * g + GB - 1, C - 1]))
                step.close()
                dve.nop(nofuse=True)
                for j in range(GC):
                    ins = V.bn_aggr(mv[:, j], st6[:, j])
                ins.then_inc(a_stat, 1)

            def norm(g):
                step = Steps(dve, a_hv, g, 16)
                dve.wait_ge(a_mean, g + 1)
                V.tensor_copy(gd[:, 1], bank[0][:, 0:GC])
                yield from step.then(V.tensor_tensor(gd[:, 0], mv[:, :, 0], bank[0][:, 0:GC], ALU.subtract))
                yield from step.then(V.tensor_tensor(gd[:, 0], gd[:, 0], gd[:, 0], ALU.mult))
                V.tensor_tensor(gd[:, 2], gd[:, 0], mv[:, :, 1], ALU.add).then_inc(a_q, 1)
                yield
                dve.wait_ge(a_var, g + 1)
                yield from step.then(V.tensor_scalar(vq[:, 0, 0:GC], bank[0][:, 0:GC], EPS, None, ALU.add))
                yield from reciprocal_root(step, vq[:, :, 0:GC], gr[:, 0])
                yield from step.then(V.scalar_tensor_tensor(out=gr[:, 1], in0=gd[:, 1], scalar=-1.0, in1=gr[:, 0],
                                                            op0=ALU.mult, op1=ALU.mult))
                step.close()
                dve.sem_inc(a_nb, 1)

            def normalise_x(g):
                for j in range(GB):
                    V.tensor_scalar(xn[:, j, 0].rearrange("p (t f) -> p f t", f=F),
                                    xs[:, GB * g + j, 0].rearrange("p (f t) -> p f t", t=T),
                                    gr[:, 0, j * C:j * C + 1], gr[:, 1, j * C:j * C + 1], ALU.mult, ALU.add
                                    ).then_inc(a_xnv, 1)

            def factors(g, step):
                for jj in range(GB // 2):
                    dve.wait_ge(a_uq, 2 * g + (jj + 1))
                    yield from step.then(V.tensor_tensor(uq[0:48, jj * 2 * T:(jj + 1) * 2 * T],
                                                         bank[3 + jj][0:48, :].rearrange("p (j f) -> p j f", f=F),
                                                         mask, ALU.mult))
                flat = lambda a: a.rearrange("p b t -> p (b t)")
                V.tensor_reduce(flat(ca[0:T, 0]), uq[0:T], AX, ALU.add)
                yield
                V.tensor_reduce(flat(ca[0:T, 1]), uq[32:32 + T], AX, ALU.add).then_inc(a_ca, 1)
                yield

            def attend(g, step):
                dve.wait_ge(a_pr, g + 1)
                bet = sml[0:T, COL["bet"]:COL["bet"] + T].rearrange("p (u t) -> p u t", u=1).to_broadcast([T, GB, T])
                e5 = bank[5][0:T, 0:GB * T].rearrange("p (b t) -> p b t", b=GB)
                V.tensor_tensor(eb[0:T, 0], e5, bet, ALU.add).then_inc(a_pb, 1)
                yield
                dve.wait_ge(a_er, g + 1)
                yield from step.then(V.tensor_reduce(es[0:T, 0], e5, AX, ALU.max))
                V.tensor_tensor(eb[0:T, 0], e5, wide(es[0:T, 0]), ALU.subtract).then_inc(a_es, 1)
                yield
                dve.wait_ge(a_ex, g + 1)
                yield from step.then(V.tensor_reduce(es[0:T, 1], eb[0:T, 2], AX, ALU.add))
                yield from step.then(V.reciprocal(es[0:T, 2], es[0:T, 1]))
                V.tensor_tensor(eb[0:T, 0], eb[0:T, 2], wide(es[0:T, 2]), ALU.mult).then_inc(a_et, 1)
                yield
                dve.wait_ge(a_ej, g + 1)
                V.tensor_copy(ej[0:T].rearrange("p b t -> p (b t)"), bank[6][0:T, 0:GB * (T + 1)]).then_inc(a_ec, 1)
                yield
                dve.wait_ge(a_rep, g + 1)
                for h in range(H):
                    r7 = bank[7][:, h * GB * (T + 1):(h + 1) * GB * (T + 1)].rearrange("p (b t) -> p b t", b=GB)
                    gg = gh[:, bass.ds(GB * g, GB), h]
                    yield from step.then(V.tensor_copy(es[:, 3], r7[:, :, T]))
                    V.tensor_tensor(gg[:, :, 0:T], sm("w2").rearrange("p (u t) -> p u t", u=1).to_broadcast([P, GB, T]),
                                    es[:, 3].rearrange("p (b u) -> p b u", u=1).to_broadcast([P, GB, T]), ALU.mult)
                    yield from step.then(V.tensor_scalar(gg[:, :, 32:32 + T], r7[:, :, 0:T], sm("w3"), None, ALU.mult))
                step.close()
                dve.sem_inc(a_gh, 1)

            def group(g, norm_next, stats_after):
                step = Steps(dve, a_v, g, 9)
                if norm_next:
                    weave(norm(g + 1), factors(g, step))
                    normalise_x(g + 1)
                else:
                    run(factors(g, step))
                if stats_after:
                    weave(attend(g, step), stats(g + 2))
                else:
                    run(attend(g, step))

            run(stats(0))
            run(norm(0))
            normalise_x(0)
            run(stats(1))
            with dve.Fori(0, GROUPS - 2) as g:
                group(g, True, True)
            group(GROUPS - 2, True, False)
            group(GROUPS - 1, False, False)

            def fetch_mix(b, p):
                dve.wait_ge(s["b_gh"], done(b - 2))
                V.tensor_copy(ghb[:, p], gh[:, b]).then_inc(s["b_gb"], 1)

            def add_bs(b, p):
                dve.wait_ge(s["b_pr"], done(b))
                dve.wait_ge(s["b_L"], done(b - 2))
                V.tensor_tensor(sg[:, p].rearrange("p c n -> p (c n)"), bank[1][:, :],
                                bs[:].rearrange("p c n -> p (c n)"), ALU.add).then_inc(s["b_bs"], 1)
                yield

            def row_max(b, p):
                dve.wait_ge(s["b_L"], done(b))
                step = Steps(dve, v_mx, b, 1)
                yield from step.then(V.tensor_reduce(nmx[:, p, 0], bank[1][:, :].rearrange("p (c n) -> p c n", c=C),
                                                     AX, ALU.max))
                step.close()
                V.tensor_scalar(nmx[:, p, 1], nmx[:, p, 0], -0.5, None, ALU.mult).then_inc(s["b_max"], 1)
                yield

            def recip(b, p):
                dve.wait_ge(s["b_exp"], done(b))
                V.reciprocal(es2[:, p, 1], es2[:, p, 0]).then_inc(s["b_rec"], 1)
                yield

            def weigh(b, p):
                dve.wait_ge(s["b_tr"], done(b))
                dve.wait_ge(s["b_main"], done(b - 2))
                for c in range(C):
                    p3 = bank[3][:, c * N:(c + 1) * N].rearrange("p (u n) -> p u n", u=1).to_broadcast([P, K, N])
                    ins = V.tensor_tensor(A[:, p, c], p3, chebs[:, c], ALU.mult)
                    if c == C - 1:
                        ins.then_inc(s["b_A"], 1)
                    yield

            yvs = [y[:, p].rearrange("p c (o t) -> p (c o) t", t=T) for p in range(2)]
            th = lambda a: a.rearrange("p (k u) -> p k u", u=1).to_broadcast([P, C * 16, T])

            def ln_a(b, p):
                dve.wait_ge(s["b_conv"], done(b))
                dve.wait_ge(s["b_x1"], done(b - 2))
                yv = yvs[p]
                step = Steps(dve, v_ln, b, 2)
                nb = negb[:].rearrange("p (u o) -> p u o", u=1).to_broadcast([P, T, 16])
                for c in range(C):
                    ins = V.tensor_tensor(y[:, p, c].rearrange("p (o t) -> p t o", t=T),
                                          bank[7][:, c * FT:(c + 1) * FT].rearrange("p (t o) -> p t o", o=16), nb, ALU.max)
                ins.then_inc(s["b_y"], 1)
                yield
                dve.wait_ge(s["b_y"], done(b))
                yield from step.then(V.tensor_reduce(s1[:].rearrange("p c o -> p (c o)"), yv, AX, ALU.add))
                yield from step.then(V.scalar_tensor_tensor(out=yv, in0=th(s1[:].rearrange("p c o -> p (c o)")), scalar=-1.0 / T, in1=yv,
                                                            op0=ALU.mult, op1=ALU.add))
                step.close()
                dve.sem_inc(s["b_cen"], 1)

            LN, GN = slice(0, C * 16), slice(C * 16, NV)

            def ln_b(b, p):
                dve.wait_ge(s["b_sq"], done(b))
                V.tensor_reduce(vq[:, 4, LN], sq[:].rearrange("p c (o t) -> p (c o) t", t=T), AX, ALU.add
                                ).then_inc(s["b_var"], 1)
                yield

            def ln_roots(b, p):
                dve.wait_ge(s["b_var"], done(b))
                step = Steps(dve, v_lq, b, 13)
                yield from step.then(V.tensor_scalar(vq[:, 0, LN], vq[:, 4, LN], 1.0 / T, EPS, ALU.mult, ALU.add))
                yield from reciprocal_root(step, vq[:, :, LN], vr[:, LN])
                step.close()

            def gn_roots(b, p):
                dve.wait_ge(s["b_g2"], done(b))
                step = Steps(dve, v_gq, b, 13)
                yield from step.then(V.tensor_scalar(vq[:, 0, GN], bank[2][:, 0:C], EPS, None, ALU.add))
                yield from reciprocal_root(step, vq[:, :, GN], vr[:, GN])
                step.close()

            def ln_c(b, p):
                yv = yvs[p]
                V.tensor_tensor(yv, yv, th(vr[:, LN]), ALU.mult).then_inc(s["b_dn"], 1)
                yield

            def gn_stats(b, p, step):
                dve.wait_ge(s["b_x1"], done(b))
                V.bn_stats(st62[:, 0], xs[:, b, 0])
                yield
                yield from step.then(V.bn_stats(st62[:, 1], xs[:, b, 1]))
                dve.nop(nofuse=True)
                for c in range(C):
                    ins = V.bn_aggr(mv2[:, c], st62[:, c])
                ins.then_inc(s["b_st"], 1)
                yield

            def gn_moments(b, p, step):
                dve.wait_ge(s["b_g1"], done(b))
                dve.wait_ge(s["b_st"], done(b))
                V.tensor_copy(gd2[:, 1], bank[2][:, 0:C])
                yield from step.then(V.tensor_tensor(gd2[:, 0], mv2[:, :, 0], bank[2][:, 0:C], ALU.subtract))
                yield from step.then(V.tensor_tensor(gd2[:, 0], gd2[:, 0], gd2[:, 0], ALU.mult))
                V.tensor_tensor(gd2[:, 2], gd2[:, 0], mv2[:, :, 1], ALU.add).then_inc(s["b_q"], 1)
                step.close()
                yield

            def gn_scale(b, p):
                dve.wait_ge(s["b_xn"], done(b - 1))
                V.tensor_copy(gr2[:, 0], vr[:, C * 16:NV])
                V.scalar_tensor_tensor(out=gr2[:, 1], in0=gd2[:, 1], scalar=-1.0, in1=vr[:, C * 16:NV], op0=ALU.mult,
                                       op1=ALU.mult).then_inc(s["b_nb"], 1)
                yield

            wide8 = lambda a: a.rearrange("p (k u) -> p k u", u=1).to_broadcast([P, TT, E])
            row8 = lambda a: a.rearrange("p (u e) -> p u e", u=1).to_broadcast([P, TT, E])

            def route_a(b, p):
                dve.wait_ge(s["b_lg"], done(b))
                dve.wait_ge(s["b_sc"], done(b - 2))
                V.tensor_copy(xtok[:, p, :, N], tok[:])
                step = Steps(dve, v_rt, b, 3)
                lg = bank[3][:, FT:FT + TT * E].rearrange("p (k e) -> p k e", k=TT)
                yield from step.then(V.tensor_reduce(r2[:, 0], lg, AX, ALU.max))
                yield from step.then(V.tensor_scalar(tok[:], tok[:], float(FT), None, ALU.add))
                yield from step.then(V.tensor_tensor(rt[:, 0], lg, wide8(r2[:, 0]), ALU.subtract))
                step.close()
                dve.sem_inc(s["b_sh"], 1)

            def route_b(b, p):
                dve.wait_ge(s["b_ex"], done(b))
                step = Steps(dve, v_rt2, b, 18)
                yield from step.then(V.tensor_reduce(r2[:, 1], rt[:, 1], AX, ALU.add))
                yield from step.then(V.reciprocal(r2[:, 2], r2[:, 1]))
                yield from step.then(V.tensor_tensor(rt[:, 2], rt[:, 1], wide8(r2[:, 2]), ALU.mult))
                src = rt[:, 2]
                for w in range(2):
                    yield from step.then(V.tensor_reduce(r2[:, 3 + w], src, AX, ALU.max))
                    yield from step.then(V.tensor_tensor(rt[:, 3], src, wide8(r2[:, 3 + w]), ALU.is_equal))
                    yield from step.then(V.tensor_tensor(rt[:, 4], rt[:, 3], row8(cs(DSC, E)), ALU.mult))
                    yield from step.then(V.tensor_reduce(r2[:, 5 + w], rt[:, 4], AX, ALU.max))
                    yield from step.then(V.tensor_tensor(rt[:, 7 + w], rt[:, 4], wide8(r2[:, 5 + w]), ALU.is_equal))
                    if w == 0:
                        yield from step.then(V.scalar_tensor_tensor(out=rt[:, 5], in0=rt[:, 7], scalar=-2.0, in1=rt[:, 2],
                                                                    op0=ALU.mult, op1=ALU.add))
                        src = rt[:, 5]
                yield from step.then(V.tensor_tensor(mb[:], rt[:, 7], rt[:, 8], ALU.add))
                dve.sem_inc(s["b_M"], 1)
                V.tensor_scalar(xtok[:, p, :, N + 1], r2[:, 5], -1.0, float(E), ALU.mult, ALU.add)
                yield from step.then(V.tensor_tensor(r2[:, 7], r2[:, 3], r2[:, 4], ALU.add))
                yield from step.then(V.reciprocal(r2[:, 8], r2[:, 7]))
                wb = wts[:, b]
                V.tensor_tensor(wb[:, 0], r2[:, 3], r2[:, 8], ALU.mult)
                yield from step.then(V.tensor_tensor(wb[:, 1], r2[:, 4], r2[:, 8], ALU.mult))
                step.close()

            def route_c(b, p):
                dve.wait_ge(s["b_pf"], done(b))
                step = Steps(dve, v_rt3, b, 5)
                pf = bank[2][:, 64:64 + TT * E].rearrange("p (k e) -> p k e", k=TT)
                yield from step.then(V.tensor_tensor(rt[:, 10], pf, row8(cnt[:]), ALU.add))
                V.tensor_tensor(cnt[:], cnt[:], bank[2][:, 80:80 + E], ALU.add)
                yield from step.then(V.tensor_tensor(rt[:, 10], rt[:, 10], row8(cs(EBASE, E)), ALU.add))
                V.tensor_tensor(rt[:, 3], rt[:, 10], rt[:, 7], ALU.mult)
                yield from step.then(V.tensor_tensor(rt[:, 4], rt[:, 10], rt[:, 8], ALU.mult))
                V.tensor_reduce(slotf[:, 0], rt[:, 3], AX, ALU.add)
                yield from step.then(V.tensor_reduce(slotf[:, 1], rt[:, 4], AX, ALU.add))
                yield from step.then(V.tensor_copy(slot[:, p].rearrange("p w k -> p (w k)"),
                                                   slotf[:].rearrange("p w k -> p (w k)")))
                step.close()
                dve.sem_inc(s["b_slot"], 1)

            def turn(i, q, ahead2, ahead1, now, back1, back2, back3):
                step = Steps(dve, v_gn, i - 2, 3)

                def pause(n):
                    for _ in range(n):
                        yield

                def statistics():
                    if back2:
                        yield from gn_stats(i - 2, q, step)

                def attention():
                    if ahead1:
                        yield from row_max(i + 1, 1 - q)
                        yield from pause(2)
                        yield from recip(i + 1, 1 - q)

                def centre():
                    if back1:
                        yield from ln_a(i - 1, 1 - q)

                def layer_norm():
                    if back1:
                        yield from ln_b(i - 1, 1 - q)
                        yield from ln_roots(i - 1, 1 - q)
                        yield from ln_c(i - 1, 1 - q)

                def group_norm():
                    if back2:
                        yield from gn_moments(i - 2, q, step)
                        yield from pause(2)
                        yield from gn_roots(i - 2, q)
                        yield from gn_scale(i - 2, q)

                def matrices():
                    if ahead1:
                        yield from pause(10)
                        yield from weigh(i + 1, 1 - q)
                    if ahead2:
                        yield from add_bs(i + 2, q)

                def router(part):
                    if back3:
                        yield from part(i - 3, 1 - q)

                choice = router(route_b)
                if ahead2:
                    fetch_mix(i + 2, q)
                weave(centre())
                weave(router(route_a), statistics())
                variance = layer_norm()
                weave(attention(), along=(variance, choice))
                weave(variance, group_norm(), matrices(), choice)
                weave(router(route_c))

            dve.wait_ge(ld_w, 48)
            schedule(dve, turn)

            step = Steps(dve, v_tb, 0, 21)
            step(V.tensor_tensor(fillf[:], cnt[:], cs(EBASE, E), ALU.add))
            step(V.tensor_copy(filli[:], fillf[:]))
            dve.sem_inc(fill_rows, 1)
            step(V.tensor_scalar(nt[:, 0], cnt[:], float(P - 1), None, ALU.add))
            step(V.tensor_copy(ci[:, 0], nt[:, 0]))
            step(V.tensor_scalar(ci[:, 1], ci[:, 0], 7, None, ALU.arith_shift_right))
            step(V.tensor_copy(nt[:, 1], ci[:, 1]))
            step(V.tensor_tensor_scan(nt[:, 2], cst[:, ONE:ONE + E], nt[:, 1], 0.0, ALU.mult, ALU.add))
            tl = lambda a: a.rearrange("p (u e) -> p u e", u=1).to_broadcast([P, TILES, E])
            ti = cs(TIDX, TILES)
            step(V.tensor_tensor(ge[:, 0], tl(nt[:, 2]), ti.rearrange("p (t u) -> p t u", u=1).to_broadcast([P, TILES, E]),
                                 ALU.is_le))
            step(V.tensor_reduce(tb3[:, 0], ge[:, 0], AX, ALU.add))
            step(V.tensor_tensor(ge[:, 1], ge[:, 0], tl(nt[:, 1]), ALU.mult))
            step(V.tensor_reduce(tb3[:, 1], ge[:, 1], AX, ALU.add))
            step(V.tensor_tensor(tb3[:, 2], ti, tb3[:, 1], ALU.subtract))
            step(V.tensor_scalar(tb3[:, 3], tb3[:, 0], float(CAP), None, ALU.mult))
            step(V.scalar_tensor_tensor(out=tb3[:, 4], in0=tb3[:, 2], scalar=float(P), in1=tb3[:, 3], op0=ALU.mult,
                                        op1=ALU.add))
            step(V.tensor_scalar(itab[:, 1], tb3[:, 4], float(E * CAP), None, ALU.min))
            step(V.tensor_scalar(pk[:, 0], tb3[:, 0], float(E - 1), None, ALU.min))
            n2, n4, n6 = TILES - 1, TILES - 3, TILES - 5
            def packed(out_, high, low, n):
                step(V.scalar_tensor_tensor(out=out_, in0=high, scalar=float(E ** n), in1=low, op0=ALU.mult, op1=ALU.add))
            packed(pk[:, 1, 0:n2], pk[:, 0, 1:n2 + 1], pk[:, 0, 0:n2], 1)
            packed(pk[:, 2, 0:n4], pk[:, 1, 2:n4 + 2], pk[:, 1, 0:n4], 2)
            packed(pk[:, 0, 0:n6], pk[:, 1, 4:n6 + 4], pk[:, 2, 0:n6], 4)
            step(V.tensor_copy(itab[:, 0, 0:n4], pk[:, 2, 0:n4]))
            step(V.tensor_copy(itab[:, 0, 0:n6], pk[:, 0, 0:n6]))
            step.close()
            dve.sem_inc(tables, 1)

            dve.sem_inc(c_xc, START)
            dve.sem_inc(c_h, START)

            def copy_x(t, q):
                dve.wait_ge(c_tr, t + 1)
                dve.wait_ge(c_up, t + START - 1)
                V.tensor_copy(xc[:, q].rearrange("p c k -> p (c k)"), bank[q][:, 0:C * P]).then_inc(c_xc, 1)
                dve.wait_ge(c_di, t + 1)
                V.tensor_scalar(dn[:, 0, t % 4], xt[:, q, N + 1:N + 2], tb3[:, 0, bass.ds(t, 1)], float(TOKENS),
                                ALU.not_equal, ALU.mult).then_inc(c_dd, 1)
                dve.wait_ge(c_dd, t + 1)
                V.tensor_tensor(dn[:, 1, t % 4], dn[:, 0, t % 4], xt[:, q, N:N + 1], ALU.add).then_inc(c_de, 1)

            def gate(t, q):
                dve.wait_ge(c_gl, t + 1)
                dve.wait_ge(c_ht, t + START - 1)
                V.tensor_tensor(hh[:, q].rearrange("p f k -> p (f k)"), bank[2 + q][:, C * P:2 * C * P],
                                gl[:, q].rearrange("p f k -> p (f k)"), ALU.mult).then_inc(c_h, 1)

            copy_x(0, 0)
            copy_x(1, 1)
            gate(0, 0)
            with dve.Fori(0, TILES // 2 - 1) as i:
                for q in range(2):
                    t = 2 * i + q
                    copy_x(t + 2, q)
                    gate(t + 1, 1 - q)
            gate(TILES - 1, 1)

            dve.sem_inc(d_o, START)
            dve.sem_inc(d_s, START)

            def combine(b, q):
                dve.wait_ge(d_in, b + 1)
                dve.wait_ge(d_ym, b + 1)
                for k in range(TT):
                    ins = V.scalar_tensor_tensor(out=ys[:, q, k], in0=yy[:, b % 4, 1, k], scalar=wts[:, b, 1, k:k + 1],
                                                 in1=ym[:, b % 4, k], op0=ALU.mult, op1=ALU.add)
                ins.then_inc(d_s, 1)

            def residual(b, q, stored):
                dve.wait_ge(d_tr, b + 1)
                if stored is not None:
                    dve.wait_ge(d_st[q], stored)
                V.tensor_tensor(oo[:, q].rearrange("p c n -> p (c n)"), bank[6 + q][:, :],
                                xs[:, b].rearrange("p c n -> p (c n)"), ALU.add).then_inc(d_o, 1)

            combine(0, 0)
            for b in range(2):
                combine(b + 1, 1 - b)
                residual(b, b, None)
            with dve.Fori(0, B // 2 - 2) as i:
                for q in range(2):
                    combine(2 * i + (q + 3), 1 - q)
                    residual(2 * i + (q + 2), q, 16 * (i + 1))
            combine(B - 1, 1)
            residual(B - 2, 0, 16 * (B // 2 - 1))
            residual(B - 1, 1, 16 * (B // 2 - 1))


def constants():
    import numpy as np

    a = np.zeros((P, NCONST), np.float32)
    p = np.arange(P)
    a[:, ID:ID + P] = np.eye(P)
    a[:, TRI:TRI + P] = p[:, None] < p[None, :]
    a[:, ONE:ONE + P] = 1.0
    a[:, GRP:GRP + P] = (p[:, None] // 8 == p[None, :] // 8) / 8.0
    a[:, BLK:BLK + TH + 4] = np.arange(TH + 4)[None, :] == p[:, None] // F + 2
    a[:, DSC:DSC + E] = E - np.arange(E)
    a[:, EBASE:EBASE + E] = np.arange(E) * CAP
    a[:, TIDX:TIDX + TILES] = np.arange(TILES)
    a[:, PCOL] = p
    a[0:T, REP:REP + FT] = np.arange(FT)[None, :] // F == np.arange(T)[:, None]
    return a


def kernel(**inputs):
    import numpy as np
    import concourse.bacc as bacc
    from concourse.bass_utils import run_bass_kernel_spmd as run

    g = {k: np.asarray(v) for k, v in inputs.items()}
    c = {k[8:]: v for k, v in g.items() if k.startswith("L0_conv_")}
    m = {k[8:]: v for k, v in g.items() if k.startswith("L1_conv_")}
    small = np.zeros((P, NSMALL), np.float32)

    def put(name, a):
        small[:a.shape[0], COL[name]:COL[name] + SIZES[name]] = a

    down = lambda a: np.tile(a, (TH, 1))
    every = lambda a: np.tile(a.reshape(1, -1), (P, 1))
    rows = lambda a: np.moveaxis(a.reshape(a.shape[:-2] + (C, P, a.shape[-1])), -2, 0)
    put("theta", down(c["Theta"].transpose(1, 0, 2).reshape(F, K * 16)))
    put("rw", down(c["rw"].T))
    put("tw", down(c["tw"][:, :, 0, :].transpose(1, 2, 0).reshape(16, 48)))
    put("w2", down(c["W2"]))
    put("w3", down(c["W3"].reshape(F, 1)))
    put("tb", every(c["tb"]))
    put("rb", every(c["rb"]))
    put("gamma", every(c["gamma"]))
    put("beta", every(c["beta"]))
    put("u3", every(c["U3"]))
    uu = np.zeros((C, P, 48), np.float32)
    uu[:, :, 0:F] = c["U2"].reshape(F, C, P).transpose(1, 2, 0)
    uu[:, :, 32:48] = c["U1"].reshape(C, P, 1)
    put("uu", uu.transpose(1, 0, 2).reshape(P, C * 48))
    put("gate", m["gate_w"].reshape(E, C, P).transpose(2, 1, 0).reshape(P, C * E))
    put("vet", c["V_e"].T)
    put("bet", c["b_e"][0].T)
    put("w1", c["W1"].reshape(T, 1))
    arrays = dict(x=g["x"], consts=constants(), small=small, cheb=c["cheb"].reshape(K, C, P, N).transpose(2, 1, 0, 3),
                  vst=rows(c["V_s"].T), bst=rows(c["b_s"][0].T), 
                  w13t=rows(np.concatenate([m["w1"].transpose(0, 2, 1), m["w3"].transpose(0, 2, 1)], -1)
                            ).reshape(P, E, C, 2, N), w2t=rows(m["w2"].transpose(0, 2, 1)))
    arrays = {k: np.ascontiguousarray(v) for k, v in arrays.items()}

    nc = bacc.Bacc("TRN2", target_bir_lowering=False, num_devices=1)
    args = {k: nc.dram_tensor(f"{k}_in", v.shape, F32, kind="ExternalInput").ap() for k, v in arrays.items()}
    xrows = nc.dram_tensor("xrows", (E * CAP + P, ROW), F32, kind="Internal").ap()
    yrows = nc.dram_tensor("yrows", (2 * TOKENS + P, N), F32, kind="Internal").ap()
    out = nc.dram_tensor("out", (B, N, F, T), F32, kind="ExternalOutput").ap()
    build(nc, xrows=xrows, yrows=yrows, out=out, **args)
    r = run(nc, [{f"{k}_in": v for k, v in arrays.items()}], core_ids=[0])
    return r.results[0]["out"]
```
